# Optimizing a Trainium2 kernel written in Bass

```python
import numpy as np
import jax
import jax.numpy as jnp

def _softmax(x, axis=-1):
    return jax.nn.softmax(x, axis=axis)

def _gelu(x):
    return jax.nn.gelu(x, approximate=True)

def _silu(x):
    return jax.nn.silu(x)

def _sigmoid(x):
    return jax.nn.sigmoid(x)

def _layernorm(x, axis=-1, eps=1e-05):
    m = jnp.mean(x, axis=axis, keepdims=True)
    v = jnp.var(x, axis=axis, keepdims=True)
    return (x - m) / jnp.sqrt(v + eps)

def _scatter_add(tgt, idx, src, axis=0):
    return tgt.at[idx].add(src)

def _segment_sum(src, seg, n):
    return jax.ops.segment_sum(src, seg, n)
kernel_name = 'mk_lm_tower_d2_tok_ids768_r4_8b26f8'

def setup_inputs(seed: int=0):
    np.random.seed(seed)
    _w = jnp.asarray

    def _rec_inputs():
        import jax
        import jax.numpy as jnp
        _rk = jax.random.key(seed)
        x = jax.random.randint(jax.random.fold_in(_rk, 1), (8, 512), 0, 12564, jnp.int32)
        return x
    x = _rec_inputs()

    def _L0_tok_setup():
        import jax, jax.numpy as jnp
        import numpy as np
        EMBED_DIM_LIST = (192, 96, 144, 192)
        MAX_EMBED_DIM = 192
        VOCAB = 50257
        BATCH, SEQ = (8, 512)
        key = jax.random.key(seed)
        k1, k2, k3 = jax.random.split(key, 3)
        x = jax.random.randint(k1, (BATCH, SEQ), 0, VOCAB, dtype=jnp.int64)
        weights = jax.random.uniform(k2, (len(EMBED_DIM_LIST),), dtype=jnp.float32)
        emb_weight = jax.random.normal(k3, (VOCAB, MAX_EMBED_DIM), dtype=jnp.float32) * 0.02
        return {'x': x, 'weights': weights, 'emb_weight': emb_weight}
    _L0_tok_all = _L0_tok_setup()
    _L0_tok_in = {k: v for k, v in _L0_tok_all.items() if k in ('weights', 'emb_weight')}
    del _L0_tok_all

    def _L0_attn_setup():
        import jax, jax.numpy as jnp
        import numpy as np
        import math
        N_EMBD = 192
        N_HEAD = 12
        HEAD_DIM = N_EMBD // N_HEAD

        def rope_cache(T, dim):
            inv_freq = 1.0 / 10000.0 ** (2.0 * jnp.arange(dim // 2, dtype=jnp.float32) / dim)
            angles = jnp.arange(T, dtype=jnp.float32)[:, None] * inv_freq[None, :]
            return jnp.stack((jnp.cos(angles), jnp.sin(angles)), axis=-1)

        def apply_rope(x, rope):
            B, H, T, D = x.shape
            xp = x.reshape(B, H, T, D // 2, 2)
            x1, x2 = (xp[..., 0], xp[..., 1])
            cos = rope[None, None, :, :, 0]
            sin = rope[None, None, :, :, 1]
            out = jnp.stack((x1 * cos - x2 * sin, x1 * sin + x2 * cos), axis=-1)
            return out.reshape(B, H, T, D)
        key = jax.random.key(seed)
        ks = jax.random.split(key, 9)
        s = 0.02
        d = N_EMBD
        return {'x': jax.random.normal(ks[0], (2, 1024, d), dtype=jnp.float32), 'Wq': jax.random.normal(ks[1], (d, d), dtype=jnp.float32) * s, 'bq': jnp.zeros((d,), jnp.float32), 'Wk': jax.random.normal(ks[2], (d, d), dtype=jnp.float32) * s, 'bk': jnp.zeros((d,), jnp.float32), 'Wv': jax.random.normal(ks[3], (d, d), dtype=jnp.float32) * s, 'bv': jnp.zeros((d,), jnp.float32), 'Wp': jax.random.normal(ks[4], (d, d), dtype=jnp.float32) * s, 'bp': jnp.zeros((d,), jnp.float32)}
    _L0_attn_all = _L0_attn_setup()
    _L0_attn_in = {k: v for k, v in _L0_attn_all.items() if k in ('Wq', 'bq', 'Wk', 'bk', 'Wv', 'bv', 'Wp', 'bp')}
    del _L0_attn_all

    def _L0_ffn_setup():
        import jax, jax.numpy as jnp
        import numpy as np
        B, S, H, D, E = (4, 512, 192, 256, 8)
        TOP_K = 2
        EPS = 1e-08
        LN_EPS = 1e-05

        def _gelu(t):
            return jax.nn.gelu(t, approximate=False)

        def _layer_norm(t, gamma, beta):
            mu = jnp.mean(t, axis=-1, keepdims=True)
            var = jnp.mean(jnp.square(t - mu), axis=-1, keepdims=True)
            return (t - mu) * jax.lax.rsqrt(var + LN_EPS) * gamma + beta
        key = jax.random.key(seed)
        ks = jax.random.split(key, 8)
        x = jax.random.normal(ks[0], (B, S, H), dtype=jnp.float32)
        w1 = jax.random.normal(ks[1], (H, H // 2), dtype=jnp.float32) * 0.02
        b1 = jnp.zeros((H // 2,), dtype=jnp.float32)
        w2 = jax.random.normal(ks[2], (H // 2, E), dtype=jnp.float32) * 0.02
        b2 = jnp.zeros((E,), dtype=jnp.float32)
        a_dn = float(np.sqrt(6.0 / (H + D)))
        a_up = float(np.sqrt(6.0 / (D + H)))
        down_w = jax.random.uniform(ks[3], (E, H, D), dtype=jnp.float32, minval=-a_dn, maxval=a_dn)
        down_b = jnp.zeros((E, D), dtype=jnp.float32)
        up_w = jax.random.uniform(ks[4], (E, D, H), dtype=jnp.float32, minval=-a_up, maxval=a_up)
        gamma = jnp.ones((H,), dtype=jnp.float32)
        beta = jnp.zeros((H,), dtype=jnp.float32)
        return {'x': x, 'w1': w1, 'b1': b1, 'w2': w2, 'b2': b2, 'down_w': down_w, 'down_b': down_b, 'up_w': up_w, 'gamma': gamma, 'beta': beta}
    _L0_ffn_all = _L0_ffn_setup()
    _L0_ffn_in = {k: v for k, v in _L0_ffn_all.items() if k in ('w1', 'b1', 'w2', 'b2', 'down_w', 'down_b', 'up_w', 'gamma', 'beta')}
    del _L0_ffn_all

    def _L1_attn_setup():
        import jax, jax.numpy as jnp
        import numpy as np
        B, N, DIM = (8, 256, 192)
        H, HD = (12, 64)
        INNER = H * HD
        SCALE = HD ** (-0.5)
        key = jax.random.key(seed)
        ks = jax.random.split(key, 6)
        return {'x': jax.random.normal(ks[0], (B, N, DIM), dtype=jnp.float32), 'w_qkv': jax.random.normal(ks[1], (DIM, 3 * INNER), dtype=jnp.float32) * 0.02, 'b_qkv': jax.random.normal(ks[2], (3 * INNER,), dtype=jnp.float32) * 0.02, 'reattn_weights': jax.random.normal(ks[3], (H, HD, HD), dtype=jnp.float32), 'w_out': jax.random.normal(ks[4], (INNER, DIM), dtype=jnp.float32) * 0.02, 'b_out': jax.random.normal(ks[5], (DIM,), dtype=jnp.float32) * 0.02}
    _L1_attn_all = _L1_attn_setup()
    _L1_attn_in = {k: v for k, v in _L1_attn_all.items() if k in ('w_qkv', 'b_qkv', 'reattn_weights', 'w_out', 'b_out')}
    del _L1_attn_all

    def _L1_ffn_setup():
        import jax, jax.numpy as jnp
        import numpy as np
        E, C, F, K = (8, 192, 768, 2)
        key = jax.random.key(seed)
        k0, k1, k2, k3 = jax.random.split(key, 4)
        B, T = (8, 512)
        return {'x': jax.random.normal(k0, (B, T, C), jnp.float32), 'router_w': jax.random.normal(k1, (E, C), jnp.float32) * 0.02, 'w1': jax.random.normal(k2, (E, C, F), jnp.float32) * 0.02, 'b1': jnp.zeros((E, F), jnp.float32), 'w2': jax.random.normal(k3, (E, F, C), jnp.float32) * 0.02, 'b2': jnp.zeros((E, C), jnp.float32)}
    _L1_ffn_all = _L1_ffn_setup()
    _L1_ffn_in = {k: v for k, v in _L1_ffn_all.items() if k in ('router_w', 'w1', 'b1', 'w2', 'b2')}
    del _L1_ffn_all
    return {'x': x, 'L0_tok_weights': _L0_tok_in['weights'], 'L0_tok_emb_weight': _L0_tok_in['emb_weight'], 'L0_attn_Wq': _L0_attn_in['Wq'], 'L0_attn_bq': _L0_attn_in['bq'], 'L0_attn_Wk': _L0_attn_in['Wk'], 'L0_attn_bk': _L0_attn_in['bk'], 'L0_attn_Wv': _L0_attn_in['Wv'], 'L0_attn_bv': _L0_attn_in['bv'], 'L0_attn_Wp': _L0_attn_in['Wp'], 'L0_attn_bp': _L0_attn_in['bp'], 'L0_ffn_w1': _L0_ffn_in['w1'], 'L0_ffn_b1': _L0_ffn_in['b1'], 'L0_ffn_w2': _L0_ffn_in['w2'], 'L0_ffn_b2': _L0_ffn_in['b2'], 'L0_ffn_down_w': _L0_ffn_in['down_w'], 'L0_ffn_down_b': _L0_ffn_in['down_b'], 'L0_ffn_up_w': _L0_ffn_in['up_w'], 'L0_ffn_gamma': _L0_ffn_in['gamma'], 'L0_ffn_beta': _L0_ffn_in['beta'], 'L1_attn_w_qkv': _L1_attn_in['w_qkv'], 'L1_attn_b_qkv': _L1_attn_in['b_qkv'], 'L1_attn_reattn_weights': _L1_attn_in['reattn_weights'], 'L1_attn_w_out': _L1_attn_in['w_out'], 'L1_attn_b_out': _L1_attn_in['b_out'], 'L1_ffn_router_w': _L1_ffn_in['router_w'], 'L1_ffn_w1': _L1_ffn_in['w1'], 'L1_ffn_b1': _L1_ffn_in['b1'], 'L1_ffn_w2': _L1_ffn_in['w2'], 'L1_ffn_b2': _L1_ffn_in['b2']}

def reference(x, L0_tok_weights, L0_tok_emb_weight, L0_attn_Wq, L0_attn_bq, L0_attn_Wk, L0_attn_bk, L0_attn_Wv, L0_attn_bv, L0_attn_Wp, L0_attn_bp, L0_ffn_w1, L0_ffn_b1, L0_ffn_w2, L0_ffn_b2, L0_ffn_down_w, L0_ffn_down_b, L0_ffn_up_w, L0_ffn_gamma, L0_ffn_beta, L1_attn_w_qkv, L1_attn_b_qkv, L1_attn_reattn_weights, L1_attn_w_out, L1_attn_b_out, L1_ffn_router_w, L1_ffn_w1, L1_ffn_b1, L1_ffn_w2, L1_ffn_b2):
    import jax
    import jax.numpy as jnp

    def _L0_tok_ref(x, weights, emb_weight):
        import jax, jax.numpy as jnp
        import numpy as np
        EMBED_DIM_LIST = (192, 96, 144, 192)
        MAX_EMBED_DIM = 192
        VOCAB = 50257
        BATCH, SEQ = (8, 512)
        dims = jnp.asarray(EMBED_DIM_LIST)
        col = jnp.arange(MAX_EMBED_DIM)
        mask = (col[None, :] < dims[:, None]).astype(weights.dtype)
        col_scale = weights @ mask
        embedding_mixture = emb_weight * col_scale[None, :]
        out = embedding_mixture[x]
        return out

    def _L0_attn_ref(x, Wq, bq, Wk, bk, Wv, bv, Wp, bp):
        import jax, jax.numpy as jnp
        import numpy as np
        import math
        N_EMBD = 192
        N_HEAD = 12
        HEAD_DIM = N_EMBD // N_HEAD

        def rope_cache(T, dim):
            inv_freq = 1.0 / 10000.0 ** (2.0 * jnp.arange(dim // 2, dtype=jnp.float32) / dim)
            angles = jnp.arange(T, dtype=jnp.float32)[:, None] * inv_freq[None, :]
            return jnp.stack((jnp.cos(angles), jnp.sin(angles)), axis=-1)

        def apply_rope(x, rope):
            B, H, T, D = x.shape
            xp = x.reshape(B, H, T, D // 2, 2)
            x1, x2 = (xp[..., 0], xp[..., 1])
            cos = rope[None, None, :, :, 0]
            sin = rope[None, None, :, :, 1]
            out = jnp.stack((x1 * cos - x2 * sin, x1 * sin + x2 * cos), axis=-1)
            return out.reshape(B, H, T, D)
        B, T, C = x.shape
        H, D = (N_HEAD, HEAD_DIM)

        def heads(W, b):
            return (x @ W.T + b).reshape(B, T, H, D).transpose(0, 2, 1, 3)
        q = heads(Wq, bq)
        k = heads(Wk, bk)
        v = heads(Wv, bv)
        rope = rope_cache(T, D)
        q = apply_rope(q, rope)
        k = apply_rope(k, rope)
        att = jnp.einsum('bhqd,bhkd->bhqk', q, k) * (1.0 / math.sqrt(D))
        causal = jnp.tril(jnp.ones((T, T), dtype=bool))
        att = jnp.where(causal[None, None], att, -jnp.inf)
        att = jax.nn.softmax(att, axis=-1)
        y = jnp.einsum('bhqk,bhkd->bhqd', att, v)
        y = y.transpose(0, 2, 1, 3).reshape(B, T, C)
        return y @ Wp.T + bp

    def _L0_ffn_ref(x, w1, b1, w2, b2, down_w, down_b, up_w, gamma, beta):
        import jax, jax.numpy as jnp
        import numpy as np
        B, S, H, D, E = (4, 512, 192, 256, 8)
        TOP_K = 2
        EPS = 1e-08
        LN_EPS = 1e-05

        def _gelu(t):
            return jax.nn.gelu(t, approximate=False)

        def _layer_norm(t, gamma, beta):
            mu = jnp.mean(t, axis=-1, keepdims=True)
            var = jnp.mean(jnp.square(t - mu), axis=-1, keepdims=True)
            return (t - mu) * jax.lax.rsqrt(var + LN_EPS) * gamma + beta
        logits = _gelu(x @ w1 + b1) @ w2 + b2
        routing = jax.nn.softmax(logits, axis=-1)
        topv, topi = jax.lax.top_k(routing, TOP_K)
        sparse = jnp.sum(jax.nn.one_hot(topi, E, dtype=routing.dtype) * topv[..., None], axis=-2)
        sparse = sparse / (jnp.sum(sparse, axis=-1, keepdims=True) + EPS)
        z = _gelu(jnp.einsum('bsh,ehd->bsed', x, down_w) + down_b)
        expert_out = jnp.einsum('bsed,edh->bseh', z, up_w)
        moe_out = jnp.einsum('bseh,bse->bsh', expert_out, sparse)
        return _layer_norm(x + moe_out, gamma, beta)

    def _L1_attn_ref(x, w_qkv, b_qkv, reattn_weights, w_out, b_out):
        import jax, jax.numpy as jnp
        import numpy as np
        B, N, DIM = (8, 256, 192)
        H, HD = (12, 64)
        INNER = H * HD
        SCALE = HD ** (-0.5)
        b, n, _ = x.shape
        qkv = x @ w_qkv + b_qkv
        q, k, v = jnp.split(qkv, 3, axis=-1)

        def to_heads(t):
            return t.reshape(b, n, H, HD).transpose(0, 2, 1, 3)
        q, k, v = (to_heads(q), to_heads(k), to_heads(v))
        dots = jnp.einsum('bhid,bhjd->bhij', q, k) * SCALE
        attn = jax.nn.softmax(dots, axis=-1)
        head_scale = reattn_weights.sum(axis=(-1, -2))
        attn = attn * head_scale[None, :, None, None]
        out = jnp.einsum('bhij,bhjd->bhid', attn, v)
        out = out.transpose(0, 2, 1, 3).reshape(b, n, INNER)
        return out @ w_out + b_out

    def _L1_ffn_ref(x, router_w, w1, b1, w2, b2):
        import jax, jax.numpy as jnp
        import numpy as np
        E, C, F, K = (8, 192, 768, 2)
        B, T, Cc = x.shape
        flat = x.reshape(-1, Cc)
        logits = flat @ router_w.T
        probs = jax.nn.softmax(logits.astype(jnp.float32), axis=-1)
        top_w, top_i = jax.lax.top_k(probs, K)
        top_w = (top_w / top_w.sum(-1, keepdims=True)).astype(x.dtype)
        out = jnp.zeros_like(flat)
        for e in range(E):
            w_e = jnp.sum(top_w * (top_i == e), axis=-1)[:, None]
            h = jax.nn.gelu(flat @ w1[e] + b1[e], approximate=False)
            out = out + w_e * (h @ w2[e] + b2[e])
        return out.reshape(B, T, Cc)
    h = _L0_tok_ref(x, L0_tok_weights, L0_tok_emb_weight)
    h = h + _L0_attn_ref(_layernorm(h, axis=-1), L0_attn_Wq, L0_attn_bq, L0_attn_Wk, L0_attn_bk, L0_attn_Wv, L0_attn_bv, L0_attn_Wp, L0_attn_bp)
    h = h + _L0_ffn_ref(_layernorm(h, axis=-1), L0_ffn_w1, L0_ffn_b1, L0_ffn_w2, L0_ffn_b2, L0_ffn_down_w, L0_ffn_down_b, L0_ffn_up_w, L0_ffn_gamma, L0_ffn_beta)
    h = h + _L1_attn_ref(_layernorm(h, axis=-1), L1_attn_w_qkv, L1_attn_b_qkv, L1_attn_reattn_weights, L1_attn_w_out, L1_attn_b_out)
    h = h + _L1_ffn_ref(_layernorm(h, axis=-1), L1_ffn_router_w, L1_ffn_w1, L1_ffn_b1, L1_ffn_w2, L1_ffn_b2)
    return h

_drawn_inputs = setup_inputs


def setup_inputs(seed=0):
    import zlib

    import numpy as np

    out = dict(_drawn_inputs(seed))
    spreads = {'L0_attn_bq': (0.0, 0.8),
     'L0_attn_bk': (0.0, 0.8),
     'L0_attn_bv': (0.0, 0.1),
     'L0_attn_bp': (0.0, 0.1),
     'L0_ffn_b1': (0.0, 0.1),
     'L0_ffn_b2': (0.0, 0.1),
     'L0_ffn_down_b': (0.0, 0.1),
     'L0_ffn_gamma': (1.0, 0.2),
     'L0_ffn_beta': (0.0, 0.1),
     'L1_ffn_b1': (0.0, 0.8),
     'L1_ffn_b2': (0.0, 0.8)}
    factors = {'L0_tok_weights': 3.394,
     'L0_attn_Wq': 8.0,
     'L0_attn_Wk': 8.0,
     'L1_attn_b_out': 8.0,
     'L1_ffn_router_w': 5.366,
     'L1_ffn_w1': 7.053,
     'L1_ffn_w2': 6.011}
    for name, (base, spread) in spreads.items():
        noise = np.random.default_rng([zlib.crc32(name.encode()), seed]).standard_normal(out[name].shape)
        drawn = base * np.exp(spread * noise) if base else spread * noise
        out[name] = jnp.asarray(drawn.astype(out[name].dtype))
    for name, factor in factors.items():
        out[name] = (out[name] * factor).astype(out[name].dtype)
    return out
```

```python
from contextlib import ExitStack

import numpy as np

import concourse.bass as bass
from concourse import mybir

F32 = mybir.dt.float32
F32R = mybir.dt.float32r
U32 = mybir.dt.uint32
ALU = mybir.AluOpType
ACT = mybir.ActivationFunctionType
AX = mybir.AxisListType.X

P = 128
BATCH, SEQ = 8, 512
TILES = SEQ // P
DIM = 192
CA, CB = 128, DIM - 128
VOCAB = 50257
EMBED_DIMS = (192, 96, 144, 192)
EXPERTS = 8
LN_EPS = 1e-5
H0, D0 = 12, 16
H1, D1 = 12, 64
GATE_HID = 96
F0, F1 = 256, 768
MASKED = -1e30


def signals(nc, ctx, prefix, names):
    return {n: ctx.enter_context(nc.semaphore(f"{prefix}.{n}")) for n in names.split()}


def reset(nc, first, last):
    nc.sync.sem_clear(range(first.num, last.num + 1))
    nc.all_engine_barrier(sem_only=True)


def layer_norm_vector(nc, dve, s, rows, stats, mv, rstd, xn):
    for t in range(TILES):
        nc.vector.bn_stats(stats[:, t, :], rows[t]).then_inc(s["stats_done"], 1)
    for t in range(TILES):
        dve.wait_ge(s["stats_done"], t + 1)
        nc.vector.bn_aggr(mv[:, t, :], stats[:, t, :]).then_inc(s["moments_done"], 1)
    dve.wait_ge(s["rstd_done"], 2)
    dve.wait_ge(s["moments_done"], TILES)
    for t in range(TILES):
        nc.vector.tensor_scalar(xn[:, t, :], rows[t], mv[:, t, 0:1], rstd[:, t:t + 1],
                                ALU.subtract, ALU.mult).then_inc(s["norm_done"], 1)


def rstd_gpsimd(nc, pool, s, mv, rstd, neg_half, moments, first=0):
    pool.wait_ge(moments, TILES)
    nc.gpsimd.tensor_scalar(rstd[:, :], mv[:, :, 1], LN_EPS, None, ALU.add).then_inc(s, 1)
    pool.wait_ge(s, first + 1)
    nc.gpsimd.tensor_tensor(rstd[:, :], rstd[:, :], neg_half[:, :], ALU.pow).then_inc(s, 1)


def transpose_tokens(nc, pe, s, xn, psum_a, psum_b, ident):
    for t in range(TILES):
        pe.wait_ge(s["norm_done"], t + 1)
        nc.tensor.transpose(psum_a[:, t * P:(t + 1) * P], xn[:, t, 0:CA], ident[:, :])
        nc.tensor.transpose(psum_b[0:CB, t * P:(t + 1) * P], xn[:, t, CA:DIM],
                            ident[:, :]).then_inc(s["xT_in_psum"], 1)


def copy_transposed(nc, act, s, psum_a, psum_b, xTa, xTb):
    act.wait_ge(s["xT_in_psum"], TILES)
    nc.scalar.copy(xTa[:, :], psum_a[:, 0:SEQ]).then_inc(s["xT_done"], 1)
    nc.scalar.copy(xTb[0:CB, :], psum_b[0:CB, 0:SEQ]).then_inc(s["xT_done"], 1)


def embed(nc, io, hid, idx, const, weights_in):
    with ExitStack() as ctx:
        s = signals(nc, ctx, "embed", "idx_in mix_in scaled_w col_in_psum col_done hid_done")
        rows_in = [ctx.enter_context(nc.semaphore(f"embed.rows_in{g}")) for g in range(BATCH)]
        w4 = ctx.enter_context(nc.sbuf_tensor("mix_w", [4, 1], F32))
        w4b = ctx.enter_context(nc.sbuf_tensor("mix_w_wide", [4, P], F32))
        mask4 = ctx.enter_context(nc.sbuf_tensor("mix_mask", [4, DIM], F32))
        col = ctx.enter_context(nc.sbuf_tensor("col_scale", [P, DIM], F32))
        col_ps = ctx.enter_context(nc.psum_tensor("col_scale_ps", [P, 512], F32))
        with nc.Block() as block:
            @block.sync
            def _(sp):
                sp.dma_start(idx[:, :], io["tok"]).then_inc(s["idx_in"], 16)
                sp.dma_start(w4[:, :], io["L0_tok_weights"]).then_inc(s["mix_in"], 16)
                sp.dma_start(mask4[:, :], io["mix_mask"]).then_inc(s["mix_in"], 16)
                weights_in(sp)

            @block.gpsimd
            def _(pool):
                pool.wait_ge(s["idx_in"], 16)
                for t in range(BATCH * TILES):
                    nc.gpsimd.indirect_dma_start(
                        hid[:, t, :], None, io["L0_tok_emb_weight"],
                        bass.IndirectOffsetOnAxis(ap=idx[:, t:t + 1], axis=0),
                    ).then_inc(rows_in[t // TILES], 16)

            @block.tensor
            def _(pe):
                pe.wait_ge(s["scaled_w"], 2)
                nc.tensor.matmul(col_ps[:, 0:DIM], w4b[:, :], mask4[:, :],
                                 start=True, stop=True).then_inc(s["col_in_psum"], 1)

            @block.vector
            def _(dve):
                nc.vector.memset(w4b[:, :], 1.0).then_inc(s["scaled_w"], 1)
                dve.wait_ge(s["mix_in"], 32)
                dve.wait_ge(s["scaled_w"], 1)
                nc.vector.tensor_scalar(w4b[:, :], w4b[:, :], w4[:, 0:1], None,
                                        ALU.mult).then_inc(s["scaled_w"], 1)
                dve.wait_ge(s["col_in_psum"], 1)
                nc.vector.tensor_copy(col[:, :], col_ps[:, 0:DIM]).then_inc(s["col_done"], 1)
                dve.wait_ge(s["col_done"], 1)
                for g in range(BATCH):
                    dve.wait_ge(rows_in[g], 16 * TILES)
                    h4 = hid[:, g * TILES:(g + 1) * TILES, :]
                    nc.vector.tensor_tensor(h4, h4, col[:, :].unsqueeze(1).broadcast_to([P, TILES, DIM]),
                                            ALU.mult).then_inc(s["hid_done"], 1)
                dve.wait_ge(s["hid_done"], BATCH)
        reset(nc, s["idx_in"], rows_in[-1])


def first_attention(nc, hid, const, w):
    QT, NH = TILES, H0
    items = [(q, h) for q in range(QT) for h in range(NH)]
    with ExitStack() as ctx:
        def sb(name, shape, dt=F32):
            return ctx.enter_context(nc.sbuf_tensor(name, shape, dt))

        s = signals(nc, ctx, "attn0", """stats_done moments_done rstd_done norm_done xT_in_psum xT_done
            qk_in_psum v_in_psum v_done rot_products rotated hi_done lo_done stacks_in_psum
            stacks_done scores_in_psum max_done exp_done probsT_in_psum probsT_done pv_done
            rden_done y_done yT_in_psum yT_done out_in_psum hid_done""")
        stats, mv, rstd = sb("a_stats", [P, TILES, 6]), sb("a_mv", [P, TILES, 2]), sb("a_rstd", [P, TILES])
        xn = sb("a_xn", [P, TILES, DIM])
        xTa, xTb = sb("a_xTa", [P, SEQ]), sb("a_xTb", [CB + 1, SEQ])
        rc, rs = sb("a_rot_cos", [P, 2, 2 * NH, D0]), sb("a_rot_sin", [P, 2, 2 * NH, D0])
        stack = sb("a_stack", [P, 2, 2 * NH, 2, 2, D0], F32R)
        qkT = sb("a_qkT", [P, NH, SEQ], F32R)
        v = sb("a_v", [P, TILES, DIM])
        probs, probsT = sb("a_probs", [P, 3, SEQ]), sb("a_probsT", [P, 2, SEQ])
        nmax, den, rden = sb("a_nmax", [P, QT * NH]), sb("a_den", [P, QT * NH]), sb("a_rden", [P, QT * NH])
        y = sb("a_y", [P, TILES, DIM])
        work = ctx.enter_context(nc.psum_tensor("a_work", [P, 4, 512], F32))
        turn = ctx.enter_context(nc.psum_tensor("a_turn", [P, 2, 512], F32))
        yps = ctx.enter_context(nc.psum_tensor("a_y_ps", [P, 2, 512], F32))
        nc.vector.memset(xTb[CB:CB + 1, :], 1.0)
        nc.all_engine_barrier()

        with nc.Fori(0, BATCH) as b:
            rows = [hid[:, bass.ds(b * TILES + t, 1), :].rearrange("p o c -> p (o c)") for t in range(TILES)]
            with nc.Block() as block:
                def copy_probs(dve, i):
                    q = items[i][0]
                    dve.wait_ge(s["probsT_in_psum"], i + 1)
                    if i >= 2:
                        dve.wait_ge(s["pv_done"], i - 1)
                    nc.vector.tensor_copy(probsT[:, i % 2, 0:(q + 1) * P],
                                          turn[:, i % 2, 0:(q + 1) * P]).then_inc(s["probsT_done"], 1)

                def scale_y(dve, q):
                    a, e = q * NH, (q + 1) * NH
                    dve.wait_ge(s["exp_done"], e)
                    nc.vector.reciprocal(rden[:, a:e], den[:, a:e]).then_inc(s["rden_done"], 1)
                    dve.wait_ge(s["rden_done"], q + 1)
                    dve.wait_ge(s["pv_done"], e)
                    nc.vector.tensor_tensor(
                        y[:, q, :].rearrange("p (h d) -> p h d", h=NH),
                        yps[:, q % 2, 0:DIM].rearrange("p (h d) -> p h d", h=NH),
                        rden[:, a:e].unsqueeze(2).broadcast_to([P, NH, D0]), ALU.mult).then_inc(s["y_done"], 1)

                @block.vector
                def _(dve):
                    layer_norm_vector(nc, dve, s, rows, stats, mv, rstd, xn)
                    for t in range(TILES):
                        dve.wait_ge(s["qk_in_psum"], t + 1)
                        if t >= 2:
                            dve.wait_ge(s["rotated"], t - 1)
                        qk = work[:, t % 2, 0:2 * DIM].rearrange("p (a h d) -> p a h d", a=2, h=NH)
                        cos = const["cos"][:, t].unsqueeze(2).broadcast_to([P, 2, NH, D0])
                        nc.vector.tensor_tensor(rc[:, t % 2].rearrange("p (a h) d -> p a h d", a=2), qk, cos,
                                                ALU.mult).then_inc(s["rot_products"], 1)
                        for a in range(2):
                            pair = work[:, t % 2, a * DIM:(a + 1) * DIM].rearrange(
                                "p (h i two) -> p h i two", h=NH, two=2)
                            dst = rs[:, t % 2, a * NH:(a + 1) * NH].rearrange("p h (i two) -> p h i two", two=2)
                            sin = const["sin"][:, t, a, :].rearrange("p (i two) -> p i two", two=2)
                            sin = sin.unsqueeze(1).broadcast_to([P, NH, D0 // 2, 2])
                            nc.vector.tensor_tensor(dst, pair[:, :, :, ::-1], sin,
                                                    ALU.mult).then_inc(s["rot_products"], 1)

                    for i, (q, h) in enumerate(items):
                        dve.wait_ge(s["scores_in_psum"], i + 1)
                        nc.vector.tensor_reduce(nmax[:, i:i + 1], work[:, i % 4, 0:(q + 1) * P], AX, ALU.max,
                                                negate=True).then_inc(s["max_done"], 1)
                        if i >= 2:
                            copy_probs(dve, i - 2)
                        if i >= 5 and (i - 5) % NH == NH - 1:
                            scale_y(dve, (i - 5) // NH)
                    for i in (len(items) - 2, len(items) - 1):
                        copy_probs(dve, i)
                    scale_y(dve, QT - 1)
                    for t in range(TILES):
                        dve.wait_ge(s["out_in_psum"], t + 1)
                        nc.vector.tensor_tensor(rows[t], work[:, 2 + t % 2, 0:DIM], rows[t],
                                                ALU.add).then_inc(s["hid_done"], 1)

                @block.gpsimd
                def _(pool):
                    rstd_gpsimd(nc, pool, s["rstd_done"], mv, rstd, const["neg_half"], s["moments_done"])
                    for t in range(TILES):
                        pool.wait_ge(s["rot_products"], 3 * (t + 1))
                        nc.gpsimd.tensor_tensor(rc[:, t % 2], rc[:, t % 2], rs[:, t % 2],
                                                ALU.add).then_inc(s["rotated"], 1)
                        pool.wait_ge(s["rotated"], t + 1)
                        pool.wait_ge(s["hi_done"], 2 * (t + 1))
                        if t >= 2:
                            pool.wait_ge(s["stacks_in_psum"], 3 * (t - 1))
                        st = stack[:, t % 2]
                        for a in range(2):
                            heads = slice(a * NH, (a + 1) * NH)
                            r = rc[:, t % 2, heads, :].unsqueeze(2).broadcast_to([P, NH, 2, D0])
                            hi = st[:, heads, 0, :, :] if a == 0 else st[:, heads, :, 0, :]
                            lo = st[:, heads, 1, :, :] if a == 0 else st[:, heads, :, 1, :]
                            nc.gpsimd.tensor_tensor(lo, r, hi.bitcast(F32), ALU.subtract).then_inc(s["lo_done"], 1)

                def copy_stacks(act, t):
                    for j in range(3):
                        n = 3 * t + j
                        act.wait_ge(s["stacks_in_psum"], n + 1)
                        nc.scalar.copy(qkT[:, 4 * j:4 * j + 4, t * P:(t + 1) * P],
                                       turn[:, n % 2, :].rearrange("p (c k) -> p c k", c=4)
                                       ).then_inc(s["stacks_done"], 1)

                @block.scalar
                def _(act):
                    copy_transposed(nc, act, s, work[:, 0], work[:, 1], xTa, xTb)
                    for t in range(TILES):
                        act.wait_ge(s["v_in_psum"], t + 1)
                        nc.scalar.copy(v[:, t, :], work[:, 2 + t % 2, 0:DIM]).then_inc(s["v_done"], 1)
                        act.wait_ge(s["rotated"], t + 1)
                        if t >= 2:
                            act.wait_ge(s["stacks_in_psum"], 3 * (t - 1))
                        st = stack[:, t % 2]
                        for a in range(2):
                            heads = slice(a * NH, (a + 1) * NH)
                            r = rc[:, t % 2, heads, :].unsqueeze(2).broadcast_to([P, NH, 2, D0])
                            hi = st[:, heads, 0, :, :] if a == 0 else st[:, heads, :, 0, :]
                            nc.scalar.copy(hi, r).then_inc(s["hi_done"], 1)
                        if t >= 1:
                            copy_stacks(act, t - 1)
                    copy_stacks(act, TILES - 1)
                    for i, (q, h) in enumerate(items):
                        act.wait_ge(s["max_done"], i + 1)
                        if i >= 3:
                            act.wait_ge(s["probsT_in_psum"], i - 2)
                        n = (q + 1) * P
                        nc.scalar.activation(probs[:, i % 3, 0:n], work[:, i % 4, 0:n], ACT.Exp,
                                             bias=nmax[:, i:i + 1],
                                             accum_out=den[:, i:i + 1]).then_inc(s["exp_done"], 1)
                    act.wait_ge(s["yT_in_psum"], TILES)
                    nc.scalar.copy(xTa[:, :], work[:, 0, :]).then_inc(s["yT_done"], 1)
                    nc.scalar.copy(xTb[0:CB, :], work[0:CB, 1, :]).then_inc(s["yT_done"], 1)

                @block.tensor
                def _(pe):
                    transpose_tokens(nc, pe, s, xn, work[:, 0], work[:, 1], const["ident"])
                    pe.wait_ge(s["xT_done"], 2)

                    def stacks(t):
                        pe.wait_ge(s["hi_done"], 2 * (t + 1))
                        pe.wait_ge(s["lo_done"], 2 * (t + 1))
                        for j in range(3):
                            n = 3 * t + j
                            if n >= 2:
                                pe.wait_ge(s["stacks_done"], n - 1)
                            for c in range(4):
                                pair = stack[:, t % 2, 2 * (4 * j + c):2 * (4 * j + c) + 2].rearrange(
                                    "p h a b d -> p (h a b d)").bitcast(F32)
                                ins = nc.tensor.transpose(turn[:, n % 2, c * P:(c + 1) * P], pair,
                                                          const["ident"][:, :])
                            ins.then_inc(s["stacks_in_psum"], 1)

                    for t in range(TILES):
                        tok = slice(t * P, (t + 1) * P)
                        if t >= 2:
                            pe.wait_ge(s["rot_products"], 3 * (t - 1))
                            pe.wait_ge(s["v_done"], t - 1)
                        nc.tensor.matmul(work[:, t % 2, 0:2 * DIM], xTa[:, tok], w["qkv_a"][:, 0:2 * DIM],
                                         start=True, stop=False)
                        nc.tensor.matmul(work[:, t % 2, 0:2 * DIM], xTb[:, tok], w["qkv_b"][:, 0:2 * DIM],
                                         start=False, stop=True).then_inc(s["qk_in_psum"], 1)
                        nc.tensor.matmul(work[:, 2 + t % 2, 0:DIM], xTa[:, tok], w["qkv_a"][:, 2 * DIM:3 * DIM],
                                         start=True, stop=False)
                        nc.tensor.matmul(work[:, 2 + t % 2, 0:DIM], xTb[:, tok], w["qkv_b"][:, 2 * DIM:3 * DIM],
                                         start=False, stop=True).then_inc(s["v_in_psum"], 1)
                        if t >= 1:
                            stacks(t - 1)
                    stacks(TILES - 1)
                    pe.wait_ge(s["stacks_done"], 3 * TILES)
                    pe.wait_ge(s["v_done"], TILES)

                    def scores(i):
                        q, h = items[i]
                        if i >= 4:
                            pe.wait_ge(s["exp_done"], i - 3)
                        at = 64 * (h % 2)
                        qT = qkT[at:at + 64, h // 2, q * P:(q + 1) * P]
                        kT = qkT[at:at + 64, NH // 2 + h // 2, 0:(q + 1) * P]
                        nc.tensor.matmul(work[:, i % 4, 0:(q + 1) * P], qT, kT, start=True, stop=False)
                        nc.tensor.matmul(work[:, i % 4, q * P:(q + 1) * P], const["ident_r"][:, :],
                                         const["causal_r"][:, :], start=False,
                                         stop=True).then_inc(s["scores_in_psum"], 1)

                    def turn_probs(i):
                        q, h = items[i]
                        pe.wait_ge(s["exp_done"], i + 1)
                        if i >= 2:
                            pe.wait_ge(s["probsT_done"], i - 1)
                        for j in range(q + 1):
                            ins = nc.tensor.transpose(turn[:, i % 2, j * P:(j + 1) * P],
                                                      probs[:, i % 3, j * P:(j + 1) * P], const["ident"][:, :])
                        ins.then_inc(s["probsT_in_psum"], 1)

                    def weigh_values(i):
                        q, h = items[i]
                        pe.wait_ge(s["probsT_done"], i + 1)
                        if h == 0 and q >= 2:
                            pe.wait_ge(s["y_done"], q - 1)
                        for j in range(q + 1):
                            ins = nc.tensor.matmul(yps[:, q % 2, h * D0:(h + 1) * D0],
                                                   probsT[:, i % 2, j * P:(j + 1) * P],
                                                   v[:, j, h * D0:(h + 1) * D0],
                                                   start=(j == 0), stop=(j == q))
                        ins.then_inc(s["pv_done"], 1)

                    for i in range(len(items) + 3):
                        if i < len(items):
                            scores(i)
                        if 2 <= i < len(items) + 2:
                            turn_probs(i - 2)
                        if i >= 3:
                            weigh_values(i - 3)
                    for t in range(TILES):
                        pe.wait_ge(s["y_done"], t + 1)
                        nc.tensor.transpose(work[:, 0, t * P:(t + 1) * P], y[:, t, 0:CA], const["ident"][:, :])
                        nc.tensor.transpose(work[0:CB, 1, t * P:(t + 1) * P], y[:, t, CA:DIM],
                                            const["ident"][:, :]).then_inc(s["yT_in_psum"], 1)
                    pe.wait_ge(s["yT_done"], 2)
                    for t in range(TILES):
                        tok = slice(t * P, (t + 1) * P)
                        if t >= 2:
                            pe.wait_ge(s["hid_done"], t - 1)
                        nc.tensor.matmul(work[:, 2 + t % 2, 0:DIM], xTa[:, tok], w["proj_a"][:, :],
                                         start=True, stop=False)
                        nc.tensor.matmul(work[:, 2 + t % 2, 0:DIM], xTb[:, tok], w["proj_b"][:, :],
                                         start=False, stop=True).then_inc(s["out_in_psum"], 1)
            reset(nc, s["stats_done"], s["hid_done"])


def second_attention(nc, hid, const, w):
    QT, NH = TILES, H1
    N = NH * QT
    INNER = NH * D1
    CH = INNER // P
    with ExitStack() as ctx:
        def sb(name, shape, dt=F32):
            return ctx.enter_context(nc.sbuf_tensor(name, shape, dt))

        s = signals(nc, ctx, "attn1", """stats_done moments_done rstd_done norm_done xT_in_psum xT_done
            v_in_psum v_done qk_in_psum qk_hi_done qk_lo_done scores_in_psum max_done exp_done
            probsT_in_psum probsT_done pv_done rden_done y_done yT_in_psum yT_done
            out_in_psum hid_done""")
        stats, mv, rstd = sb("c_stats", [P, TILES, 6]), sb("c_mv", [P, TILES, 2]), sb("c_rstd", [P, TILES])
        xn = sb("c_xn", [P, TILES, DIM])
        xTa, xTb = sb("c_xTa", [P, SEQ]), sb("c_xTb", [CB + 1, SEQ])
        qs, kh, kl = sb("c_q", [P, 2, SEQ], F32R), sb("c_kh", [P, 2, SEQ], F32R), sb("c_kl", [P, 2, SEQ], F32R)
        v = sb("c_v", [P, TILES, INNER])
        probs, probsT = sb("c_probs", [P, 3, SEQ]), sb("c_probsT", [P, 2, SEQ])
        nmax, den, rden = sb("c_nmax", [P, N]), sb("c_den", [P, N]), sb("c_rden", [P, N])
        y, yT = sb("c_y", [P, TILES, INNER]), sb("c_yT", [P, CH, SEQ])
        work = ctx.enter_context(nc.psum_tensor("c_work", [P, 4, 512], F32))
        turn = ctx.enter_context(nc.psum_tensor("c_turn", [P, 2, 512], F32))
        yps = ctx.enter_context(nc.psum_tensor("c_y_ps", [P, 2, 512], F32))
        nc.vector.memset(xTb[CB:CB + 1, :], 1.0)
        nc.all_engine_barrier()
        VH = INNER // 2
        copy_by_act = [i % 4 == 3 for i in range(N)]

        with nc.Fori(0, BATCH) as b:
            rows = [hid[:, bass.ds(b * TILES + t, 1), :].rearrange("p o c -> p (o c)") for t in range(TILES)]
            with nc.Block() as block:
                @block.vector
                def _(dve):
                    layer_norm_vector(nc, dve, s, rows, stats, mv, rstd, xn)

                    def low_part(n):
                        h, is_k = n // 2, n % 2
                        dve.wait_ge(s["qk_hi_done"], n + 1)
                        if is_k:
                            nc.vector.tensor_tensor(kl[:, h % 2, :], work[:, 3, :],
                                                    kh[:, h % 2, :].bitcast(F32),
                                                    ALU.subtract).then_inc(s["qk_lo_done"], 1)
                        else:
                            low = qs[D1:P, h % 2, :]
                            nc.vector.scalar_tensor_tensor(low, work[D1:P, 3, :], D1 ** -0.5,
                                                           low.bitcast(F32), ALU.mult,
                                                           ALU.subtract).then_inc(s["qk_lo_done"], 1)

                    def copy_probs(i):
                        dve.wait_ge(s["probsT_in_psum"], i + 1)
                        if i >= 2:
                            dve.wait_ge(s["pv_done"], i - 1)
                        nc.vector.tensor_copy(probsT[:, i % 2, :], turn[:, i % 2, :]).then_inc(s["probsT_done"], 1)

                    def scale_y(h):
                        a, e = h * QT, (h + 1) * QT
                        dve.wait_ge(s["exp_done"], e)
                        nc.vector.reciprocal(rden[:, a:e], den[:, a:e]).then_inc(s["rden_done"], 1)
                        dve.wait_ge(s["rden_done"], h + 1)
                        dve.wait_ge(s["pv_done"], e)
                        nc.vector.scalar_tensor_tensor(
                            y[:, :, h * D1:(h + 1) * D1],
                            yps[:, h % 2, 0:QT * D1].rearrange("p (q d) -> p q d", q=QT),
                            w["head_scale"][:, h:h + 1],
                            rden[:, a:e].unsqueeze(2).broadcast_to([P, QT, D1]),
                            ALU.mult, ALU.mult).then_inc(s["y_done"], 1)

                    low_part(0)
                    low_part(1)
                    for i in range(N):
                        h, q = divmod(i, QT)
                        dve.wait_ge(s["scores_in_psum"], i + 1)
                        nc.vector.tensor_reduce(nmax[:, i:i + 1], work[:, i % 3, :], AX, ALU.max,
                                                negate=True).then_inc(s["max_done"], 1)
                        if h + 1 < NH and q == 1:
                            low_part(2 * h + 2)
                        if h + 1 < NH and q == 3:
                            low_part(2 * h + 3)
                        if i >= 2:
                            copy_probs(i - 2)
                        if i >= 5 and (i - 5) % QT == QT - 1:
                            scale_y((i - 5) // QT)
                    copy_probs(N - 2)
                    scale_y(NH - 2)
                    copy_probs(N - 1)
                    scale_y(NH - 1)
                    for t in range(TILES):
                        dve.wait_ge(s["out_in_psum"], t + 1)
                        nc.vector.tensor_tensor(rows[t], work[:, t % 2, 0:DIM], rows[t],
                                                ALU.add).then_inc(s["hid_done"], 1)

                @block.gpsimd
                def _(pool):
                    rstd_gpsimd(nc, pool, s["rstd_done"], mv, rstd, const["neg_half"], s["moments_done"])

                @block.scalar
                def _(act):
                    copy_transposed(nc, act, s, work[:, 0], work[:, 1], xTa, xTb)

                    def high_part(n):
                        h, is_k = n // 2, n % 2
                        act.wait_ge(s["qk_in_psum"], n + 1)
                        if h >= 2:
                            act.wait_ge(s["scores_in_psum"], QT * (h - 1))
                        dst = kh if is_k else qs
                        nc.scalar.activation(dst[:, h % 2, :], work[:, 3, :], ACT.Copy,
                                             scale=1.0 if is_k else D1 ** -0.5).then_inc(s["qk_hi_done"], 1)

                    for n in range(2 * TILES):
                        act.wait_ge(s["v_in_psum"], n + 1)
                        nc.scalar.copy(v[:, n // 2, (n % 2) * VH:(n % 2 + 1) * VH],
                                       work[:, n % 2, 0:VH]).then_inc(s["v_done"], 1)
                    high_part(0)
                    high_part(1)
                    for i in range(N):
                        h, q = divmod(i, QT)
                        act.wait_ge(s["max_done"], i + 1)
                        if i >= 3:
                            act.wait_ge(s["probsT_in_psum"], i - 2)
                        nc.scalar.activation(probs[:, i % 3, :], work[:, i % 3, :], ACT.Exp,
                                             bias=nmax[:, i:i + 1],
                                             accum_out=den[:, i:i + 1]).then_inc(s["exp_done"], 1)
                        if h + 1 < NH and q == 1:
                            high_part(2 * h + 2)
                        if h + 1 < NH and q == 3:
                            high_part(2 * h + 3)
                    for n in range(CH):
                        act.wait_ge(s["yT_in_psum"], n + 1)
                        nc.scalar.copy(yT[:, n, :], turn[:, n % 2, :]).then_inc(s["yT_done"], 1)

                @block.tensor
                def _(pe):
                    transpose_tokens(nc, pe, s, xn, work[:, 0], work[:, 1], const["ident"])
                    pe.wait_ge(s["xT_done"], 2)
                    for n in range(2 * TILES):
                        t, half = divmod(n, 2)
                        tok = slice(t * P, (t + 1) * P)
                        cols = slice(2 * NH * P + half * VH, 2 * NH * P + (half + 1) * VH)
                        if n >= 2:
                            pe.wait_ge(s["v_done"], n - 1)
                        nc.tensor.matmul(work[:, n % 2, 0:VH], xTa[:, tok], w["qkv_a"][:, cols],
                                         start=True, stop=False)
                        nc.tensor.matmul(work[:, n % 2, 0:VH], xTb[:, tok], w["qkv_b"][:, cols],
                                         start=False, stop=True).then_inc(s["v_in_psum"], 1)

                    def project(n):
                        h, is_k = n // 2, n % 2
                        if n >= 1:
                            pe.wait_ge(s["qk_lo_done"], n)
                        cols = slice((is_k * NH + h) * P, (is_k * NH + h + 1) * P)
                        nc.tensor.matmul(work[:, 3, :], w["qkv_a"][:, cols], xTa[:, :], start=True, stop=False)
                        nc.tensor.matmul(work[:, 3, :], w["qkv_b"][:, cols], xTb[:, :], start=False,
                                         stop=True).then_inc(s["qk_in_psum"], 1)

                    def scores(i):
                        h, q = divmod(i, QT)
                        if q == 0:
                            pe.wait_ge(s["qk_lo_done"], 2 * (h + 1))
                            pe.wait_ge(s["qk_hi_done"], 2 * (h + 1))
                        if i >= 3:
                            pe.wait_ge(s["exp_done"], i - 2)
                        qT = qs[:, h % 2, q * P:(q + 1) * P]
                        nc.tensor.matmul(work[:, i % 3, :], qT, kh[:, h % 2, :], start=True, stop=False)
                        nc.tensor.matmul(work[:, i % 3, :], qT, kl[:, h % 2, :], start=False,
                                         stop=True).then_inc(s["scores_in_psum"], 1)

                    def turn_probs(i):
                        pe.wait_ge(s["exp_done"], i + 1)
                        if i >= 2:
                            pe.wait_ge(s["probsT_done"], i - 1)
                        for j in range(TILES):
                            ins = nc.tensor.transpose(turn[:, i % 2, j * P:(j + 1) * P],
                                                      probs[:, i % 3, j * P:(j + 1) * P], const["ident"][:, :])
                        ins.then_inc(s["probsT_in_psum"], 1)

                    def weigh_values(i):
                        h, q = divmod(i, QT)
                        pe.wait_ge(s["probsT_done"], i + 1)
                        if q == 0 and h >= 2:
                            pe.wait_ge(s["y_done"], h - 1)
                        for j in range(TILES):
                            ins = nc.tensor.matmul(yps[:, h % 2, q * D1:(q + 1) * D1],
                                                   probsT[:, i % 2, j * P:(j + 1) * P],
                                                   v[:, j, h * D1:(h + 1) * D1],
                                                   start=(j == 0), stop=(j == TILES - 1))
                        ins.then_inc(s["pv_done"], 1)

                    project(0)
                    project(1)
                    pe.wait_ge(s["v_done"], 2 * TILES)
                    for i in range(N + 3):
                        if i < N:
                            h, q = divmod(i, QT)
                            scores(i)
                            if h + 1 < NH and q == 0:
                                project(2 * h + 2)
                            if h + 1 < NH and q == 2:
                                project(2 * h + 3)
                        if 2 <= i < N + 2:
                            turn_probs(i - 2)
                        if i >= 3:
                            weigh_values(i - 3)
                    pe.wait_ge(s["y_done"], NH)
                    for n in range(CH):
                        if n >= 2:
                            pe.wait_ge(s["yT_done"], n - 1)
                        for t in range(TILES):
                            ins = nc.tensor.transpose(turn[:, n % 2, t * P:(t + 1) * P],
                                                      y[:, t, n * P:(n + 1) * P], const["ident"][:, :])
                        ins.then_inc(s["yT_in_psum"], 1)
                    pe.wait_ge(s["yT_done"], CH)
                    for t in range(TILES):
                        if t >= 2:
                            pe.wait_ge(s["hid_done"], t - 1)
                        nc.tensor.matmul(work[:, t % 2, 0:DIM], const["ones_row"][0:1, :], w["out_bias"][0:1, :],
                                         start=True, stop=False)
                        for n in range(CH):
                            ins = nc.tensor.matmul(work[:, t % 2, 0:DIM], yT[:, n, t * P:(t + 1) * P],
                                                   w["out"][:, n, :], start=False, stop=(n == CH - 1))
                        ins.then_inc(s["out_in_psum"], 1)
            reset(nc, s["stats_done"], s["hid_done"])


def experts(nc, hid, const, w, tag, width, first_layer, out=None):
    NF = width // P
    N = EXPERTS * NF
    M = EXPERTS * TILES
    with ExitStack() as ctx:
        def sb(name, shape, dt=F32):
            return ctx.enter_context(nc.sbuf_tensor(f"{tag}_{name}", shape, dt))

        names = """stats_done moments_done rstd_done norm_done xT_in_psum xT_done gate_in_psum gate_done
            logits_in_psum shifted exp_done route combine_done combineT_in_psum combineT_done bias_in_psum
            hidden_in_psum hidden_done up_in_psum sum_done hid_done stored"""
        s = signals(nc, ctx, tag, names)
        stats, mv, rstd = sb("stats", [P, TILES, 6]), sb("mv", [P, TILES, 2]), sb("rstd", [P, TILES])
        xn = sb("xn", [P, TILES, DIM])
        xTa, xTb = sb("xTa", [P, SEQ]), sb("xTb", [CB, SEQ])
        gT = sb("gT", [GATE_HID + 1, SEQ])
        top = sb("top", [P, TILES])
        e = sb("e", [P, TILES, EXPERTS])
        esum = sb("esum", [P, TILES])
        best, where = sb("best", [P, TILES, 8]), sb("where", [P, TILES, 8], U32)
        wheref = sb("wheref", [P, TILES, 8])
        one, two = sb("one", [P, TILES, EXPERTS]), sb("two", [P, TILES, EXPERTS])
        combine = sb("combine", [P, TILES, EXPERTS])
        combineT = sb("combineT", [EXPERTS, SEQ])
        hiddenT = sb("hiddenT", [P, 2, NF, SEQ])
        work = ctx.enter_context(nc.psum_tensor(f"{tag}_work", [P, 4, 512], F32))
        ups = ctx.enter_context(nc.psum_tensor(f"{tag}_ups", [P, 4, 512], F32))
        nc.vector.memset(gT[GATE_HID:GATE_HID + 1, :], 1.0)
        nc.all_engine_barrier()

        with nc.Fori(0, BATCH) as b:
            rows = [hid[:, bass.ds(b * TILES + t, 1), :].rearrange("p o c -> p (o c)") for t in range(TILES)]
            with nc.Block() as block:
                @block.vector
                def _(dve):
                    layer_norm_vector(nc, dve, s, rows, stats, mv, rstd, xn)
                    dve.wait_ge(s["logits_in_psum"], 1)
                    logits = work[:, 3, 0:TILES * EXPERTS].rearrange("p (t e) -> p t e", t=TILES)
                    nc.vector.tensor_reduce(top[:, :], logits, AX, ALU.max).then_inc(s["route"], 1)
                    dve.wait_ge(s["route"], 1)
                    nc.vector.tensor_tensor(e[:, :, :], logits,
                                            top[:, :].unsqueeze(2).broadcast_to([P, TILES, EXPERTS]),
                                            ALU.subtract).then_inc(s["shifted"], 1)
                    dve.wait_ge(s["exp_done"], 1)
                    nc.vector.tensor_reduce(esum[:, :], e[:, :, :], AX, ALU.add).then_inc(s["route"], 1)
                    dve.wait_ge(s["route"], 2)
                    nc.vector.reciprocal(esum[:, :], esum[:, :]).then_inc(s["route"], 1)
                    dve.wait_ge(s["route"], 3)
                    wide = esum[:, :].unsqueeze(2).broadcast_to([P, TILES, EXPERTS])
                    nc.vector.tensor_tensor(e[:, :, :], e[:, :, :], wide, ALU.mult).then_inc(s["route"], 1)
                    dve.wait_ge(s["route"], 4)
                    for t in range(TILES):
                        nc.vector.max(best[:, t, :], e[:, t, :]).then_inc(s["route"], 1)
                    for t in range(TILES):
                        dve.wait_ge(s["route"], 5 + t)
                        nc.vector.max_index(where[:, t, :], best[:, t, :], e[:, t, :]).then_inc(s["route"], 1)
                    dve.wait_ge(s["route"], 4 + 2 * TILES)
                    nc.vector.tensor_copy(wheref[:, :, :], where[:, :, :]).then_inc(s["route"], 1)
                    dve.wait_ge(s["route"], 5 + 2 * TILES)
                    for k, mask in enumerate((one, two)):
                        place = wheref[:, :, k:k + 1].broadcast_to([P, TILES, EXPERTS])
                        nc.vector.tensor_tensor(mask[:, :, :], const["places"][:, :, :], place,
                                                ALU.is_equal).then_inc(s["route"], 1)
                    dve.wait_ge(s["route"], 7 + 2 * TILES)
                    nc.vector.tensor_tensor(one[:, :, :], one[:, :, :], two[:, :, :],
                                            ALU.add).then_inc(s["route"], 1)
                    dve.wait_ge(s["route"], 8 + 2 * TILES)
                    nc.vector.tensor_tensor(two[:, :, :], one[:, :, :], e[:, :, :],
                                            ALU.mult).then_inc(s["route"], 1)
                    dve.wait_ge(s["route"], 9 + 2 * TILES)
                    nc.vector.tensor_reduce(top[:, :], two[:, :, :], AX, ALU.add).then_inc(s["route"], 1)
                    dve.wait_ge(s["route"], 10 + 2 * TILES)
                    if first_layer:
                        nc.vector.tensor_scalar(top[:, :], top[:, :], 1e-8, None, ALU.add).then_inc(s["route"], 1)
                        dve.wait_ge(s["route"], 11 + 2 * TILES)
                    nc.vector.reciprocal(esum[:, :], top[:, :]).then_inc(s["route"], 1)
                    dve.wait_ge(s["route"], 11 + 2 * TILES + first_layer)
                    nc.vector.tensor_tensor(combine[:, :, :], two[:, :, :], wide,
                                            ALU.mult).then_inc(s["combine_done"], 1)
                    dve.wait_ge(s["combine_done"], 1)
                    if not first_layer:
                        for t in range(TILES):
                            dve.wait_ge(s["bias_in_psum"], t + 1)
                            nc.vector.tensor_tensor(rows[t], ups[:, t, 0:DIM], rows[t],
                                                    ALU.add).then_inc(s["sum_done"], 1)
                    base = 0 if first_layer else TILES
                    for m in range(M):
                        x, t = divmod(m, TILES)
                        dve.wait_ge(s["up_in_psum"], m + 1)
                        if m + base >= TILES:
                            dve.wait_ge(s["sum_done"], m + base - TILES + 1)
                        acc = xn[:, t, :] if first_layer else rows[t]
                        nc.vector.scalar_tensor_tensor(acc, ups[:, m % 4, 0:DIM], combine[:, t, x:x + 1], acc,
                                                       ALU.mult, ALU.add).then_inc(s["sum_done"], 1)
                    if first_layer:
                        dve.wait_ge(s["sum_done"], M)
                        for t in range(TILES):
                            nc.vector.bn_stats(stats[:, t, :], xn[:, t, :]).then_inc(s["stats_done"], 1)
                        for t in range(TILES):
                            dve.wait_ge(s["stats_done"], TILES + t + 1)
                            nc.vector.bn_aggr(mv[:, t, :], stats[:, t, :]).then_inc(s["moments_done"], 1)
                        dve.wait_ge(s["moments_done"], 2 * TILES)
                        dve.wait_ge(s["rstd_done"], 4)
                        for t in range(TILES):
                            nc.vector.tensor_scalar(xn[:, t, :], xn[:, t, :], mv[:, t, 0:1], rstd[:, t:t + 1],
                                                    ALU.subtract, ALU.mult).then_inc(s["norm_done"], 1)
                        dve.wait_ge(s["norm_done"], 2 * TILES)
                        for k, (par, op) in enumerate(((w["gamma"], ALU.mult), (w["beta"], ALU.add))):
                            if k:
                                dve.wait_ge(s["hid_done"], k)
                            nc.vector.tensor_tensor(xn[:, :, :], xn[:, :, :],
                                                    par[:, :].unsqueeze(1).broadcast_to([P, TILES, DIM]),
                                                    op).then_inc(s["hid_done"], 1)
                        dve.wait_ge(s["hid_done"], 2)
                        for t in range(TILES):
                            nc.vector.tensor_tensor(rows[t], xn[:, t, :], rows[t],
                                                    ALU.add).then_inc(s["hid_done"], 1)
                        dve.wait_ge(s["hid_done"], 2 + TILES)

                @block.gpsimd
                def _(pool):
                    rstd_gpsimd(nc, pool, s["rstd_done"], mv, rstd, const["neg_half"], s["moments_done"])
                    if first_layer:
                        pool.wait_ge(s["moments_done"], 2 * TILES)
                        nc.gpsimd.tensor_scalar(rstd[:, :], mv[:, :, 1], LN_EPS, None,
                                                ALU.add).then_inc(s["rstd_done"], 1)
                        pool.wait_ge(s["rstd_done"], 3)
                        nc.gpsimd.tensor_tensor(rstd[:, :], rstd[:, :], const["neg_half"][:, :],
                                                ALU.pow).then_inc(s["rstd_done"], 1)

                @block.sync
                def _(sp):
                    if out is not None:
                        sp.wait_ge(s["sum_done"], TILES + M)
                        sp.dma_start(out.rearrange("(t p) c -> p t c", p=P)[:, bass.ds(b * TILES, TILES), :],
                                     hid[:, bass.ds(b * TILES, TILES), :]).then_inc(s["stored"], 16)
                        sp.wait_ge(s["stored"], 16)

                @block.scalar
                def _(act):
                    copy_transposed(nc, act, s, work[:, 0], work[:, 1], xTa, xTb)
                    if first_layer:
                        act.wait_ge(s["gate_in_psum"], 1)
                        nc.scalar.activation(gT[0:GATE_HID, :], work[0:GATE_HID, 2, :], ACT.Gelu,
                                             bias=w["gate_bias"][:, 0:1]).then_inc(s["gate_done"], 1)
                    act.wait_ge(s["shifted"], 1)
                    nc.scalar.activation(e[:, :, :], e[:, :, :], ACT.Exp).then_inc(s["exp_done"], 1)
                    if not first_layer:
                        act.wait_ge(s["combineT_in_psum"], 1)
                        nc.scalar.copy(combineT[:, :], work[0:EXPERTS, 2, :]).then_inc(s["combineT_done"], 1)
                    for n in range(N):
                        x, c = divmod(n, NF)
                        act.wait_ge(s["hidden_in_psum"], n + 1)
                        if x >= 2 and c == 0:
                            act.wait_ge(s["up_in_psum"], TILES * (x - 1))
                        nc.scalar.activation(hiddenT[:, x % 2, c, :], work[:, n % 4, :], ACT.Gelu,
                                             bias=w["bias1"][:, n:n + 1]).then_inc(s["hidden_done"], 1)

                @block.tensor
                def _(pe):
                    transpose_tokens(nc, pe, s, xn, work[:, 0], work[:, 1], const["ident"])
                    pe.wait_ge(s["xT_done"], 2)
                    if first_layer:
                        nc.tensor.matmul(work[0:GATE_HID, 2, :], w["gate_a"][:, :], xTa[:, :],
                                         start=True, stop=False)
                        nc.tensor.matmul(work[0:GATE_HID, 2, :], w["gate_b"][:, :], xTb[:, :], start=False,
                                         stop=True).then_inc(s["gate_in_psum"], 1)
                        pe.wait_ge(s["gate_done"], 1)
                    for t in range(TILES):
                        tok = slice(t * P, (t + 1) * P)
                        lg = work[:, 3, t * EXPERTS:(t + 1) * EXPERTS]
                        if first_layer:
                            ins = nc.tensor.matmul(lg, gT[:, tok], w["gate2"][:, :], start=True, stop=True)
                        else:
                            nc.tensor.matmul(lg, xTa[:, tok], w["router_a"][:, :], start=True, stop=False)
                            ins = nc.tensor.matmul(lg, xTb[:, tok], w["router_b"][:, :], start=False, stop=True)
                    ins.then_inc(s["logits_in_psum"], 1)

                    def hidden(n):
                        x, c = divmod(n, NF)
                        if n >= 4:
                            pe.wait_ge(s["hidden_done"], n - 3)
                        if n % 4 == 3 and n < 4:
                            pe.wait_ge(s["shifted"], 1)
                        cols = slice(c * P, (c + 1) * P)
                        nc.tensor.matmul(work[:, n % 4, :], w["down_a"][:, x, cols], xTa[:, :],
                                         start=True, stop=False)
                        nc.tensor.matmul(work[:, n % 4, :], w["down_b"][:, x, cols], xTb[:, :],
                                         start=False, stop=True).then_inc(s["hidden_in_psum"], 1)

                    def up(x):
                        pe.wait_ge(s["hidden_done"], NF * (x + 1))
                        for t in range(TILES):
                            m = x * TILES + t
                            if m >= 4 or not first_layer:
                                pe.wait_ge(s["sum_done"], m - 3 + (0 if first_layer else TILES))
                            for c in range(NF):
                                ins = nc.tensor.matmul(ups[:, m % 4, 0:DIM],
                                                       hiddenT[:, x % 2, c, t * P:(t + 1) * P],
                                                       w["up"][:, x, c, :], start=(c == 0), stop=(c == NF - 1))
                            ins.then_inc(s["up_in_psum"], 1)

                    if not first_layer:
                        pe.wait_ge(s["combine_done"], 1)
                        for t in range(TILES):
                            ins = nc.tensor.transpose(work[0:EXPERTS, 2, t * P:(t + 1) * P], combine[:, t, :],
                                                      const["ident"][:, :])
                        ins.then_inc(s["combineT_in_psum"], 1)
                        pe.wait_ge(s["combineT_done"], 1)
                        for t in range(TILES):
                            nc.tensor.matmul(ups[:, t, 0:DIM], combineT[:, t * P:(t + 1) * P], w["bias2"][:, :],
                                             start=True, stop=True).then_inc(s["bias_in_psum"], 1)
                    for x in range(EXPERTS + 1):
                        if x < EXPERTS:
                            for c in range(NF):
                                hidden(x * NF + c)
                        if x >= 1:
                            up(x - 1)
            reset(nc, s["stats_done"], s["stored"])


def build(nc, io, out, phases=4):
    with ExitStack() as ctx:
        def sb(name, shape, dt=F32):
            return ctx.enter_context(nc.sbuf_tensor(name, shape, dt))

        hid = sb("hid", [P, BATCH * TILES, DIM])
        idx = sb("tok_ids", [P, BATCH * TILES], U32)
        const = {}
        const["ident"] = sb("ident", [P, P])
        const["ident_r"], const["causal_r"] = sb("ident_r", [P, P], F32R), sb("causal_r", [P, P], F32R)
        const["causal"] = sb("causal", [P, P])
        const["cos"], const["sin"] = sb("rope_cos", [P, TILES, 2, D0]), sb("rope_sin", [P, TILES, 2, D0])
        const["places"] = sb("places", [P, TILES, EXPERTS])
        const["neg_half"] = sb("neg_half", [P, TILES])
        const["ones_row"] = sb("ones_row", [1, P])
        inputs_in = ctx.enter_context(nc.semaphore("inputs_in"))
        consts_done = ctx.enter_context(nc.semaphore("consts_done"))

        w_first = ExitStack()
        w0, f0 = {}, {}
        loads = []

        def weight(scope, group, name, shape, src):
            t = scope.enter_context(nc.sbuf_tensor(name, shape, F32))
            group[name.split(".")[1]] = t
            loads.append((t, src))

        with w_first:
            def w(group, name, shape, src):
                weight(w_first, group, name, shape, src)

            w(w0, "attn0.qkv_a", [P, 3 * DIM], io["L0_qkv"][0:CA, :])
            w(w0, "attn0.qkv_b", [CB + 1, 3 * DIM], io["L0_qkv"][CA:DIM + 1, :])
            w(w0, "attn0.proj_a", [P, DIM], io["L0_proj"][0:CA, :])
            w(w0, "attn0.proj_b", [CB + 1, DIM], io["L0_proj"][CA:DIM + 1, :])
            w(f0, "ffn0.gate_a", [P, GATE_HID], io["L0_ffn_w1"][0:CA, :])
            w(f0, "ffn0.gate_b", [CB, GATE_HID], io["L0_ffn_w1"][CA:DIM, :])
            w(f0, "ffn0.gate_bias", [GATE_HID, 1], io["L0_ffn_b1"])
            w(f0, "ffn0.gate2", [GATE_HID + 1, EXPERTS], io["L0_gate2"])
            w(f0, "ffn0.down_a", [P, EXPERTS, F0], io["L0_down"][0:CA])
            w(f0, "ffn0.down_b", [CB, EXPERTS, F0], io["L0_down"][CA:DIM])
            w(f0, "ffn0.bias1", [P, EXPERTS * F0 // P], io["L0_down_bias"])
            w(f0, "ffn0.up", [P, EXPERTS, F0 // P, DIM], io["L0_up"])
            w(f0, "ffn0.gamma", [P, DIM], io["L0_ffn_gamma"].broadcast_to([P, DIM]))
            w(f0, "ffn0.beta", [P, DIM], io["L0_ffn_beta"].broadcast_to([P, DIM]))
            for t, src in ((const["ident"], io["ident"]), (const["causal"], io["causal"]), (const["cos"], io["cos"]),
                           (const["sin"], io["sin"]), (const["places"], io["places"])):
                loads.append((t, src))

            def weights_in(sp):
                for t, src in loads:
                    sp.dma_start(t[:], src).then_inc(inputs_in, 16)

            embed(nc, io, hid, idx, const, weights_in)
            with nc.Block() as block:
                @block.vector
                def _(dve):
                    dve.wait_ge(inputs_in, 16 * len(loads))
                    nc.vector.tensor_copy(const["ident_r"][:, :], const["ident"][:, :])
                    nc.vector.tensor_copy(const["causal_r"][:, :], const["causal"][:, :])
                    nc.vector.memset(const["neg_half"][:, :], -0.5)
                    nc.vector.memset(const["ones_row"][:, :], 1.0).then_inc(consts_done, 1)
                    dve.wait_ge(consts_done, 1)
            if phases >= 1:
                first_attention(nc, hid, const, w0)
            if phases >= 2:
                experts(nc, hid, const, f0, "d", F0, True)

        def load_weights(name, scope, group, which):
            done = ctx.enter_context(nc.semaphore(name))
            loads.clear()
            for n, shape, src in which:
                weight(scope, group, n, shape, src)
            with nc.Block() as block:
                @block.sync
                def _(sp):
                    for t, src in loads:
                        sp.dma_start(t[:], src).then_inc(done, 16)
                    sp.wait_ge(done, 16 * len(loads))

        if phases >= 3:
            with ExitStack() as scope:
                w1 = {}
                cols = 2 * H1 * P + H1 * D1
                load_weights("w1_in", scope, w1, [
                    ("attn1.qkv_a", [P, cols], io["L1_qkv"][0:CA, :]),
                    ("attn1.qkv_b", [CB + 1, cols], io["L1_qkv"][CA:DIM + 1, :]),
                    ("attn1.out", [P, H1 * D1 // P, DIM], io["L1_out"]),
                    ("attn1.out_bias", [1, DIM], io["L1_attn_b_out"]),
                    ("attn1.reattn", [H1, D1 * D1], io["L1_attn_reattn_weights"])])
                w1["head_scale"] = scope.enter_context(nc.sbuf_tensor("head_scale", [P, H1], F32))
                with ExitStack() as sub:
                    hs = sub.enter_context(nc.sbuf_tensor("reattn_sum", [H1, 1], F32))
                    diag = sub.enter_context(nc.sbuf_tensor("reattn_diag", [H1, H1], F32))
                    ones = sub.enter_context(nc.sbuf_tensor("ones_heads", [H1, P], F32))
                    ps = sub.enter_context(nc.psum_tensor("head_scale_ps", [P, 512], F32))
                    summed = sub.enter_context(nc.semaphore("reattn_summed"))
                    spread = sub.enter_context(nc.semaphore("reattn_spread"))
                    with nc.Block() as block:
                        @block.vector
                        def _(dve):
                            nc.vector.memset(ones[:, :], 1.0).then_inc(summed, 1)
                            nc.vector.tensor_reduce(hs[:, :], w1["reattn"][:, :], AX, ALU.add).then_inc(summed, 1)
                            dve.wait_ge(summed, 2)
                            nc.vector.tensor_scalar(diag[:, :], const["ident"][0:H1, 0:H1], hs[:, 0:1], None,
                                                    ALU.mult).then_inc(summed, 1)
                            dve.wait_ge(spread, 1)
                            nc.vector.tensor_copy(w1["head_scale"][:, :], ps[:, 0:H1]).then_inc(summed, 1)
                            dve.wait_ge(summed, 4)

                        @block.tensor
                        def _(pe):
                            pe.wait_ge(summed, 3)
                            nc.tensor.matmul(ps[:, 0:H1], ones[:, :], diag[:, :], start=True,
                                             stop=True).then_inc(spread, 1)
                second_attention(nc, hid, const, w1)
        if phases >= 4:
            with ExitStack() as scope:
                f1 = {}
                load_weights("f1_in", scope, f1, [
                    ("ffn1.router_a", [P, EXPERTS], io["L1_router"][0:CA, :]),
                    ("ffn1.router_b", [CB, EXPERTS], io["L1_router"][CA:DIM, :]),
                    ("ffn1.down_a", [P, EXPERTS, F1], io["L1_down"][0:CA]),
                    ("ffn1.down_b", [CB, EXPERTS, F1], io["L1_down"][CA:DIM]),
                    ("ffn1.bias1", [P, EXPERTS * F1 // P], io["L1_down_bias"]),
                    ("ffn1.up", [P, EXPERTS, F1 // P, DIM], io["L1_up"]),
                    ("ffn1.bias2", [EXPERTS, DIM], io["L1_ffn_b2"])])
                experts(nc, hid, const, f1, "g", F1, False, out)
        if phases < 4:
            done = ctx.enter_context(nc.semaphore("dump"))
            with nc.Block() as block:
                @block.sync
                def _(sp):
                    sp.dma_start(out.rearrange("(t p) c -> p t c", p=P), hid[:, :, :]).then_inc(done, 16)
                    sp.wait_ge(done, 16)


def layout(x, L0_tok_weights, L0_tok_emb_weight, L0_attn_Wq, L0_attn_bq, L0_attn_Wk, L0_attn_bk, L0_attn_Wv,
           L0_attn_bv, L0_attn_Wp, L0_attn_bp, L0_ffn_w1, L0_ffn_b1, L0_ffn_w2, L0_ffn_b2, L0_ffn_down_w,
           L0_ffn_down_b, L0_ffn_up_w, L0_ffn_gamma, L0_ffn_beta, L1_attn_w_qkv, L1_attn_b_qkv,
           L1_attn_reattn_weights, L1_attn_w_out, L1_attn_b_out, L1_ffn_router_w, L1_ffn_w1, L1_ffn_b1,
           L1_ffn_w2, L1_ffn_b2):
    a = {}
    a["tok"] = x.reshape(BATCH * TILES, P).T.astype(np.uint32)
    a["L0_tok_weights"] = L0_tok_weights[:, None]
    a["L0_tok_emb_weight"] = L0_tok_emb_weight
    a["L0_qkv"] = np.concatenate([np.concatenate([wt.T, bi[None]]) for wt, bi in (
        (L0_attn_Wq, L0_attn_bq), (L0_attn_Wk, L0_attn_bk), (L0_attn_Wv, L0_attn_bv))], axis=1)
    a["L0_proj"] = np.concatenate([L0_attn_Wp.T, L0_attn_bp[None]])
    a["L0_ffn_w1"], a["L0_ffn_b1"] = L0_ffn_w1, L0_ffn_b1[:, None]
    a["L0_gate2"] = np.concatenate([L0_ffn_w2, L0_ffn_b2[None]])
    a["L0_down"] = L0_ffn_down_w.transpose(1, 0, 2)
    a["L0_down_bias"] = L0_ffn_down_b.reshape(EXPERTS * F0 // P, P).T
    a["L0_up"] = L0_ffn_up_w.reshape(EXPERTS, F0 // P, P, DIM).transpose(2, 0, 1, 3)
    a["L0_ffn_gamma"], a["L0_ffn_beta"] = L0_ffn_gamma[None], L0_ffn_beta[None]
    qkv = np.concatenate([L1_attn_w_qkv, L1_attn_b_qkv[None]])
    inner = H1 * D1
    twice = np.repeat(qkv[:, 0:2 * inner].reshape(DIM + 1, 2 * H1, 1, D1), 2, axis=2)
    a["L1_qkv"] = np.concatenate([twice.reshape(DIM + 1, 4 * inner), qkv[:, 2 * inner:]], axis=1)
    a["L1_out"] = L1_attn_w_out.reshape(inner // P, P, DIM).transpose(1, 0, 2)
    a["L1_attn_b_out"] = L1_attn_b_out[None]
    a["L1_attn_reattn_weights"] = L1_attn_reattn_weights.reshape(H1, D1 * D1)
    a["L1_router"] = L1_ffn_router_w.T
    a["L1_down"] = L1_ffn_w1.transpose(1, 0, 2)
    a["L1_down_bias"] = L1_ffn_b1.reshape(EXPERTS * F1 // P, P).T
    a["L1_up"] = L1_ffn_w2.reshape(EXPERTS, F1 // P, P, DIM).transpose(2, 0, 1, 3)
    a["L1_ffn_b2"] = L1_ffn_b2
    a["mix_mask"] = (np.arange(DIM)[None] < np.array(EMBED_DIMS)[:, None]).astype(np.float32)
    a["ident"] = np.eye(P, dtype=np.float32)
    a["causal"] = np.where(np.arange(P)[None] > np.arange(P)[:, None], MASKED, 0).astype(np.float32)
    a["places"] = np.broadcast_to(np.arange(EXPERTS, dtype=np.float32), (P, TILES, EXPERTS))
    f = np.float32
    inv = (f(1) / f(10000) ** (f(2) * np.arange(D0 // 2, dtype=f) / f(D0))).astype(f)
    ang = np.arange(SEQ, dtype=f)[:, None] * inv[None]
    cos = np.repeat(np.cos(ang), 2, axis=1)
    sin = np.stack([-np.sin(ang), np.sin(ang)], axis=-1).reshape(SEQ, D0)
    for name, table in (("cos", cos), ("sin", sin)):
        both = np.stack([table * f(D0 ** -0.5), table], axis=1)
        a[name] = both.reshape(TILES, P, 2, D0).transpose(1, 0, 2, 3)
    return {k: np.ascontiguousarray(v) for k, v in a.items()}


def declare(nc, arrays):
    io = {}
    for name, v in arrays.items():
        io[name] = nc.dram_tensor(f"in_{name}", v.shape, mybir.dt.from_np(v.dtype), kind="ExternalInput").ap()
    out = nc.dram_tensor("out", (BATCH * SEQ, DIM), F32, kind="ExternalOutput").ap()
    return io, out


def kernel(**inputs):
    import concourse.bacc as bacc
    from concourse.bass_utils import run_bass_kernel_spmd

    arrays = layout(**{k: np.asarray(v) for k, v in inputs.items()})
    nc = bacc.Bacc("TRN2", target_bir_lowering=False, num_devices=1)
    io, out = declare(nc, arrays)
    build(nc, io, out)
    r = run_bass_kernel_spmd(nc, [{f"in_{k}": v for k, v in arrays.items()}], core_ids=[0])
    return r.results[0]["out"].reshape(BATCH, SEQ, DIM)
```

```python
from contextlib import ExitStack

import numpy as np

import concourse.bass as bass
from concourse import mybir

F32 = mybir.dt.float32
F32R = mybir.dt.float32r
U32 = mybir.dt.uint32
ALU = mybir.AluOpType
ACT = mybir.ActivationFunctionType
AX = mybir.AxisListType.X

P = 128
BATCH, SEQ = 8, 512
TILES = SEQ // P
DIM = 192
CA, CB = 128, DIM - 128
VOCAB = 50257
EMBED_DIMS = (192, 96, 144, 192)
EXPERTS = 8
LN_EPS = 1e-5
H0, D0 = 12, 16
H1, D1 = 12, 64
GATE_HID = 96
F0, F1 = 256, 768
MASKED = -1e30
SLOT_TILES = 2 * BATCH * TILES + EXPERTS
ROUNDS = 9


def signals(nc, ctx, prefix, names):
    return {n: ctx.enter_context(nc.semaphore(f"{prefix}.{n}")) for n in names.split()}


def reset(nc, handles):
    nums = sorted(h.num for h in handles)
    start = nums[0]
    for n, after in zip(nums, nums[1:] + [None]):
        if after != n + 1:
            nc.sync.sem_clear(range(start, n + 1))
            start = after
    nc.all_engine_barrier(sem_only=True)


def layer_norm_vector(nc, dve, s, rows, stats, mv, rstd, xn):
    for t in range(TILES):
        nc.vector.bn_stats(stats[:, t, :], rows[t]).then_inc(s["stats_done"], 1)
    for t in range(TILES):
        dve.wait_ge(s["stats_done"], t + 1)
        nc.vector.bn_aggr(mv[:, t, :], stats[:, t, :]).then_inc(s["moments_done"], 1)
    dve.wait_ge(s["rstd_done"], 2)
    dve.wait_ge(s["moments_done"], TILES)
    for t in range(TILES):
        nc.vector.tensor_scalar(xn[:, t, :], rows[t], mv[:, t, 0:1], rstd[:, t:t + 1],
                                ALU.subtract, ALU.mult).then_inc(s["norm_done"], 1)


def rstd_gpsimd(nc, pool, s, mv, rstd, neg_half, moments, first=0, tiles=TILES):
    pool.wait_ge(moments, tiles)
    nc.gpsimd.tensor_scalar(rstd[:, :], mv[:, :, 1], LN_EPS, None, ALU.add).then_inc(s, 1)
    pool.wait_ge(s, first + 1)
    nc.gpsimd.tensor_tensor(rstd[:, :], rstd[:, :], neg_half[:, :], ALU.pow).then_inc(s, 1)


def transpose_tokens(nc, pe, s, xn, psum_a, psum_b, ident):
    for t in range(TILES):
        pe.wait_ge(s["norm_done"], t + 1)
        nc.tensor.transpose(psum_a[:, t * P:(t + 1) * P], xn[:, t, 0:CA], ident[:, :])
        nc.tensor.transpose(psum_b[0:CB, t * P:(t + 1) * P], xn[:, t, CA:DIM],
                            ident[:, :]).then_inc(s["xT_in_psum"], 1)


def copy_transposed(nc, act, s, psum_a, psum_b, xTa, xTb):
    act.wait_ge(s["xT_in_psum"], TILES)
    nc.scalar.copy(xTa[:, :], psum_a[:, 0:SEQ]).then_inc(s["xT_done"], 1)
    nc.scalar.copy(xTb[0:CB, :], psum_b[0:CB, 0:SEQ]).then_inc(s["xT_done"], 1)


def embed(nc, io, hid, idx, const, weights_in, pool_sems):
    with ExitStack() as ctx:
        s = signals(nc, ctx, "embed", "idx_in mix_in scaled_w col_in_psum col_done hid_done")
        rows_in = pool_sems[0:BATCH]
        w4 = ctx.enter_context(nc.sbuf_tensor("mix_w", [4, 1], F32))
        w4b = ctx.enter_context(nc.sbuf_tensor("mix_w_wide", [4, P], F32))
        mask4 = ctx.enter_context(nc.sbuf_tensor("mix_mask", [4, DIM], F32))
        col = ctx.enter_context(nc.sbuf_tensor("col_scale", [P, DIM], F32))
        col_ps = ctx.enter_context(nc.psum_tensor("col_scale_ps", [P, 512], F32))
        with nc.Block() as block:
            @block.sync
            def _(sp):
                sp.dma_start(idx[:, :], io["tok"]).then_inc(s["idx_in"], 16)
                sp.dma_start(w4[:, :], io["L0_tok_weights"]).then_inc(s["mix_in"], 16)
                sp.dma_start(mask4[:, :], io["mix_mask"]).then_inc(s["mix_in"], 16)
                weights_in(sp)

            @block.gpsimd
            def _(pool):
                pool.wait_ge(s["idx_in"], 16)
                for t in range(BATCH * TILES):
                    nc.gpsimd.indirect_dma_start(
                        hid[:, t, :], None, io["L0_tok_emb_weight"],
                        bass.IndirectOffsetOnAxis(ap=idx[:, t:t + 1], axis=0),
                    ).then_inc(rows_in[t // TILES], 16)

            @block.tensor
            def _(pe):
                pe.wait_ge(s["scaled_w"], 2)
                nc.tensor.matmul(col_ps[:, 0:DIM], w4b[:, :], mask4[:, :],
                                 start=True, stop=True).then_inc(s["col_in_psum"], 1)

            @block.vector
            def _(dve):
                nc.vector.memset(w4b[:, :], 1.0).then_inc(s["scaled_w"], 1)
                dve.wait_ge(s["mix_in"], 32)
                dve.wait_ge(s["scaled_w"], 1)
                nc.vector.tensor_scalar(w4b[:, :], w4b[:, :], w4[:, 0:1], None,
                                        ALU.mult).then_inc(s["scaled_w"], 1)
                dve.wait_ge(s["col_in_psum"], 1)
                nc.vector.tensor_copy(col[:, :], col_ps[:, 0:DIM]).then_inc(s["col_done"], 1)
                dve.wait_ge(s["col_done"], 1)
                for g in range(BATCH):
                    dve.wait_ge(rows_in[g], 16 * TILES)
                    h4 = hid[:, g * TILES:(g + 1) * TILES, :]
                    nc.vector.tensor_tensor(h4, h4, col[:, :].unsqueeze(1).broadcast_to([P, TILES, DIM]),
                                            ALU.mult).then_inc(s["hid_done"], 1)
                dve.wait_ge(s["hid_done"], BATCH)
        reset(nc, s.values())


def first_attention(nc, hid, const, w):
    QT, NH = TILES, H0
    items = [(q, h) for q in range(QT) for h in range(NH)]
    with ExitStack() as ctx:
        def sb(name, shape, dt=F32):
            return ctx.enter_context(nc.sbuf_tensor(name, shape, dt))

        s = signals(nc, ctx, "attn0", """stats_done moments_done rstd_done norm_done xT_in_psum xT_done
            qk_in_psum v_in_psum v_done rot_products rotated hi_done lo_done stacks_in_psum
            stacks_done scores_in_psum max_done exp_done probsT_in_psum probsT_done pv_done
            rden_done y_done yT_in_psum yT_done out_in_psum hid_done""")
        stats, mv, rstd = sb("a_stats", [P, TILES, 6]), sb("a_mv", [P, TILES, 2]), sb("a_rstd", [P, TILES])
        xn = sb("a_xn", [P, TILES, DIM])
        xTa, xTb = sb("a_xTa", [P, SEQ]), sb("a_xTb", [CB + 1, SEQ])
        rc, rs = sb("a_rot_cos", [P, 2, 2 * NH, D0]), sb("a_rot_sin", [P, 2, 2 * NH, D0])
        stack = sb("a_stack", [P, 2, 2 * NH, 2, 2, D0], F32R)
        qkT = sb("a_qkT", [P, NH, SEQ], F32R)
        v = sb("a_v", [P, TILES, DIM])
        probs, probsT = sb("a_probs", [P, 3, SEQ]), sb("a_probsT", [P, 2, SEQ])
        nmax, den, rden = sb("a_nmax", [P, QT * NH]), sb("a_den", [P, QT * NH]), sb("a_rden", [P, QT * NH])
        y = sb("a_y", [P, TILES, DIM])
        work = ctx.enter_context(nc.psum_tensor("a_work", [P, 4, 512], F32))
        turn = ctx.enter_context(nc.psum_tensor("a_turn", [P, 2, 512], F32))
        yps = ctx.enter_context(nc.psum_tensor("a_y_ps", [P, 2, 512], F32))
        nc.vector.memset(xTb[CB:CB + 1, :], 1.0)
        nc.all_engine_barrier()

        with nc.Fori(0, BATCH) as b:
            rows = [hid[:, bass.ds(b * TILES + t, 1), :].rearrange("p o c -> p (o c)") for t in range(TILES)]
            with nc.Block() as block:
                def copy_probs(dve, i):
                    q = items[i][0]
                    dve.wait_ge(s["probsT_in_psum"], i + 1)
                    if i >= 2:
                        dve.wait_ge(s["pv_done"], i - 1)
                    nc.vector.tensor_copy(probsT[:, i % 2, 0:(q + 1) * P],
                                          turn[:, i % 2, 0:(q + 1) * P]).then_inc(s["probsT_done"], 1)

                def scale_y(dve, q):
                    a, e = q * NH, (q + 1) * NH
                    dve.wait_ge(s["exp_done"], e)
                    nc.vector.reciprocal(rden[:, a:e], den[:, a:e]).then_inc(s["rden_done"], 1)
                    dve.wait_ge(s["rden_done"], q + 1)
                    dve.wait_ge(s["pv_done"], e)
                    nc.vector.tensor_tensor(
                        y[:, q, :].rearrange("p (h d) -> p h d", h=NH),
                        yps[:, q % 2, 0:DIM].rearrange("p (h d) -> p h d", h=NH),
                        rden[:, a:e].unsqueeze(2).broadcast_to([P, NH, D0]), ALU.mult).then_inc(s["y_done"], 1)

                @block.vector
                def _(dve):
                    layer_norm_vector(nc, dve, s, rows, stats, mv, rstd, xn)
                    for t in range(TILES):
                        dve.wait_ge(s["qk_in_psum"], t + 1)
                        if t >= 2:
                            dve.wait_ge(s["rotated"], t - 1)
                        qk = work[:, t % 2, 0:2 * DIM].rearrange("p (a h d) -> p a h d", a=2, h=NH)
                        cos = const["cos"][:, t].unsqueeze(2).broadcast_to([P, 2, NH, D0])
                        nc.vector.tensor_tensor(rc[:, t % 2].rearrange("p (a h) d -> p a h d", a=2), qk, cos,
                                                ALU.mult).then_inc(s["rot_products"], 1)
                        for a in range(2):
                            pair = work[:, t % 2, a * DIM:(a + 1) * DIM].rearrange(
                                "p (h i two) -> p h i two", h=NH, two=2)
                            dst = rs[:, t % 2, a * NH:(a + 1) * NH].rearrange("p h (i two) -> p h i two", two=2)
                            sin = const["sin"][:, t, a, :].rearrange("p (i two) -> p i two", two=2)
                            sin = sin.unsqueeze(1).broadcast_to([P, NH, D0 // 2, 2])
                            nc.vector.tensor_tensor(dst, pair[:, :, :, ::-1], sin,
                                                    ALU.mult).then_inc(s["rot_products"], 1)

                    for i, (q, h) in enumerate(items):
                        dve.wait_ge(s["scores_in_psum"], i + 1)
                        nc.vector.tensor_reduce(nmax[:, i:i + 1], work[:, i % 4, 0:(q + 1) * P], AX, ALU.max,
                                                negate=True).then_inc(s["max_done"], 1)
                        if i >= 2:
                            copy_probs(dve, i - 2)
                        if i >= 5 and (i - 5) % NH == NH - 1:
                            scale_y(dve, (i - 5) // NH)
                    for i in (len(items) - 2, len(items) - 1):
                        copy_probs(dve, i)
                    scale_y(dve, QT - 1)
                    for t in range(TILES):
                        dve.wait_ge(s["out_in_psum"], t + 1)
                        nc.vector.tensor_tensor(rows[t], work[:, 2 + t % 2, 0:DIM], rows[t],
                                                ALU.add).then_inc(s["hid_done"], 1)

                @block.gpsimd
                def _(pool):
                    rstd_gpsimd(nc, pool, s["rstd_done"], mv, rstd, const["neg_half"], s["moments_done"])
                    for t in range(TILES):
                        pool.wait_ge(s["rot_products"], 3 * (t + 1))
                        nc.gpsimd.tensor_tensor(rc[:, t % 2], rc[:, t % 2], rs[:, t % 2],
                                                ALU.add).then_inc(s["rotated"], 1)
                        pool.wait_ge(s["rotated"], t + 1)
                        pool.wait_ge(s["hi_done"], 2 * (t + 1))
                        if t >= 2:
                            pool.wait_ge(s["stacks_in_psum"], 3 * (t - 1))
                        st = stack[:, t % 2]
                        for a in range(2):
                            heads = slice(a * NH, (a + 1) * NH)
                            r = rc[:, t % 2, heads, :].unsqueeze(2).broadcast_to([P, NH, 2, D0])
                            hi = st[:, heads, 0, :, :] if a == 0 else st[:, heads, :, 0, :]
                            lo = st[:, heads, 1, :, :] if a == 0 else st[:, heads, :, 1, :]
                            nc.gpsimd.tensor_tensor(lo, r, hi.bitcast(F32), ALU.subtract).then_inc(s["lo_done"], 1)

                def copy_stacks(act, t):
                    for j in range(3):
                        n = 3 * t + j
                        act.wait_ge(s["stacks_in_psum"], n + 1)
                        nc.scalar.copy(qkT[:, 4 * j:4 * j + 4, t * P:(t + 1) * P],
                                       turn[:, n % 2, :].rearrange("p (c k) -> p c k", c=4)
                                       ).then_inc(s["stacks_done"], 1)

                @block.scalar
                def _(act):
                    copy_transposed(nc, act, s, work[:, 0], work[:, 1], xTa, xTb)
                    for t in range(TILES):
                        act.wait_ge(s["v_in_psum"], t + 1)
                        nc.scalar.copy(v[:, t, :], work[:, 2 + t % 2, 0:DIM]).then_inc(s["v_done"], 1)
                        act.wait_ge(s["rotated"], t + 1)
                        if t >= 2:
                            act.wait_ge(s["stacks_in_psum"], 3 * (t - 1))
                        st = stack[:, t % 2]
                        for a in range(2):
                            heads = slice(a * NH, (a + 1) * NH)
                            r = rc[:, t % 2, heads, :].unsqueeze(2).broadcast_to([P, NH, 2, D0])
                            hi = st[:, heads, 0, :, :] if a == 0 else st[:, heads, :, 0, :]
                            nc.scalar.copy(hi, r).then_inc(s["hi_done"], 1)
                        if t >= 1:
                            copy_stacks(act, t - 1)
                    copy_stacks(act, TILES - 1)
                    for i, (q, h) in enumerate(items):
                        act.wait_ge(s["max_done"], i + 1)
                        if i >= 3:
                            act.wait_ge(s["probsT_in_psum"], i - 2)
                        n = (q + 1) * P
                        nc.scalar.activation(probs[:, i % 3, 0:n], work[:, i % 4, 0:n], ACT.Exp,
                                             bias=nmax[:, i:i + 1],
                                             accum_out=den[:, i:i + 1]).then_inc(s["exp_done"], 1)
                    act.wait_ge(s["yT_in_psum"], TILES)
                    nc.scalar.copy(xTa[:, :], work[:, 0, :]).then_inc(s["yT_done"], 1)
                    nc.scalar.copy(xTb[0:CB, :], work[0:CB, 1, :]).then_inc(s["yT_done"], 1)

                @block.tensor
                def _(pe):
                    transpose_tokens(nc, pe, s, xn, work[:, 0], work[:, 1], const["ident"])
                    pe.wait_ge(s["xT_done"], 2)

                    def stacks(t):
                        pe.wait_ge(s["hi_done"], 2 * (t + 1))
                        pe.wait_ge(s["lo_done"], 2 * (t + 1))
                        for j in range(3):
                            n = 3 * t + j
                            if n >= 2:
                                pe.wait_ge(s["stacks_done"], n - 1)
                            for c in range(4):
                                pair = stack[:, t % 2, 2 * (4 * j + c):2 * (4 * j + c) + 2].rearrange(
                                    "p h a b d -> p (h a b d)").bitcast(F32)
                                ins = nc.tensor.transpose(turn[:, n % 2, c * P:(c + 1) * P], pair,
                                                          const["ident"][:, :])
                            ins.then_inc(s["stacks_in_psum"], 1)

                    for t in range(TILES):
                        tok = slice(t * P, (t + 1) * P)
                        if t >= 2:
                            pe.wait_ge(s["rot_products"], 3 * (t - 1))
                            pe.wait_ge(s["v_done"], t - 1)
                        nc.tensor.matmul(work[:, t % 2, 0:2 * DIM], xTa[:, tok], w["qkv_a"][:, 0:2 * DIM],
                                         start=True, stop=False)
                        nc.tensor.matmul(work[:, t % 2, 0:2 * DIM], xTb[:, tok], w["qkv_b"][:, 0:2 * DIM],
                                         start=False, stop=True).then_inc(s["qk_in_psum"], 1)
                        nc.tensor.matmul(work[:, 2 + t % 2, 0:DIM], xTa[:, tok], w["qkv_a"][:, 2 * DIM:3 * DIM],
                                         start=True, stop=False)
                        nc.tensor.matmul(work[:, 2 + t % 2, 0:DIM], xTb[:, tok], w["qkv_b"][:, 2 * DIM:3 * DIM],
                                         start=False, stop=True).then_inc(s["v_in_psum"], 1)
                        if t >= 1:
                            stacks(t - 1)
                    stacks(TILES - 1)
                    pe.wait_ge(s["stacks_done"], 3 * TILES)
                    pe.wait_ge(s["v_done"], TILES)

                    def scores(i):
                        q, h = items[i]
                        if i >= 4:
                            pe.wait_ge(s["exp_done"], i - 3)
                        at = 64 * (h % 2)
                        qT = qkT[at:at + 64, h // 2, q * P:(q + 1) * P]
                        kT = qkT[at:at + 64, NH // 2 + h // 2, 0:(q + 1) * P]
                        nc.tensor.matmul(work[:, i % 4, 0:(q + 1) * P], qT, kT, start=True, stop=False)
                        nc.tensor.matmul(work[:, i % 4, q * P:(q + 1) * P], const["ident_r"][:, :],
                                         const["causal_r"][:, :], start=False,
                                         stop=True).then_inc(s["scores_in_psum"], 1)

                    def turn_probs(i):
                        q, h = items[i]
                        pe.wait_ge(s["exp_done"], i + 1)
                        if i >= 2:
                            pe.wait_ge(s["probsT_done"], i - 1)
                        for j in range(q + 1):
                            ins = nc.tensor.transpose(turn[:, i % 2, j * P:(j + 1) * P],
                                                      probs[:, i % 3, j * P:(j + 1) * P], const["ident"][:, :])
                        ins.then_inc(s["probsT_in_psum"], 1)

                    def weigh_values(i):
                        q, h = items[i]
                        pe.wait_ge(s["probsT_done"], i + 1)
                        if h == 0 and q >= 2:
                            pe.wait_ge(s["y_done"], q - 1)
                        for j in range(q + 1):
                            ins = nc.tensor.matmul(yps[:, q % 2, h * D0:(h + 1) * D0],
                                                   probsT[:, i % 2, j * P:(j + 1) * P],
                                                   v[:, j, h * D0:(h + 1) * D0],
                                                   start=(j == 0), stop=(j == q))
                        ins.then_inc(s["pv_done"], 1)

                    for i in range(len(items) + 3):
                        if i < len(items):
                            scores(i)
                        if 2 <= i < len(items) + 2:
                            turn_probs(i - 2)
                        if i >= 3:
                            weigh_values(i - 3)
                    for t in range(TILES):
                        pe.wait_ge(s["y_done"], t + 1)
                        nc.tensor.transpose(work[:, 0, t * P:(t + 1) * P], y[:, t, 0:CA], const["ident"][:, :])
                        nc.tensor.transpose(work[0:CB, 1, t * P:(t + 1) * P], y[:, t, CA:DIM],
                                            const["ident"][:, :]).then_inc(s["yT_in_psum"], 1)
                    pe.wait_ge(s["yT_done"], 2)
                    for t in range(TILES):
                        tok = slice(t * P, (t + 1) * P)
                        if t >= 2:
                            pe.wait_ge(s["hid_done"], t - 1)
                        nc.tensor.matmul(work[:, 2 + t % 2, 0:DIM], xTa[:, tok], w["proj_a"][:, :],
                                         start=True, stop=False)
                        nc.tensor.matmul(work[:, 2 + t % 2, 0:DIM], xTb[:, tok], w["proj_b"][:, :],
                                         start=False, stop=True).then_inc(s["out_in_psum"], 1)
            reset(nc, s.values())


def split_weights(nc, io, w, scope):
    cols = 3 * H1 * D1
    for name in ("a_hi", "a_lo", "b_hi", "b_lo"):
        w[name] = scope.enter_context(nc.sbuf_tensor(f"attn1.{name}", [P, cols], F32R))
    with ExitStack() as sub:
        wa = sub.enter_context(nc.sbuf_tensor("attn1.a", [P, cols], F32))
        wb = sub.enter_context(nc.sbuf_tensor("attn1.b", [P, cols], F32))
        bias = sub.enter_context(nc.sbuf_tensor("attn1.bias", [1, cols], F32))
        bias_hi = sub.enter_context(nc.sbuf_tensor("attn1.bias_hi", [1, cols], F32R))
        loaded = sub.enter_context(nc.semaphore("attn1.qkv_in"))
        rounded = sub.enter_context(nc.semaphore("attn1.qkv_hi"))
        split = sub.enter_context(nc.semaphore("attn1.qkv_lo"))
        with nc.Block() as block:
            @block.sync
            def _(sp):
                sp.dma_start(wa[:, :], io["L1_qkv"][0:CA, :]).then_inc(loaded, 16)
                for k in range(2):
                    sp.dma_start(wb[k * CB:(k + 1) * CB, :], io["L1_qkv"][CA:DIM, :]).then_inc(loaded, 16)
                sp.dma_start(bias[:, :], io["L1_qkv"][DIM:DIM + 1, :]).then_inc(loaded, 16)

            @block.scalar
            def _(act):
                act.wait_ge(loaded, 64)
                nc.scalar.copy(bias_hi[:, :], bias[:, :]).then_inc(rounded, 1)
                nc.scalar.copy(w["a_hi"][:, :], wa[:, :]).then_inc(rounded, 1)
                nc.scalar.copy(w["b_hi"][:, :], wb[:, :]).then_inc(rounded, 1)

            @block.vector
            def _(dve):
                nc.vector.memset(w["b_lo"][CB:P, :].bitcast(F32), 0.0).then_inc(split, 1)
                dve.wait_ge(split, 1)
                dve.wait_ge(rounded, 3)
                nc.vector.tensor_copy(w["b_lo"][CB:CB + 1, :], bias_hi[:, :].bitcast(F32)).then_inc(split, 1)
                nc.vector.tensor_tensor(w["b_lo"][96:97, :], bias[:, :], bias_hi[:, :].bitcast(F32),
                                        ALU.subtract).then_inc(split, 1)
                nc.vector.tensor_tensor(w["a_lo"][:, :], wa[:, :], w["a_hi"][:, :].bitcast(F32),
                                        ALU.subtract).then_inc(split, 1)
                nc.vector.tensor_tensor(w["b_lo"][0:CB, :], wb[0:CB, :], w["b_hi"][0:CB, :].bitcast(F32),
                                        ALU.subtract).then_inc(split, 1)
                dve.wait_ge(split, 5)


def second_attention(nc, hid, const, w):
    QT, NH = TILES, H1
    INNER = NH * D1
    CH = INNER // P
    VH = INNER // 2
    WIDE = D1 + 1
    scale = D1 ** -0.5

    shared = {(g, 3): [("maxima", g + 1)] for g in range(NH)}
    slots = [(g, j) for g in range(NH) for j in range(3)]

    def share(first, kind, numbers):
        for at, n in zip(slots[slots.index(first):], numbers):
            shared[at] = [(kind, n)]

    share((1, 0), "v_high", range(TILES - 1))
    share((2, 0), "yT", range(CH))
    share((4, 0), "v_high", [TILES - 1])
    share((4, 1), "out", range(TILES))
    share((8, 1), "xT_a", [0])
    share((8, 2), "xT_b", [0])
    share((10, 0), "v_low", range(TILES))
    steps = [(g, j) for g in range(NH) for j in range(4)]

    with ExitStack() as ctx:
        def sb(name, shape, dt=F32):
            return ctx.enter_context(nc.sbuf_tensor(name, shape, dt))

        s = signals(nc, ctx, "attn1", """stats_done moments_done rstd_done norm_done x_hi_done x_lo_done
            bank_filled bank_taken qk_in_psum qk_hi_done q_twice qk_lo_done k_copied scores_in_psum max_done
            turned_in_psum exp_done pv_done rden_done y_done hid_done""")
        stats, mv, rstd = sb("c_stats", [P, TILES, 6]), sb("c_mv", [P, TILES, 2]), sb("c_rstd", [P, TILES])
        xn = sb("c_xn", [P, TILES, DIM + CB])
        xa, xb = sb("c_xa", [P, SEQ]), sb("c_xb", [P, SEQ])
        a_hi, a_lo = sb("c_a_hi", [P, SEQ], F32R), sb("c_a_lo", [P, SEQ], F32R)
        b_both, b_one = sb("c_b_both", [P, SEQ], F32R), sb("c_b_one", [P, SEQ], F32R)
        q_hi, q_lo = sb("c_q_hi", [P, 4, SEQ], F32R), sb("c_q_lo", [WIDE, 4, SEQ], F32R)
        k_both, k_one = sb("c_k_both", [P, 4, SEQ], F32R), sb("c_k_one", [WIDE, 4, SEQ], F32R)
        v = sb("c_v", [P, TILES, NH, WIDE])
        probs = sb("c_probs", [P, 2, TILES, SEQ])
        nmax = sb("c_nmax", [P, NH * QT], F32R)
        rden = sb("c_rden", [P, NH, QT])
        y, yT = sb("c_y", [P, TILES, INNER]), sb("c_yT", [P, CH, SEQ])
        added = sb("c_added", [P, TILES, DIM])
        rows_ps = ctx.enter_context(nc.psum_tensor("c_scores", [P, 2, 512], F32))
        cols_ps = ctx.enter_context(nc.psum_tensor("c_turned", [P, 2, 512], F32))
        y_ps = ctx.enter_context(nc.psum_tensor("c_y_ps", [P, 2, 512], F32))
        qk_ps = ctx.enter_context(nc.psum_tensor("c_qk_ps", [P, 512], F32))
        bank = ctx.enter_context(nc.psum_tensor("c_bank", [P, 512], F32))
        nc.vector.tensor_copy(b_one[CB:P, :], const["bias_rows"][CB:P, 0:1].broadcast_to([CB, SEQ]))
        for k in range(4):
            nc.vector.tensor_copy(k_one[D1:WIDE, k, :], const["ones_row"][0:1, 0:1].broadcast_to([1, SEQ]))
        nc.vector.memset(v[:, :, :, D1:WIDE], 1.0)
        nc.all_engine_barrier()

        def wait(eng, sem, value):
            if value > 0:
                eng.wait_ge(s[sem], value)

        def halves(h):
            low, high = slice(0, D1), slice(D1, P)
            return (high, low) if h % 2 else (low, high)

        def sequence(b, has_prev, has_own, has_next):
            def mine(h):
                return has_prev if h < 0 else has_own if h < NH else has_next

            def rows(seq, t):
                return hid[:, bass.ds(seq * TILES + t, 1), :].rearrange("p o c -> p (o c)")

            def projected(g, j):
                h, is_k = (g + 3, 0) if g % 2 else (g + 2, 1)
                return [(h, is_k), (h + 1, is_k)] if j == (1 if is_k else 3) and mine(h) else []

            def repeated(g, j):
                return [g + 2, g + 3] if g % 2 == 0 and j == 1 and mine(g + 2) else []

            def uses(g, j):
                wanted = {"xT_a": has_next, "xT_b": has_next, "v_low": has_next, "v_high": has_own,
                          "yT": has_prev, "out": has_prev}
                return [(kind, n) for kind, n in shared.get((g, j), [])
                        if (mine(n) if kind == "maxima" else wanted[kind])]

            everything = [use for g, j in steps for use in uses(g, j)]
            place = {use: i for i, use in enumerate(everything)}
            qk = [hk for g, j in steps for hk in projected(g, j)]
            order = {hk: i for i, hk in enumerate(qk)}
            q_order = {h: i for i, h in enumerate(h for g, j in steps for h in repeated(g, j))}
            k_order = {h: i for i, (h, _) in enumerate(hk for hk in qk if hk[1])}
            scored = [h for h in range(1, NH + 1) if mine(h)]

            def score_place(h, q):
                return QT * (h - scored[0]) + q

            def turned_count(h):
                return TILES * (h + 1) if has_own else 0

            def pv_count(h):
                return QT * (h + (2 if has_prev else 1))

            def y_count(h):
                return h + (3 if has_prev else 1)

            with nc.Block() as block:
                @block.vector
                def _(dve):
                    def moments():
                        for t in range(TILES):
                            nc.vector.bn_stats(stats[:, t, :], rows(b + 1, t)).then_inc(s["stats_done"], 1)
                        for t in range(TILES):
                            dve.wait_ge(s["stats_done"], t + 1)
                            nc.vector.bn_aggr(mv[:, t, :], stats[:, t, :]).then_inc(s["moments_done"], 1)

                    def norm():
                        dve.wait_ge(s["rstd_done"], 2)
                        dve.wait_ge(s["moments_done"], TILES)
                        for t in range(TILES):
                            nc.vector.tensor_scalar(xn[:, t, 0:DIM], rows(b + 1, t), mv[:, t, 0:1], rstd[:, t:t + 1],
                                                    ALU.subtract, ALU.mult).then_inc(s["norm_done"], 1)
                        dve.wait_ge(s["norm_done"], TILES)
                        nc.vector.tensor_copy(xn[:, :, DIM:DIM + CB], xn[:, :, CA:DIM]).then_inc(s["norm_done"], 1)

                    def split_x():
                        dve.wait_ge(s["bank_taken"], place["xT_a", 0] + 1)
                        if has_own:
                            dve.wait_ge(s["qk_in_psum"], order[NH - 2, 1] // 2 + 1)
                        nc.vector.tensor_copy(a_hi[:, :], xa[:, :]).then_inc(s["x_hi_done"], 1)
                        dve.wait_ge(s["bank_taken"], place["xT_b", 0] + 1)
                        nc.vector.tensor_copy(b_both[:, :], xb[:, :]).then_inc(s["x_hi_done"], 1)
                        nc.vector.tensor_copy(b_one[0:CB, :], xb[0:CB, :]).then_inc(s["x_hi_done"], 1)
                        dve.wait_ge(s["x_hi_done"], 2)
                        nc.vector.tensor_tensor(a_lo[:, :], xa[:, :], a_hi[:, :].bitcast(F32),
                                                ALU.subtract).then_inc(s["x_lo_done"], 1)
                        low = b_both[CB:P, :]
                        nc.vector.tensor_tensor(low, xb[CB:P, :], low.bitcast(F32),
                                                ALU.subtract).then_inc(s["x_lo_done"], 1)

                    def row_max(h, q):
                        n = score_place(h, q)
                        dve.wait_ge(s["scores_in_psum"], n + 1)
                        nc.vector.tensor_reduce(nmax[:, n:n + 1], rows_ps[:, n % 2, :], AX, ALU.max,
                                                negate=True).then_inc(s["max_done"], 1)

                    def low_part(h, is_k):
                        own, other = halves(h)
                        dve.wait_ge(s["qk_hi_done"], order[h, is_k] + 1)
                        wait(dve, "turned_in_psum", turned_count(h - 4))
                        if is_k:
                            nc.vector.tensor_tensor(k_both[other, h % 4, :], qk_ps[own, :],
                                                    k_both[own, h % 4, :].bitcast(F32),
                                                    ALU.subtract).then_inc(s["qk_lo_done"], 1)
                        else:
                            nc.vector.scalar_tensor_tensor(q_lo[0:D1, h % 4, :], qk_ps[own, :], scale,
                                                           q_hi[own, h % 4, :].bitcast(F32), ALU.mult,
                                                           ALU.subtract).then_inc(s["qk_lo_done"], 1)

                    def scale_y(h):
                        wait(dve, "pv_done", pv_count(h))
                        hh = h % NH
                        got = y_ps[:, h % 2, 0:QT * WIDE].rearrange("p (q d) -> p q d", q=QT)
                        nc.vector.reciprocal(rden[:, hh, :], got[:, :, D1]).then_inc(s["rden_done"], 1)
                        dve.wait_ge(s["rden_done"], y_count(h))
                        if h >= 0 and has_prev:
                            dve.wait_ge(s["bank_filled"], place["yT", hh // 2] + 1)
                        nc.vector.scalar_tensor_tensor(
                            y[:, :, hh * D1:(hh + 1) * D1], got[:, :, 0:D1], w["head_scale"][:, hh:hh + 1],
                            rden[:, hh, :].unsqueeze(2).broadcast_to([P, QT, D1]),
                            ALU.mult, ALU.mult).then_inc(s["y_done"], 1)

                    for g, j in steps:
                        if mine(g + 1):
                            for q in ((0, 1), (2, 3), (), ())[j]:
                                row_max(g + 1, q)
                        for h, is_k in projected(g, j):
                            low_part(h, is_k)
                        if j == 1 and mine(g - 2):
                            scale_y(g - 2)
                        if has_next and (g, j) == (5, 3):
                            moments()
                        if has_next and (g, j) == (6, 3):
                            norm()
                        if has_next and (g, j) == (8, 3):
                            split_x()

                @block.gpsimd
                def _(pool):
                    for g, j in steps:
                        for h, is_k in projected(g, j):
                            if is_k:
                                pool.wait_ge(s["qk_hi_done"], order[h, 1] + 1)
                                wait(pool, "turned_in_psum", turned_count(h - 4))
                                nc.gpsimd.tensor_copy(k_one[0:D1, h % 4, :], k_both[halves(h)[0], h % 4, :]
                                                      ).then_inc(s["k_copied"], 1)
                                pool.wait_ge(s["k_copied"], k_order[h] + 1)
                        if has_next and (g, j) == (5, 3):
                            rstd_gpsimd(nc, pool, s["rstd_done"], mv, rstd, const["neg_half"], s["moments_done"])
                            pool.wait_ge(s["rstd_done"], 2)
                        for kind, t in uses(g, j):
                            if kind == "out":
                                pool.wait_ge(s["bank_taken"], place[kind, t] + 1)
                                nc.gpsimd.tensor_tensor(rows(b - 1, t), added[:, t, :], rows(b - 1, t),
                                                        ALU.add).then_inc(s["hid_done"], 1)
                                pool.wait_ge(s["hid_done"], t + 1)

                @block.scalar
                def _(act):
                    def high_part(h, is_k):
                        own, other = halves(h)
                        act.wait_ge(s["qk_in_psum"], order[h, is_k] // 2 + 1)
                        wait(act, "turned_in_psum", turned_count(h - 4))
                        dst, by = (k_both, 1.0) if is_k else (q_hi, scale)
                        nc.scalar.activation(dst[own, h % 4, :], qk_ps[own, :], ACT.Copy,
                                             scale=by).then_inc(s["qk_hi_done"], 1)

                    def repeat_q(h):
                        own, other = halves(h)
                        if (h, 0) in order:
                            act.wait_ge(s["qk_hi_done"], order[h, 0] + 1)
                            wait(act, "turned_in_psum", turned_count(h - 4))
                        nc.scalar.copy(q_hi[other, h % 4, :], q_hi[own, h % 4, :]).then_inc(s["q_twice"], 1)

                    def exponentials(h, j):
                        n = TILES * h + j
                        act.wait_ge(s["turned_in_psum"], n + 1)
                        if mine(h - 2):
                            wait(act, "pv_done", pv_count(h - 2))
                        nc.scalar.activation(probs[:, h % 2, j, :], cols_ps[:, n % 2, :],
                                             ACT.Exp).then_inc(s["exp_done"], 1)

                    def take(kind, n):
                        act.wait_ge(s["bank_filled"], place[kind, n] + 1)
                        src = bank[:, :]
                        if kind == "maxima":
                            dst, src = q_lo[D1:WIDE, n % 4, :], bank[D1:WIDE, :]
                        elif kind == "xT_a":
                            dst = xa[:, :]
                        elif kind == "xT_b":
                            dst = xb[:, :]
                        elif kind in ("v_low", "v_high"):
                            if kind == "v_high" and has_prev:
                                act.wait_ge(s["pv_done"], pv_count(-1))
                            if kind == "v_low" and has_own:
                                act.wait_ge(s["pv_done"], pv_count(NH // 2 - 1))
                            heads = slice(0, NH // 2) if kind == "v_low" else slice(NH // 2, NH)
                            dst = v[:, n, heads, 0:D1]
                            src = bank[:, 0:VH].rearrange("p (h d) -> p h d", d=D1)
                        elif kind == "yT":
                            dst = yT[:, n, :]
                        else:
                            dst, src = added[:, n, :], bank[:, 0:DIM]
                        nc.scalar.copy(dst, src).then_inc(s["bank_taken"], 1)

                    for g, j in steps:
                        for use in uses(g, j):
                            take(*use)
                        if mine(g):
                            exponentials(g, j)
                        for h, is_k in projected(g, j):
                            high_part(h, is_k)
                        for h in repeated(g, j):
                            repeat_q(h)

                @block.tensor
                def _(pe):
                    def wait_x(h):
                        if h >= NH:
                            pe.wait_ge(s["x_hi_done"], 3)
                            pe.wait_ge(s["x_lo_done"], 2)

                    def project(h, is_k):
                        wait(pe, "qk_lo_done", order[h, is_k])
                        wait_x(h)
                        hh = h % NH
                        c = slice((is_k * NH + hh) * D1, (is_k * NH + hh + 2) * D1)
                        pairs = ((w["a_hi"], a_hi), (w["b_hi"], b_both), (w["a_hi"], a_lo),
                                 (w["a_lo"], a_hi), (w["b_lo"], b_one))
                        for i, (m, x) in enumerate(pairs):
                            ins = nc.tensor.matmul(qk_ps[:, :], m[:, c], x[:, :], start=(i == 0),
                                                   stop=(i == len(pairs) - 1))
                        ins.then_inc(s["qk_in_psum"], 1)

                    def scores(h, q):
                        n = score_place(h, q)
                        if q == 0:
                            if (h, 1) in order:
                                pe.wait_ge(s["qk_lo_done"], order[h, 1] + 1)
                            if h in q_order:
                                pe.wait_ge(s["q_twice"], q_order[h] + 1)
                        wait(pe, "max_done", n - 1)
                        nc.tensor.matmul(rows_ps[:, n % 2, :], q_hi[:, h % 4, q * P:(q + 1) * P],
                                         k_both[:, h % 4, :], start=True, stop=True).then_inc(s["scores_in_psum"], 1)

                    def scores_turned(h, j):
                        n = TILES * h + j
                        if j == 0:
                            if ("maxima", h) in place:
                                pe.wait_ge(s["bank_taken"], place["maxima", h] + 1)
                            if h in k_order:
                                pe.wait_ge(s["k_copied"], k_order[h] + 1)
                        wait(pe, "exp_done", n - 1)
                        keys = slice(j * P, (j + 1) * P)
                        nc.tensor.matmul(cols_ps[:, n % 2, :], k_both[:, h % 4, keys], q_hi[:, h % 4, :],
                                         start=True, stop=False)
                        nc.tensor.matmul(cols_ps[:, n % 2, :], k_one[:, h % 4, keys], q_lo[:, h % 4, :],
                                         start=False, stop=True).then_inc(s["turned_in_psum"], 1)

                    def weigh_values(h, q):
                        if q == 0:
                            if h >= 0:
                                pe.wait_ge(s["exp_done"], TILES * (h + 1))
                            if mine(h - 2):
                                wait(pe, "y_done", y_count(h - 2))
                            if h >= NH // 2:
                                pe.wait_ge(s["bank_taken"], place["v_high", TILES - 1] + 1)
                        for j in range(TILES):
                            ins = nc.tensor.matmul(y_ps[:, h % 2, q * WIDE:(q + 1) * WIDE],
                                                   probs[:, h % 2, j, q * P:(q + 1) * P],
                                                   v[:, j, h % NH, :],
                                                   start=(j == 0), stop=(j == TILES - 1))
                        ins.then_inc(s["pv_done"], 1)

                    def fill(kind, n):
                        wait(pe, "bank_taken", place[kind, n])
                        if kind == "maxima":
                            pe.wait_ge(s["max_done"], score_place(n, QT - 1) + 1)
                            for q in range(QT):
                                i = score_place(n, q)
                                ins = nc.tensor.matmul(bank[0:WIDE, q * P:(q + 1) * P],
                                                       nmax[:, i:i + 1].broadcast_to([P, WIDE]),
                                                       const["ident_r"][:, :], start=True, stop=True)
                        elif kind in ("xT_a", "xT_b"):
                            pe.wait_ge(s["norm_done"], TILES + 1)
                            c = 0 if kind == "xT_a" else CA
                            for t in range(TILES):
                                ins = nc.tensor.transpose(bank[:, t * P:(t + 1) * P], xn[:, t, c:c + P],
                                                          const["ident"][:, :])
                        elif kind in ("v_low", "v_high"):
                            if kind == "v_low":
                                wait_x(NH)
                            tok = slice(n * P, (n + 1) * P)
                            first = 2 * INNER + (0 if kind == "v_low" else VH)
                            cols = slice(first, first + VH)
                            pairs = ((a_hi, w["a_hi"]), (b_both, w["b_hi"]), (a_lo, w["a_hi"]),
                                     (a_hi, w["a_lo"]), (b_one, w["b_lo"]))
                            for i, (x, m) in enumerate(pairs):
                                ins = nc.tensor.matmul(bank[:, 0:VH], x[:, tok], m[:, cols],
                                                       start=(i == 0), stop=(i == len(pairs) - 1))
                        elif kind == "yT":
                            pe.wait_ge(s["y_done"], y_count(-1))
                            for t in range(TILES):
                                ins = nc.tensor.transpose(bank[:, t * P:(t + 1) * P],
                                                          y[:, t, n * P:(n + 1) * P], const["ident"][:, :])
                        else:
                            nc.tensor.matmul(bank[:, 0:DIM], const["ones_row"][0:1, :], w["out_bias"][0:1, :],
                                             start=True, stop=False)
                            for c in range(CH):
                                ins = nc.tensor.matmul(bank[:, 0:DIM], yT[:, c, n * P:(n + 1) * P],
                                                       w["out"][:, c, :], start=False, stop=(c == CH - 1))
                        ins.then_inc(s["bank_filled"], 1)

                    for g, j in steps:
                        for use in uses(g, j):
                            fill(*use)
                        if mine(g + 1):
                            for q in ((0, 1), (2, 3), (), ())[j]:
                                scores(g + 1, q)
                        if mine(g):
                            scores_turned(g, j)
                        if mine(g - 1):
                            weigh_values(g - 1, j)
                        for h, is_k in projected(g, j)[0:1]:
                            project(h, is_k)
            reset(nc, s.values())

        sequence(-1, False, False, True)
        sequence(0, False, True, True)
        with nc.Fori(1, BATCH - 1) as b:
            sequence(b, True, True, True)
        sequence(BATCH - 1, True, True, False)
        sequence(BATCH, True, False, False)


def route(nc, hid, xn_all, const, w, tag, first_layer, logits):
    ALL = BATCH * TILES
    R = 8
    with ExitStack() as ctx:
        def sb(name, shape, dt=F32):
            return ctx.enter_context(nc.sbuf_tensor(f"{tag}_{name}", shape, dt))

        s = signals(nc, ctx, tag + "route", """stats_done moments_done rstd_done norm_done kept xT_in_psum
            xTa_done xTb_done gate_in_psum gate_done logits_in_psum logits_done""")
        stats, mv, rstd = sb("stats", [P, ALL, 6]), sb("mv", [P, ALL, 2]), sb("rstd", [P, ALL])
        xn = sb("xn", [P, R, DIM])
        xTa, xTb = sb("xTa", [P, R * P]), sb("xTb", [CB, R * P])
        gT = sb("gT", [GATE_HID + 1, R * P])
        ps_a = ctx.enter_context(nc.psum_tensor(f"{tag}_xT_a", [P, R * P], F32))
        ps_b = ctx.enter_context(nc.psum_tensor(f"{tag}_xT_b", [P, R * P], F32))
        ps_g = ctx.enter_context(nc.psum_tensor(f"{tag}_gate", [P, R * P], F32))
        ps_l = ctx.enter_context(nc.psum_tensor(f"{tag}_logits_ps", [P, 512], F32))
        with nc.Block() as block:
            @block.vector
            def _(dve):
                nc.vector.memset(gT[GATE_HID:GATE_HID + 1, :], 1.0).then_inc(s["gate_done"], 1)
                dve.wait_ge(s["gate_done"], 1)
                with dve.Fori(0, ALL) as t:
                    nc.vector.bn_stats(stats[:, bass.ds(t, 1), :].rearrange("p o c -> p (o c)"),
                                       hid[:, bass.ds(t, 1), :].rearrange("p o c -> p (o c)")
                                       ).then_inc(s["stats_done"], 1)
                dve.wait_ge(s["stats_done"], ALL)
                for t in range(ALL):
                    nc.vector.bn_aggr(mv[:, t, :], stats[:, t, :]).then_inc(s["moments_done"], 1)

            @block.gpsimd
            def _(pool):
                pool.wait_ge(s["moments_done"], ALL)
                nc.gpsimd.tensor_scalar(rstd[:, :], mv[:, :, 1], LN_EPS, None,
                                        ALU.add).then_inc(s["rstd_done"], 1)
                pool.wait_ge(s["rstd_done"], 1)
                nc.gpsimd.tensor_tensor(rstd[:, :], rstd[:, :], const["neg_half"][:, 0:1].broadcast_to([P, ALL]),
                                        ALU.pow).then_inc(s["rstd_done"], 1)
                pool.wait_ge(s["rstd_done"], 2)
        reset(nc, s.values())

        with nc.Fori(0, ALL // R) as r:
            with nc.Block() as block:
                @block.vector
                def _(dve):
                    for j in range(R):
                        t = bass.ds(r * R + j, 1)
                        nc.vector.tensor_scalar(xn[:, j, :], hid[:, t, :].rearrange("p o c -> p (o c)"),
                                                mv[:, t, 0], rstd[:, t], ALU.subtract,
                                                ALU.mult).then_inc(s["norm_done"], 1)
                    for k in range(2):
                        half = slice(k * 512, (k + 1) * 512)
                        dve.wait_ge(s["xT_in_psum"], (R // 2) * (k + 1))
                        nc.vector.tensor_copy(xTb[:, half], ps_b[0:CB, half]).then_inc(s["xTb_done"], 1)
                    dve.wait_ge(s["logits_in_psum"], 1)
                    nc.vector.tensor_copy(logits[:, bass.ds(r * R, R), :],
                                          ps_l[:, 0:R * EXPERTS].rearrange("p (t e) -> p t e", t=R)
                                          ).then_inc(s["logits_done"], 1)
                    dve.wait_ge(s["logits_done"], 1)

                @block.gpsimd
                def _(pool):
                    pool.wait_ge(s["norm_done"], R)
                    nc.gpsimd.tensor_copy(xn_all[:, bass.ds(r * R, R), :], xn[:, :, :]).then_inc(s["kept"], 1)
                    pool.wait_ge(s["kept"], 1)

                @block.scalar
                def _(act):
                    for k in range(2):
                        half = slice(k * 512, (k + 1) * 512)
                        act.wait_ge(s["xT_in_psum"], (R // 2) * (k + 1))
                        nc.scalar.copy(xTa[:, half], ps_a[:, half]).then_inc(s["xTa_done"], 1)
                    if first_layer:
                        for k in range(2):
                            half = slice(k * 512, (k + 1) * 512)
                            act.wait_ge(s["gate_in_psum"], k + 1)
                            nc.scalar.activation(gT[0:GATE_HID, half], ps_g[0:GATE_HID, half], ACT.Gelu,
                                                 bias=w["gate_bias"][:, 0:1]).then_inc(s["gate_done"], 1)

                @block.tensor
                def _(pe):
                    for j in range(R):
                        pe.wait_ge(s["norm_done"], j + 1)
                        tok = slice(j * P, (j + 1) * P)
                        nc.tensor.transpose(ps_a[:, tok], xn[:, j, 0:CA], const["ident"][:, :])
                        nc.tensor.transpose(ps_b[0:CB, tok], xn[:, j, CA:DIM],
                                            const["ident"][:, :]).then_inc(s["xT_in_psum"], 1)
                    if first_layer:
                        for k in range(2):
                            half = slice(k * 512, (k + 1) * 512)
                            pe.wait_ge(s["xTa_done"], k + 1)
                            pe.wait_ge(s["xTb_done"], k + 1)
                            nc.tensor.matmul(ps_g[0:GATE_HID, half], w["gate_a"][:, :], xTa[:, half],
                                             start=True, stop=False)
                            nc.tensor.matmul(ps_g[0:GATE_HID, half], w["gate_b"][:, :], xTb[:, half],
                                             start=False, stop=True).then_inc(s["gate_in_psum"], 1)
                        pe.wait_ge(s["gate_done"], 2)
                    else:
                        pe.wait_ge(s["xTa_done"], 2)
                        pe.wait_ge(s["xTb_done"], 2)
                    for j in range(R):
                        tok = slice(j * P, (j + 1) * P)
                        lg = ps_l[:, j * EXPERTS:(j + 1) * EXPERTS]
                        if first_layer:
                            ins = nc.tensor.matmul(lg, gT[:, tok], w["gate2"][:, :], start=True, stop=True)
                        else:
                            nc.tensor.matmul(lg, xTa[:, tok], w["router_a"][:, :], start=True, stop=False)
                            ins = nc.tensor.matmul(lg, xTb[:, tok], w["router_b"][:, :], start=False, stop=True)
                    ins.then_inc(s["logits_in_psum"], 1)
            reset(nc, s.values())


def assign(nc, const, tag, first_layer, logits, weight, slot, owner):
    ALL = BATCH * TILES
    E = EXPERTS
    with ExitStack() as ctx:
        def sb(name, shape, dt=F32):
            return ctx.enter_context(nc.sbuf_tensor(f"{tag}_{name}", shape, dt))

        s = signals(nc, ctx, tag + "assign", "step shifted exp_done marked counts_in_psum done")
        e = sb("probs", [P, ALL, E])
        top, norm = sb("top", [P, ALL]), sb("norm", [P, ALL])
        best, where, wheref = sb("best", [P, ALL, 8]), sb("where", [P, ALL, 8], U32), sb("wheref", [P, ALL, 8])
        pick = sb("pick", [P, 2, ALL, E])
        both, tmp = sb("both", [P, ALL, E]), sb("tmp", [P, ALL, E])
        run = sb("run", [P, 2, ALL, E])
        full = sb("full", [P, E, ALL])
        tiles, first, last = sb("tiles", [P, E]), sb("first", [P, E]), sb("last", [P, E])
        square = sb("square", [P, E, E])
        slotf = sb("slotf", [P, 2, ALL])
        ended = sb("ended", [1, SLOT_TILES, E])
        ownerf = sb("ownerf", [1, SLOT_TILES])
        ps = ctx.enter_context(nc.psum_tensor(f"{tag}_counts", [P, 2, 512], F32))
        wide = [P, ALL, E]
        with nc.Block() as block:
            @block.vector
            def _(dve):
                n = 0

                def chain(ins):
                    nonlocal n
                    n += 1
                    ins.then_inc(s["step"], 1)
                    dve.wait_ge(s["step"], n)

                chain(nc.vector.tensor_reduce(top[:, :], logits[:, :, :], AX, ALU.max))
                nc.vector.tensor_tensor(e[:, :, :], logits[:, :, :], top[:, :].unsqueeze(2).broadcast_to(wide),
                                        ALU.subtract).then_inc(s["shifted"], 1)
                dve.wait_ge(s["exp_done"], 1)
                chain(nc.vector.tensor_reduce(norm[:, :], e[:, :, :], AX, ALU.add))
                chain(nc.vector.reciprocal(norm[:, :], norm[:, :]))
                chain(nc.vector.tensor_tensor(e[:, :, :], e[:, :, :], norm[:, :].unsqueeze(2).broadcast_to(wide),
                                              ALU.mult))
                for t in range(ALL):
                    ins = nc.vector.max(best[:, t, :], e[:, t, :])
                chain(ins)
                for t in range(ALL):
                    ins = nc.vector.max_index(where[:, t, :], best[:, t, :], e[:, t, :])
                chain(ins)
                chain(nc.vector.tensor_copy(wheref[:, :, :], where[:, :, :]))
                for k in range(2):
                    ins = nc.vector.tensor_tensor(pick[:, k], const["places"][:, 0:1, :].broadcast_to(wide),
                                                  wheref[:, :, k:k + 1].broadcast_to(wide), ALU.is_equal)
                chain(ins)
                nc.vector.tensor_tensor(both[:, :, :], pick[:, 0], pick[:, 1], ALU.add).then_inc(s["marked"], 1)
                chain(nc.vector.tensor_tensor(norm[:, :], best[:, :, 0], best[:, :, 1], ALU.add))
                if first_layer:
                    chain(nc.vector.tensor_scalar(norm[:, :], norm[:, :], 1e-8, None, ALU.add))
                chain(nc.vector.reciprocal(norm[:, :], norm[:, :]))
                for k in range(2):
                    ins = nc.vector.tensor_tensor(weight[:, k, :], best[:, :, k], norm[:, :], ALU.mult)
                chain(ins)
                dve.wait_ge(s["counts_in_psum"], 1)
                total = ps[:, 1, 0:ALL * E].rearrange("p (t e) -> p t e", t=ALL)
                before = ps[:, 0, 0:ALL * E].rearrange("p (t e) -> p t e", t=ALL)
                chain(nc.vector.tensor_copy(run[:, 0], total))
                cur, d = 0, 1
                while d < ALL:
                    chain(nc.vector.tensor_copy(run[:, 1 - cur, 0:d, :], run[:, cur, 0:d, :]))
                    chain(nc.vector.tensor_tensor(run[:, 1 - cur, d:ALL, :], run[:, cur, d:ALL, :],
                                                  run[:, cur, 0:ALL - d, :], ALU.add))
                    cur, d = 1 - cur, 2 * d
                count = run[:, cur, ALL - 1, :].unsqueeze(2).broadcast_to([P, E, ALL])
                chain(nc.vector.tensor_tensor(full[:, :, :], count,
                                              const["steps"][:, 0:ALL].unsqueeze(1).broadcast_to([P, E, ALL]),
                                              ALU.is_gt))
                chain(nc.vector.tensor_reduce(tiles[:, :], full[:, :, :], AX, ALU.add))
                chain(nc.vector.tensor_tensor(square[:, :, :], const["lower"][:, :, :],
                                              tiles[:, :].unsqueeze(1).broadcast_to([P, E, E]), ALU.mult))
                chain(nc.vector.tensor_reduce(first[:, :], square[:, :, :], AX, ALU.add))
                chain(nc.vector.tensor_tensor(last[:, :], first[:, :], tiles[:, :], ALU.add))
                chain(nc.vector.tensor_tensor(ended[:, :, :],
                                              const["counting"][0:1, :].unsqueeze(2).broadcast_to(
                                                  [1, SLOT_TILES, E]),
                                              last[0:1, :].unsqueeze(1).broadcast_to([1, SLOT_TILES, E]),
                                              ALU.is_ge))
                chain(nc.vector.tensor_reduce(ownerf[:, :], ended[:, :, :], AX, ALU.add))
                chain(nc.vector.tensor_scalar(owner[:, :], ownerf[:, :], float(E - 1), None, ALU.min))
                chain(nc.vector.tensor_tensor(run[:, cur], run[:, cur], total, ALU.subtract))
                chain(nc.vector.tensor_tensor(run[:, cur], before, run[:, cur], ALU.add))
                chain(nc.vector.tensor_scalar(first[:, :], first[:, :], float(P), None, ALU.mult))
                chain(nc.vector.tensor_tensor(run[:, cur], run[:, cur],
                                              first[:, :].unsqueeze(1).broadcast_to(wide), ALU.add))
                for k in range(2):
                    chain(nc.vector.tensor_tensor(tmp[:, :, :], pick[:, k], run[:, cur], ALU.mult))
                    chain(nc.vector.tensor_reduce(slotf[:, k, :], tmp[:, :, :], AX, ALU.add))
                chain(nc.vector.tensor_copy(slot[:, :, :], slotf[:, :, :]))

            @block.scalar
            def _(act):
                act.wait_ge(s["shifted"], 1)
                nc.scalar.activation(e[:, :, :], e[:, :, :], ACT.Exp).then_inc(s["exp_done"], 1)

            @block.tensor
            def _(pe):
                pe.wait_ge(s["marked"], 1)
                marks = both[:, :, :].rearrange("p t e -> p (t e)")
                nc.tensor.matmul(ps[:, 0, 0:ALL * E], const["before"][:, :], marks, start=True, stop=True)
                nc.tensor.matmul(ps[:, 1, 0:ALL * E], const["ones"][:, :], marks, start=True,
                                 stop=True).then_inc(s["counts_in_psum"], 1)
        reset(nc, s.values())


def experts(nc, hid, const, w, tag, width, first_layer, scratch, out=None):
    ALL = BATCH * TILES
    NF = width // P
    HALF = width // 2 if width > 512 else width
    NH = width // HALF
    U = SLOT_TILES // ROUNDS
    rows_in, rows_out, zeroed, pool_sems = scratch
    with ExitStack() as ctx:
        def sb(name, shape, dt=F32):
            return ctx.enter_context(nc.sbuf_tensor(f"{tag}_{name}", shape, dt))

        xn_all = sb("xn_all", [P, ALL, DIM])
        logits = sb("logits", [P, ALL, EXPERTS])
        weight = sb("weight", [P, 2, ALL])
        slot = sb("slot", [P, 2, ALL], U32)
        owner = sb("owner", [1, SLOT_TILES], mybir.dt.int32)
        route(nc, hid, xn_all, const, w, tag, first_layer, logits)
        assign(nc, const, tag, first_layer, logits, weight, slot, owner)

        sent = pool_sems[-1]
        with nc.Block() as block:
            @block.gpsimd
            def _(pool):
                if first_layer:
                    pool.wait_ge(zeroed, 16 * ROUNDS)
                for t in range(ALL):
                    for k in range(2):
                        nc.gpsimd.indirect_dma_start(
                            rows_in, bass.IndirectOffsetOnAxis(ap=slot[:, k, t:t + 1], axis=0),
                            xn_all[:, t, :], None).then_inc(sent, 16)
                pool.wait_ge(sent, 16 * 2 * ALL * (1 if first_layer else 2))

        with ExitStack() as loop:
            def lsb(name, shape, dt=F32):
                return loop.enter_context(nc.sbuf_tensor(f"{tag}_{name}", shape, dt))

            def lps(name, shape):
                return loop.enter_context(nc.psum_tensor(f"{tag}_{name}", shape, F32))

            s = signals(nc, loop, tag + "mlp", """x_first xT_in_psum xT_done hidden_in_psum gelu_done
                hiddenT_in_psum hiddenT_done y_in_psum y_done stored done""")
            x_in = [loop.enter_context(nc.semaphore(f"{tag}mlp.x_in{j}")) for j in range(U)]
            x = lsb("x", [P, U, DIM])
            xTa, xTb = lsb("mxTa", [P, 2, P]), lsb("mxTb", [CB + 1, 2, P])
            hidden = lsb("hidden", [P, 2, width])
            hiddenT = lsb("hiddenT", [P, 2, NF, P])
            y = lsb("y", [P, 2, DIM])
            xT_ps = lps("mxT_ps", [P, 512])
            h_ps = lps("h_ps", [P, 2 * NH, 512])
            hT_ps = lps("hT_ps", [P, NH, 512])
            y_ps = lps("y_ps", [P, 512])
            CH = NF // NH
            nc.vector.memset(xTb[CB:CB + 1, :, :], 1.0)
            nc.all_engine_barrier()
            x_tiles = rows_in.rearrange("(i p) c -> p i c", p=P)
            y_tiles = rows_out.rearrange("(i p) c -> p i c", p=P)
            with nc.Fori(0, ROUNDS) as r:
                with nc.Block() as block:
                    @block.sync
                    def _(sp):
                        for j in range(U):
                            sp.dma_start(x[:, j:j + 1, :], x_tiles[:, bass.ds(r * U + j, 1), :]
                                         ).then_inc(x_in[j], 16)
                        for j in range(U):
                            sp.wait_ge(s["y_done"], j + 1)
                            sp.dma_start(y_tiles[:, bass.ds(r * U + j, 1), :], y[:, j % 2:j % 2 + 1, :]
                                         ).then_inc(s["stored"], 16)
                            sp.wait_ge(s["stored"], 16 * (j + 1))

                    @block.vector
                    def _(dve):
                        def copy_x(j):
                            dve.wait_ge(s["xT_in_psum"], j + 1)
                            if j >= 2:
                                dve.wait_ge(s["hidden_in_psum"], NH * (j - 1))
                            nc.vector.tensor_copy(xTa[:, j % 2, :], xT_ps[:, 0:P]).then_inc(s["xT_done"], 1)
                            nc.vector.tensor_copy(xTb[0:CB, j % 2, :], xT_ps[0:CB, P:2 * P]
                                                  ).then_inc(s["xT_done"], 1)

                        def copy_hidden(j):
                            for k in range(NH):
                                dve.wait_ge(s["hiddenT_in_psum"], NH * j + k + 1)
                                if k == 0 and j >= 2:
                                    dve.wait_ge(s["y_in_psum"], j - 1)
                                nc.vector.tensor_copy(
                                    hiddenT[:, j % 2, k * CH:(k + 1) * CH, :],
                                    hT_ps[:, k, 0:CH * P].rearrange("p (c q) -> p c q", c=CH)
                                ).then_inc(s["hiddenT_done"], 1)

                        def copy_y(j):
                            dve.wait_ge(s["y_in_psum"], j + 1)
                            if j >= 2:
                                dve.wait_ge(s["stored"], 16 * (j - 1))
                            nc.vector.tensor_copy(y[:, j % 2, :], y_ps[:, 0:DIM]).then_inc(s["y_done"], 1)

                        copy_x(0)
                        for j in range(U + 2):
                            if j + 1 < U:
                                copy_x(j + 1)
                            if 1 <= j < U + 1:
                                copy_hidden(j - 1)
                            if j >= 2:
                                copy_y(j - 2)

                    @block.scalar
                    def _(act):
                        for j in range(U):
                            for k in range(NH):
                                n = NH * j + k
                                act.wait_ge(s["hidden_in_psum"], n + 1)
                                if j >= 2:
                                    act.wait_ge(s["hiddenT_in_psum"], NH * (j - 1))
                                nc.scalar.activation(hidden[:, j % 2, k * HALF:(k + 1) * HALF],
                                                     h_ps[:, n % (2 * NH), 0:HALF], ACT.Gelu
                                                     ).then_inc(s["gelu_done"], 1)

                    @block.tensor
                    def _(pe):
                        own = [None] * U

                        def turn_x(j):
                            pe.wait_ge(x_in[j], 16)
                            if j >= 1:
                                pe.wait_ge(s["xT_done"], 2 * j)
                            nc.tensor.transpose(xT_ps[:, 0:P], x[:, j, 0:CA], const["ident"][:, :])
                            nc.tensor.transpose(xT_ps[0:CB, P:2 * P], x[:, j, CA:DIM],
                                                const["ident"][:, :]).then_inc(s["xT_in_psum"], 1)

                        def down(j):
                            own[j] = pe.value_load(owner[0:1, bass.ds(r * U + j, 1)], min_val=0,
                                                   max_val=EXPERTS - 1)
                            pe.wait_ge(s["xT_done"], 2 * (j + 1))
                            for k in range(NH):
                                n = NH * j + k
                                if j >= 2:
                                    pe.wait_ge(s["gelu_done"], n - 2 * NH + 1)
                                cols = slice(k * HALF, (k + 1) * HALF)
                                wa = w["down_a"][:, bass.ds(own[j], 1), cols].rearrange("p o c -> p (o c)")
                                wb = w["down_b"][:, bass.ds(own[j], 1), cols].rearrange("p o c -> p (o c)")
                                o = h_ps[:, n % (2 * NH), 0:HALF]
                                nc.tensor.matmul(o, xTa[:, j % 2, :], wa, start=True, stop=False)
                                nc.tensor.matmul(o, xTb[:, j % 2, :], wb, start=False,
                                                 stop=True).then_inc(s["hidden_in_psum"], 1)

                        def turn_hidden(j):
                            for k in range(NH):
                                pe.wait_ge(s["gelu_done"], NH * j + k + 1)
                                if j >= 1:
                                    pe.wait_ge(s["hiddenT_done"], NH * (j - 1) + k + 1)
                                for c in range(CH):
                                    f = (k * CH + c) * P
                                    ins = nc.tensor.transpose(hT_ps[:, k, c * P:(c + 1) * P],
                                                              hidden[:, j % 2, f:f + P], const["ident"][:, :])
                                ins.then_inc(s["hiddenT_in_psum"], 1)

                        def up(j):
                            pe.wait_ge(s["hiddenT_done"], NH * (j + 1))
                            if j >= 1:
                                pe.wait_ge(s["y_done"], j)
                            if not first_layer:
                                b2 = w["bias2"][0:1, bass.ds(own[j], 1), :].rearrange("p o c -> p (o c)")
                                nc.tensor.matmul(y_ps[:, 0:DIM], const["ones_row"][0:1, :], b2,
                                                 start=True, stop=False)
                            for c in range(NF):
                                wu = w["up"][:, bass.ds(own[j], 1), c, :].rearrange("p o c -> p (o c)")
                                ins = nc.tensor.matmul(y_ps[:, 0:DIM], hiddenT[:, j % 2, c, :], wu,
                                                       start=(first_layer and c == 0), stop=(c == NF - 1))
                            ins.then_inc(s["y_in_psum"], 1)

                        turn_x(0)
                        for j in range(U + 2):
                            if j < U:
                                down(j)
                            if j + 1 < U:
                                turn_x(j + 1)
                            if 1 <= j < U + 1:
                                turn_hidden(j - 1)
                            if j >= 2:
                                up(j - 2)
                reset(nc, [*s.values(), *x_in])

        combine(nc, hid, xn_all, const, w, tag, first_layer, weight, slot, rows_out, pool_sems, out)


def combine(nc, hid, xn_all, const, w, tag, first_layer, weight, slot, rows_out, pool_sems, out):
    ALL = BATCH * TILES
    RING = 8
    with ExitStack() as ctx:
        def sb(name, shape, dt=F32):
            return ctx.enter_context(nc.sbuf_tensor(f"{tag}_{name}", shape, dt))

        s = signals(nc, ctx, tag + "combine", "added stats_done moments_done rstd_done norm_done hid_done stored")
        got = pool_sems[0:RING]
        y = sb("gathered", [P, RING, 2, DIM])
        stats, mv, rstd = sb("cstats", [P, ALL, 6]), sb("cmv", [P, ALL, 2]), sb("crstd", [P, ALL])
        acc = xn_all if first_layer else hid
        with nc.Block() as block:
            @block.gpsimd
            def _(pool):
                for t in range(ALL):
                    if t >= RING:
                        pool.wait_ge(s["added"], 2 * (t - RING + 1))
                    for k in range(2):
                        nc.gpsimd.indirect_dma_start(
                            y[:, t % RING, k, :], None, rows_out,
                            bass.IndirectOffsetOnAxis(ap=slot[:, k, t:t + 1], axis=0)
                        ).then_inc(got[t % RING], 16)
                if first_layer:
                    pool.wait_ge(s["moments_done"], ALL)
                    nc.gpsimd.tensor_scalar(rstd[:, :], mv[:, :, 1], LN_EPS, None,
                                            ALU.add).then_inc(s["rstd_done"], 1)
                    pool.wait_ge(s["rstd_done"], 1)
                    nc.gpsimd.tensor_tensor(rstd[:, :], rstd[:, :],
                                            const["neg_half"][:, 0:1].broadcast_to([P, ALL]),
                                            ALU.pow).then_inc(s["rstd_done"], 1)

            @block.vector
            def _(dve):
                def moments(t):
                    dve.wait_ge(s["stats_done"], t + 1)
                    nc.vector.bn_aggr(mv[:, t, :], stats[:, t, :]).then_inc(s["moments_done"], 1)

                had = 16 * TILES + (0 if first_layer else 32 * (ALL // RING))
                for t in range(ALL):
                    dve.wait_ge(got[t % RING], had + 32 * (t // RING + 1))
                    for k in range(2):
                        if k:
                            dve.wait_ge(s["added"], 2 * t + 1)
                        nc.vector.scalar_tensor_tensor(acc[:, t, :], y[:, t % RING, k, :],
                                                       weight[:, k, t:t + 1], acc[:, t, :],
                                                       ALU.mult, ALU.add).then_inc(s["added"], 1)
                    if first_layer:
                        dve.wait_ge(s["added"], 2 * (t + 1))
                        nc.vector.bn_stats(stats[:, t, :], acc[:, t, :]).then_inc(s["stats_done"], 1)
                        if t >= 1:
                            moments(t - 1)
                if first_layer:
                    moments(ALL - 1)
                    dve.wait_ge(s["moments_done"], ALL)
                    dve.wait_ge(s["rstd_done"], 2)
                    for g in range(BATCH):
                        tiles = slice(g * TILES, (g + 1) * TILES)
                        for t in range(g * TILES, (g + 1) * TILES):
                            nc.vector.tensor_scalar(acc[:, t, :], acc[:, t, :], mv[:, t, 0:1],
                                                    rstd[:, t:t + 1], ALU.subtract,
                                                    ALU.mult).then_inc(s["norm_done"], 1)
                        dve.wait_ge(s["norm_done"], (TILES + 2) * g + TILES)
                        a = acc[:, tiles, :]
                        for k, (par, op) in enumerate(((w["gamma"], ALU.mult), (w["beta"], ALU.add))):
                            nc.vector.tensor_tensor(a, a, par[:, :].unsqueeze(1).broadcast_to([P, TILES, DIM]),
                                                    op).then_inc(s["norm_done"], 1)
                            dve.wait_ge(s["norm_done"], (TILES + 2) * g + TILES + k + 1)
                        nc.vector.tensor_tensor(hid[:, tiles, :], a, hid[:, tiles, :],
                                                ALU.add).then_inc(s["hid_done"], 1)

            @block.sync
            def _(sp):
                if out is not None:
                    for g in range(BATCH):
                        sp.wait_ge(s["added"], 2 * TILES * (g + 1))
                        sp.dma_start(out.rearrange("(t p) c -> p t c", p=P)[:, g * TILES:(g + 1) * TILES, :],
                                     hid[:, g * TILES:(g + 1) * TILES, :]).then_inc(s["stored"], 16)
                    sp.wait_ge(s["stored"], 16 * BATCH)
        reset(nc, s.values())


def build(nc, io, out):
    with ExitStack() as ctx:
        def sb(name, shape, dt=F32):
            return ctx.enter_context(nc.sbuf_tensor(name, shape, dt))

        hid = sb("hid", [P, BATCH * TILES, DIM])
        idx = sb("tok_ids", [P, BATCH * TILES], U32)
        const = {}
        const["ident"] = sb("ident", [P, P])
        const["ident_r"], const["causal_r"] = sb("ident_r", [P, P], F32R), sb("causal_r", [P, P], F32R)
        const["causal"] = sb("causal", [P, P])
        const["cos"], const["sin"] = sb("rope_cos", [P, TILES, 2, D0]), sb("rope_sin", [P, TILES, 2, D0])
        const["places"] = sb("places", [P, 1, EXPERTS])
        const["steps"] = sb("steps", [P, BATCH * TILES])
        const["counting"] = sb("counting", [1, SLOT_TILES])
        const["lower"] = sb("lower", [P, EXPERTS, EXPERTS])
        const["bias_rows"] = sb("bias_rows", [P, 1])
        const["before"], const["ones"] = sb("before", [P, P]), sb("ones", [P, P])
        zeros = sb("zeros", [P, SLOT_TILES // ROUNDS, DIM])
        rows_in = nc.dram_tensor("dispatch_in", (SLOT_TILES * P, DIM), F32, kind="Internal").ap()
        rows_out = nc.dram_tensor("dispatch_out", (SLOT_TILES * P, DIM), F32, kind="Internal").ap()
        zeroed = ctx.enter_context(nc.semaphore("zeroed"))
        cleared = ctx.enter_context(nc.semaphore("cleared"))
        const["neg_half"] = sb("neg_half", [P, TILES])
        const["ones_row"] = sb("ones_row", [1, P])
        inputs_in = ctx.enter_context(nc.semaphore("inputs_in"))
        consts_done = ctx.enter_context(nc.semaphore("consts_done"))

        pool_sems = [ctx.enter_context(nc.semaphore(f"pool_dma{i}")) for i in range(BATCH + 1)]
        scratch = (rows_in, rows_out, zeroed, pool_sems)
        w_first = ExitStack()
        w0, f0 = {}, {}
        loads = []

        def weight(scope, group, name, shape, src):
            t = scope.enter_context(nc.sbuf_tensor(name, shape, F32))
            group[name.split(".")[1]] = t
            loads.append((t, src))

        with w_first:
            def w(group, name, shape, src):
                weight(w_first, group, name, shape, src)

            w(w0, "attn0.qkv_a", [P, 3 * DIM], io["L0_qkv"][0:CA, :])
            w(w0, "attn0.qkv_b", [CB + 1, 3 * DIM], io["L0_qkv"][CA:DIM + 1, :])
            w(w0, "attn0.proj_a", [P, DIM], io["L0_proj"][0:CA, :])
            w(w0, "attn0.proj_b", [CB + 1, DIM], io["L0_proj"][CA:DIM + 1, :])
            w(f0, "ffn0.gate_a", [P, GATE_HID], io["L0_ffn_w1"][0:CA, :])
            w(f0, "ffn0.gate_b", [CB, GATE_HID], io["L0_ffn_w1"][CA:DIM, :])
            w(f0, "ffn0.gate_bias", [GATE_HID, 1], io["L0_ffn_b1"])
            w(f0, "ffn0.gate2", [GATE_HID + 1, EXPERTS], io["L0_gate2"])
            w(f0, "ffn0.down_a", [P, EXPERTS, F0], io["L0_down"][0:CA])
            w(f0, "ffn0.down_b", [CB + 1, EXPERTS, F0], io["L0_down"][CA:DIM + 1])
            w(f0, "ffn0.up", [P, EXPERTS, F0 // P, DIM], io["L0_up"])
            w(f0, "ffn0.gamma", [P, DIM], io["L0_ffn_gamma"].broadcast_to([P, DIM]))
            w(f0, "ffn0.beta", [P, DIM], io["L0_ffn_beta"].broadcast_to([P, DIM]))
            for t, src in ((const["ident"], io["ident"]), (const["causal"], io["causal"]), (const["cos"], io["cos"]),
                           (const["sin"], io["sin"]), (const["places"], io["places"]),
                           (const["steps"], io["steps"]), (const["counting"], io["counting"]),
                           (const["lower"], io["lower"]), (const["before"], io["before"]),
                           (const["bias_rows"], io["bias_rows"])):
                loads.append((t, src))

            def weights_in(sp):
                for t, src in loads:
                    sp.dma_start(t[:], src).then_inc(inputs_in, 16)
                sp.wait_ge(cleared, 1)
                for r in range(ROUNDS):
                    u = SLOT_TILES // ROUNDS
                    sp.dma_start(rows_in.rearrange("(i p) c -> p i c", p=P)[:, r * u:(r + 1) * u, :],
                                 zeros[:, :, :]).then_inc(zeroed, 16)

            nc.vector.memset(zeros[:, :, :], 0.0).then_inc(cleared, 1)
            nc.vector.memset(const["ones"][:, :], 1.0)
            embed(nc, io, hid, idx, const, weights_in, pool_sems)
            with nc.Block() as block:
                @block.vector
                def _(dve):
                    dve.wait_ge(inputs_in, 16 * len(loads))
                    nc.vector.tensor_copy(const["ident_r"][:, :], const["ident"][:, :])
                    nc.vector.tensor_copy(const["causal_r"][:, :], const["causal"][:, :])
                    nc.vector.memset(const["neg_half"][:, :], -0.5)
                    nc.vector.memset(const["ones_row"][:, :], 1.0).then_inc(consts_done, 1)
                    dve.wait_ge(consts_done, 1)
            first_attention(nc, hid, const, w0)
            experts(nc, hid, const, f0, "ffn0", F0, True, scratch)

        def load_weights(name, scope, group, which):
            done = ctx.enter_context(nc.semaphore(name))
            loads.clear()
            for n, shape, src in which:
                weight(scope, group, n, shape, src)
            with nc.Block() as block:
                @block.sync
                def _(sp):
                    for t, src in loads:
                        sp.dma_start(t[:], src).then_inc(done, 16)
                    sp.wait_ge(done, 16 * len(loads))

        with ExitStack() as scope:
            w1 = {}
            load_weights("w1_in", scope, w1, [
                ("attn1.out", [P, H1 * D1 // P, DIM], io["L1_out"]),
                ("attn1.out_bias", [1, DIM], io["L1_attn_b_out"])])
            w1["head_scale"] = scope.enter_context(nc.sbuf_tensor("head_scale", [P, H1], F32))
            with ExitStack() as sub:
                reattn = sub.enter_context(nc.sbuf_tensor("reattn", [H1, D1 * D1], F32))
                reattn_in = sub.enter_context(nc.semaphore("reattn_in"))
                hs = sub.enter_context(nc.sbuf_tensor("reattn_sum", [H1, 1], F32))
                diag = sub.enter_context(nc.sbuf_tensor("reattn_diag", [H1, H1], F32))
                ones = sub.enter_context(nc.sbuf_tensor("ones_heads", [H1, P], F32))
                ps = sub.enter_context(nc.psum_tensor("head_scale_ps", [P, 512], F32))
                summed = sub.enter_context(nc.semaphore("reattn_summed"))
                spread = sub.enter_context(nc.semaphore("reattn_spread"))
                with nc.Block() as block:
                    @block.sync
                    def _(sp):
                        sp.dma_start(reattn[:, :], io["L1_attn_reattn_weights"]).then_inc(reattn_in, 16)

                    @block.vector
                    def _(dve):
                        nc.vector.memset(ones[:, :], 1.0).then_inc(summed, 1)
                        dve.wait_ge(reattn_in, 16)
                        nc.vector.tensor_reduce(hs[:, :], reattn[:, :], AX, ALU.add).then_inc(summed, 1)
                        dve.wait_ge(summed, 2)
                        nc.vector.tensor_scalar(diag[:, :], const["ident"][0:H1, 0:H1], hs[:, 0:1], None,
                                                ALU.mult).then_inc(summed, 1)
                        dve.wait_ge(spread, 1)
                        nc.vector.tensor_copy(w1["head_scale"][:, :], ps[:, 0:H1]).then_inc(summed, 1)
                        dve.wait_ge(summed, 4)

                    @block.tensor
                    def _(pe):
                        pe.wait_ge(summed, 3)
                        nc.tensor.matmul(ps[:, 0:H1], ones[:, :], diag[:, :], start=True,
                                         stop=True).then_inc(spread, 1)
            split_weights(nc, io, w1, scope)
            second_attention(nc, hid, const, w1)
        with ExitStack() as scope:
            f1 = {}
            load_weights("f1_in", scope, f1, [
                ("ffn1.router_a", [P, EXPERTS], io["L1_router"][0:CA, :]),
                ("ffn1.router_b", [CB, EXPERTS], io["L1_router"][CA:DIM, :]),
                ("ffn1.down_a", [P, EXPERTS, F1], io["L1_down"][0:CA]),
                ("ffn1.down_b", [CB + 1, EXPERTS, F1], io["L1_down"][CA:DIM + 1]),
                ("ffn1.up", [P, EXPERTS, F1 // P, DIM], io["L1_up"]),
                ("ffn1.bias2", [1, EXPERTS, DIM], io["L1_ffn_b2"])])
            experts(nc, hid, const, f1, "ffn1", F1, False, scratch, out)


def layout(x, L0_tok_weights, L0_tok_emb_weight, L0_attn_Wq, L0_attn_bq, L0_attn_Wk, L0_attn_bk, L0_attn_Wv,
           L0_attn_bv, L0_attn_Wp, L0_attn_bp, L0_ffn_w1, L0_ffn_b1, L0_ffn_w2, L0_ffn_b2, L0_ffn_down_w,
           L0_ffn_down_b, L0_ffn_up_w, L0_ffn_gamma, L0_ffn_beta, L1_attn_w_qkv, L1_attn_b_qkv,
           L1_attn_reattn_weights, L1_attn_w_out, L1_attn_b_out, L1_ffn_router_w, L1_ffn_w1, L1_ffn_b1,
           L1_ffn_w2, L1_ffn_b2):
    a = {}
    a["tok"] = x.reshape(BATCH * TILES, P).T.astype(np.uint32)
    a["L0_tok_weights"] = L0_tok_weights[:, None]
    a["L0_tok_emb_weight"] = L0_tok_emb_weight
    a["L0_qkv"] = np.concatenate([np.concatenate([wt.T, bi[None]]) for wt, bi in (
        (L0_attn_Wq, L0_attn_bq), (L0_attn_Wk, L0_attn_bk), (L0_attn_Wv, L0_attn_bv))], axis=1)
    a["L0_proj"] = np.concatenate([L0_attn_Wp.T, L0_attn_bp[None]])
    a["L0_ffn_w1"], a["L0_ffn_b1"] = L0_ffn_w1, L0_ffn_b1[:, None]
    a["L0_gate2"] = np.concatenate([L0_ffn_w2, L0_ffn_b2[None]])
    a["L0_down"] = np.concatenate([L0_ffn_down_w.transpose(1, 0, 2), L0_ffn_down_b[None]])
    a["L0_up"] = L0_ffn_up_w.reshape(EXPERTS, F0 // P, P, DIM).transpose(2, 0, 1, 3)
    a["L0_ffn_gamma"], a["L0_ffn_beta"] = L0_ffn_gamma[None], L0_ffn_beta[None]
    a["L1_qkv"] = np.concatenate([L1_attn_w_qkv, L1_attn_b_qkv[None]])
    a["L1_out"] = L1_attn_w_out.reshape(H1 * D1 // P, P, DIM).transpose(1, 0, 2)
    a["L1_attn_b_out"] = L1_attn_b_out[None]
    a["L1_attn_reattn_weights"] = L1_attn_reattn_weights.reshape(H1, D1 * D1)
    a["L1_router"] = L1_ffn_router_w.T
    a["L1_down"] = np.concatenate([L1_ffn_w1.transpose(1, 0, 2), L1_ffn_b1[None]])
    a["L1_up"] = L1_ffn_w2.reshape(EXPERTS, F1 // P, P, DIM).transpose(2, 0, 1, 3)
    a["L1_ffn_b2"] = L1_ffn_b2[None]
    a["mix_mask"] = (np.arange(DIM)[None] < np.array(EMBED_DIMS)[:, None]).astype(np.float32)
    a["ident"] = np.eye(P, dtype=np.float32)
    a["causal"] = np.where(np.arange(P)[None] > np.arange(P)[:, None], MASKED, 0).astype(np.float32)
    a["places"] = np.broadcast_to(np.arange(EXPERTS, dtype=np.float32), (P, 1, EXPERTS))
    a["steps"] = np.broadcast_to(np.arange(BATCH * TILES, dtype=np.float32) * P, (P, BATCH * TILES))
    a["counting"] = np.arange(SLOT_TILES, dtype=np.float32)[None]
    a["lower"] = np.broadcast_to(np.tri(EXPERTS, k=-1, dtype=np.float32), (P, EXPERTS, EXPERTS))
    a["bias_rows"] = np.isin(np.arange(P), (CB, 96)).astype(np.float32)[:, None]
    a["before"] = np.triu(np.ones((P, P), np.float32), 1)
    f = np.float32
    inv = (f(1) / f(10000) ** (f(2) * np.arange(D0 // 2, dtype=f) / f(D0))).astype(f)
    ang = np.arange(SEQ, dtype=f)[:, None] * inv[None]
    cos = np.repeat(np.cos(ang), 2, axis=1)
    sin = np.stack([-np.sin(ang), np.sin(ang)], axis=-1).reshape(SEQ, D0)
    for name, table in (("cos", cos), ("sin", sin)):
        both = np.stack([table * f(D0 ** -0.5), table], axis=1)
        a[name] = both.reshape(TILES, P, 2, D0).transpose(1, 0, 2, 3)
    return {k: np.ascontiguousarray(v) for k, v in a.items()}


def declare(nc, arrays):
    io = {}
    for name, v in arrays.items():
        io[name] = nc.dram_tensor(f"in_{name}", v.shape, mybir.dt.from_np(v.dtype), kind="ExternalInput").ap()
    out = nc.dram_tensor("out", (BATCH * SEQ, DIM), F32, kind="ExternalOutput").ap()
    return io, out


def kernel(**inputs):
    import concourse.bacc as bacc
    from concourse.bass_utils import run_bass_kernel_spmd

    arrays = layout(**{k: np.asarray(v) for k, v in inputs.items()})
    nc = bacc.Bacc("TRN2", target_bir_lowering=False, num_devices=1)
    io, out = declare(nc, arrays)
    build(nc, io, out)
    r = run_bass_kernel_spmd(nc, [{f"in_{k}": v for k, v in arrays.items()}], core_ids=[0])
    return r.results[0]["out"].reshape(BATCH, SEQ, DIM)
```

```python
from contextlib import ExitStack

import numpy as np

import concourse.bass as bass
from concourse import mybir

F32 = mybir.dt.float32
F32R = mybir.dt.float32r
U32 = mybir.dt.uint32
ALU = mybir.AluOpType
ACT = mybir.ActivationFunctionType
AX = mybir.AxisListType.X

P = 128
BATCH, SEQ = 8, 512
TILES = SEQ // P
DIM = 192
CA, CB = 128, DIM - 128
VOCAB = 50257
EMBED_DIMS = (192, 96, 144, 192)
EXPERTS = 8
LN_EPS = 1e-5
H0, D0 = 12, 16
H1, D1 = 12, 64
GATE_HID = 96
F0, F1 = 256, 768
MASKED = -1e30
SLOT_TILES = 2 * BATCH * TILES + EXPERTS
ROUNDS = 3


def signals(nc, ctx, prefix, names):
    return {n: ctx.enter_context(nc.semaphore(f"{prefix}.{n}")) for n in names.split()}


def reset(nc, handles):
    nums = sorted(h.num for h in handles)
    start = nums[0]
    for n, after in zip(nums, nums[1:] + [None]):
        if after != n + 1:
            nc.sync.sem_clear(range(start, n + 1))
            start = after
    nc.all_engine_barrier(sem_only=True)


def layer_norm_vector(nc, dve, s, rows, stats, mv, rstd, xn):
    for t in range(len(rows)):
        nc.vector.bn_stats(stats[:, t, :], rows[t]).then_inc(s["stats_done"], 1)
    for t in range(len(rows)):
        dve.wait_ge(s["stats_done"], t + 1)
        nc.vector.bn_aggr(mv[:, t, :], stats[:, t, :]).then_inc(s["moments_done"], 1)
    dve.wait_ge(s["rstd_done"], 2)
    dve.wait_ge(s["moments_done"], len(rows))
    for t in range(len(rows)):
        for to, channels in ((0, slice(0, DIM)), (DIM, slice(CA, DIM))):
            n = channels.stop - channels.start
            nc.vector.tensor_scalar(xn[:, t, to:to + n], rows[t][:, channels], mv[:, t, 0:1], rstd[:, t:t + 1],
                                    ALU.subtract, ALU.mult).then_inc(s["norm_done"], 1)


def rstd_gpsimd(nc, pool, s, mv, rstd, neg_half, moments, tiles):
    pool.wait_ge(moments, tiles)
    nc.gpsimd.tensor_scalar(rstd[:, :], mv[:, :, 1], LN_EPS, None, ALU.add).then_inc(s, 1)
    pool.wait_ge(s, 1)
    nc.gpsimd.tensor_tensor(rstd[:, :], rstd[:, :], neg_half[:, 0:tiles], ALU.pow).then_inc(s, 1)


def split_weights(nc, ctx, w, tag, scope, temp, src, cols):
    for name in ("a_hi", "a_lo", "b_hi", "b_lo"):
        w[name] = scope.enter_context(nc.sbuf_tensor(f"{tag}.{name}", [P, cols], F32R))
    wa = temp.enter_context(nc.sbuf_tensor(f"{tag}.a", [P, cols], F32))
    wb = temp.enter_context(nc.sbuf_tensor(f"{tag}.b", [P, cols], F32))
    bias = temp.enter_context(nc.sbuf_tensor(f"{tag}.bias", [1, cols], F32))
    bias_hi = temp.enter_context(nc.sbuf_tensor(f"{tag}.bias_hi", [1, cols], F32R))
    loaded = ctx.enter_context(nc.semaphore(f"{tag}.qkv_in"))
    rounded = ctx.enter_context(nc.semaphore(f"{tag}.qkv_hi"))
    split = ctx.enter_context(nc.semaphore(f"{tag}.qkv_lo"))

    def load(sp):
        sp.dma_start(wa[:, :], src[0:CA, :]).then_inc(loaded, 16)
        for k in range(2):
            sp.dma_start(wb[k * CB:(k + 1) * CB, :], src[CA:DIM, :]).then_inc(loaded, 16)
        sp.dma_start(bias[:, :], src[DIM:DIM + 1, :]).then_inc(loaded, 16)

    def high_parts(act):
        act.wait_ge(loaded, 64)
        nc.scalar.copy(bias_hi[:, :], bias[:, :]).then_inc(rounded, 1)
        nc.scalar.copy(w["a_hi"][:, :], wa[:, :]).then_inc(rounded, 1)
        nc.scalar.copy(w["b_hi"][:, :], wb[:, :]).then_inc(rounded, 1)

    def low_parts(dve):
        nc.vector.memset(w["b_lo"][CB:P, :].bitcast(F32), 0.0).then_inc(split, 1)
        dve.wait_ge(split, 1)
        dve.wait_ge(rounded, 3)
        nc.vector.tensor_copy(w["b_lo"][CB:CB + 1, :], bias_hi[:, :].bitcast(F32)).then_inc(split, 1)
        nc.vector.tensor_tensor(w["b_lo"][96:97, :], bias[:, :], bias_hi[:, :].bitcast(F32),
                                ALU.subtract).then_inc(split, 1)
        nc.vector.tensor_tensor(w["a_lo"][:, :], wa[:, :], w["a_hi"][:, :].bitcast(F32),
                                ALU.subtract).then_inc(split, 1)
        nc.vector.tensor_tensor(w["b_lo"][0:CB, :], wb[0:CB, :], w["b_hi"][0:CB, :].bitcast(F32),
                                ALU.subtract).then_inc(split, 1)
        dve.wait_ge(split, 5)

    return load, high_parts, low_parts


def embed(nc, io, hid, idx, weights_in, split, pool_sems):
    with ExitStack() as ctx:
        s = signals(nc, ctx, "embed", "idx_in mix_in scaled_w col_in_psum col_done hid_done")
        rows_in = pool_sems[0:BATCH]
        w4 = ctx.enter_context(nc.sbuf_tensor("mix_w", [4, 1], F32))
        w4b = ctx.enter_context(nc.sbuf_tensor("mix_w_wide", [4, P], F32))
        mask4 = ctx.enter_context(nc.sbuf_tensor("mix_mask", [4, DIM], F32))
        col = ctx.enter_context(nc.sbuf_tensor("col_scale", [P, DIM], F32))
        col_ps = ctx.enter_context(nc.psum_tensor("col_scale_ps", [P, 512], F32))
        with nc.Block() as block:
            @block.sync
            def _(sp):
                sp.dma_start(idx[:, :], io["tok"]).then_inc(s["idx_in"], 16)
                sp.dma_start(w4[:, :], io["L0_tok_weights"]).then_inc(s["mix_in"], 16)
                sp.dma_start(mask4[:, :], io["mix_mask"]).then_inc(s["mix_in"], 16)
                split[0](sp)
                weights_in(sp)

            @block.scalar
            def _(act):
                split[1](act)

            @block.gpsimd
            def _(pool):
                pool.wait_ge(s["idx_in"], 16)
                for t in range(BATCH * TILES):
                    nc.gpsimd.indirect_dma_start(
                        hid[:, t, :], None, io["L0_tok_emb_weight"],
                        bass.IndirectOffsetOnAxis(ap=idx[:, t:t + 1], axis=0),
                    ).then_inc(rows_in[t // TILES], 16)

            @block.tensor
            def _(pe):
                pe.wait_ge(s["scaled_w"], 2)
                nc.tensor.matmul(col_ps[:, 0:DIM], w4b[:, :], mask4[:, :],
                                 start=True, stop=True).then_inc(s["col_in_psum"], 1)

            @block.vector
            def _(dve):
                nc.vector.memset(w4b[:, :], 1.0).then_inc(s["scaled_w"], 1)
                dve.wait_ge(s["mix_in"], 32)
                dve.wait_ge(s["scaled_w"], 1)
                nc.vector.tensor_scalar(w4b[:, :], w4b[:, :], w4[:, 0:1], None,
                                        ALU.mult).then_inc(s["scaled_w"], 1)
                dve.wait_ge(s["col_in_psum"], 1)
                nc.vector.tensor_copy(col[:, :], col_ps[:, 0:DIM]).then_inc(s["col_done"], 1)
                dve.wait_ge(s["col_done"], 1)
                split[2](dve)
                for g in range(BATCH):
                    dve.wait_ge(rows_in[g], 16 * TILES)
                    h4 = hid[:, g * TILES:(g + 1) * TILES, :]
                    nc.vector.tensor_tensor(h4, h4, col[:, :].unsqueeze(1).broadcast_to([P, TILES, DIM]),
                                            ALU.mult).then_inc(s["hid_done"], 1)
                dve.wait_ge(s["hid_done"], BATCH)
        reset(nc, s.values())


def first_attention(nc, hid, const, w):
    QT, NH = TILES, H0
    PAIR = 2
    T = PAIR * TILES
    HEADS = PAIR * NH
    N = HEADS * TILES
    WIDE = 32
    AHEAD, BEHIND, RING = 14, 2, 4
    TURN = 3
    GROUP = P // WIDE
    with ExitStack() as ctx:
        def sb(name, shape, dt=F32):
            return ctx.enter_context(nc.sbuf_tensor(name, shape, dt))

        s = signals(nc, ctx, "attn0", """stats_done moments_done rstd_done norm_done xT_in_psum xT_done
            x_hi_done x_lo_done ones_done
            qk_in_psum v_in_psum v_done rot_products rotated hi_done lo_done stacks_in_psum
            stacks_done scores_in_psum max_done maxima_in_psum maxima_in_q turned_in_psum exp_done pv_done
            group_copied group_in_psum group_done rden_done y_done yT_in_psum yT_done out_in_psum hid_done""")
        stats, mv, rstd = sb("a_stats", [P, T, 6]), sb("a_mv", [P, T, 2]), sb("a_rstd", [P, T])
        xn = sb("a_xn", [P, T, DIM + CB])
        xTa, xTb = sb("a_xTa", [P, T * P]), sb("a_xTb", [P, T * P])
        a_hi, a_lo = sb("a_a_hi", [P, T * P], F32R), sb("a_a_lo", [P, T * P], F32R)
        b_both, b_one = sb("a_b_both", [P, T * P], F32R), sb("a_b_one", [P, T * P], F32R)
        rc, rs = sb("a_rot_cos", [P, 3, 2 * NH, D0]), sb("a_rot_sin", [P, 3, 2 * NH, D0])
        stack = sb("a_stack", [P, 3, 2 * NH, 4, D0], F32R)
        qkT = sb("a_qkT", [P, PAIR, NH, SEQ], F32R)
        v = sb("a_v", [P, T, NH, WIDE])
        probs = sb("a_probs", [P, RING, SEQ])
        nmax = sb("a_nmax", [P, 2, QT, 97], F32R)
        group = sb("a_group", [P, SEQ])
        weighed = sb("a_weighed", [P, TILES, GROUP, WIDE])
        rden = sb("a_rden", [P, TILES, GROUP])
        y = xn
        work = ctx.enter_context(nc.psum_tensor("a_work", [P, 4, 512], F32))
        ps_a = work[:, 0:2, :].rearrange("p b k -> p (b k)")
        ps_b = work[:, 2:4, :].rearrange("p b k -> p (b k)")
        turn = ctx.enter_context(nc.psum_tensor("a_turn", [P, 2, 512], F32))
        yps = ctx.enter_context(nc.psum_tensor("a_y_ps", [P, 2, 512], F32))
        nc.vector.tensor_copy(b_one[CB:P, :], const["bias_rows"][CB:P, 0:1].broadcast_to([CB, T * P]))
        nc.gpsimd.memset(v[:, :, :, D0:WIDE], 1.0)
        nc.vector.memset(nmax[:, :, :, :].bitcast(F32), 0.0)
        nc.vector.memset(stack[:, :, :, 2, :].bitcast(F32), 0.0)
        nc.all_engine_barrier()
        nc.vector.memset(stack[:, :, NH:2 * NH, 2, 0:1].bitcast(F32), 1.0)
        nc.all_engine_barrier()

        with nc.Fori(0, BATCH // PAIR) as b:
            rows = [hid[:, bass.ds(b * T + t, 1), :].rearrange("p o c -> p (o c)") for t in range(T)]
            with nc.Block() as block:
                def parts(a, high):
                    if a == 0:
                        return slice(0, 2) if high else slice(3, 4)
                    return slice(0, 4, 3) if high else slice(1, 2)

                @block.vector
                def _(dve):
                    layer_norm_vector(nc, dve, s, rows, stats, mv, rstd, xn)
                    for k in range(PAIR):
                        half = slice(k * SEQ, (k + 1) * SEQ)
                        dve.wait_ge(s["xT_done"], 2 * (k + 1))
                        nc.vector.tensor_copy(a_hi[:, half], xTa[:, half]).then_inc(s["x_hi_done"], 1)
                        nc.vector.tensor_copy(b_both[:, half], xTb[:, half]).then_inc(s["x_hi_done"], 1)
                        nc.vector.tensor_copy(b_one[0:CB, half], xTb[0:CB, half]).then_inc(s["x_hi_done"], 1)
                        dve.wait_ge(s["x_hi_done"], 3 * k + 2)
                        nc.vector.tensor_tensor(a_lo[:, half], xTa[:, half], a_hi[:, half].bitcast(F32),
                                                ALU.subtract).then_inc(s["x_lo_done"], 1)
                        low = b_both[CB:P, half]
                        nc.vector.tensor_tensor(low, xTb[CB:P, half], low.bitcast(F32),
                                                ALU.subtract).then_inc(s["x_lo_done"], 1)
                    for t in range(T):
                        dve.wait_ge(s["qk_in_psum"], t + 1)
                        if t >= 3:
                            dve.wait_ge(s["lo_done"], 2 * (t - 2))
                        qk = work[:, t % 2, 0:2 * DIM].rearrange("p (a h d) -> p a h d", a=2, h=NH)
                        cos = const["cos"][:, t % TILES].unsqueeze(2).broadcast_to([P, 2, NH, D0])
                        nc.vector.tensor_tensor(rc[:, t % 3].rearrange("p (a h) d -> p a h d", a=2), qk, cos,
                                                ALU.mult).then_inc(s["rot_products"], 1)
                        for a in range(2):
                            pair = work[:, t % 2, a * DIM:(a + 1) * DIM].rearrange(
                                "p (h i two) -> p h i two", h=NH, two=2)
                            dst = rs[:, t % 3, a * NH:(a + 1) * NH].rearrange("p h (i two) -> p h i two", two=2)
                            sin = const["sin"][:, t % TILES, a, :].rearrange("p (i two) -> p i two", two=2)
                            sin = sin.unsqueeze(1).broadcast_to([P, NH, D0 // 2, 2])
                            nc.vector.tensor_tensor(dst, pair[:, :, :, ::-1], sin,
                                                    ALU.mult).then_inc(s["rot_products"], 1)

                    def row_max(m):
                        h, q = divmod(m, QT)
                        dve.wait_ge(s["scores_in_psum"], m + 1)
                        if m % (2 * QT) == 0 and m >= 4 * QT:
                            dve.wait_ge(s["maxima_in_psum"], m // (2 * QT) - 1)
                        at = 32 + 64 * (h % 2)
                        nc.vector.tensor_reduce(nmax[:, (h // 2) % 2, q, at:at + 1],
                                                work[:, m % 2, 0:(q + 1) * P], AX, ALU.max,
                                                negate=True).then_inc(s["max_done"], 1)

                    def scale_y(g):
                        dve.wait_ge(s["group_done"], g + 1)
                        nc.vector.reciprocal(rden[:, :, :], weighed[:, :, :, D0]).then_inc(s["rden_done"], 1)
                        dve.wait_ge(s["rden_done"], g + 1)
                        seq, part = divmod(g, NH // GROUP)
                        cols = slice(part * GROUP * D0, (part + 1) * GROUP * D0)
                        nc.vector.tensor_tensor(
                            y[:, seq * TILES:(seq + 1) * TILES, cols].rearrange("p t (h d) -> p t h d", h=GROUP),
                            weighed[:, :, :, 0:D0],
                            rden[:, :, :].unsqueeze(3).broadcast_to([P, TILES, GROUP, D0]),
                            ALU.mult).then_inc(s["y_done"], 1)

                    dve.wait_ge(s["x_lo_done"], 2 * PAIR)
                    nc.vector.memset(xTb[CB:CB + 1, :], 1.0).then_inc(s["ones_done"], 1)
                    for m in range(AHEAD):
                        row_max(m)
                    for n in range(N + BEHIND):
                        if n + AHEAD < N:
                            row_max(n + AHEAD)
                        if n >= GROUP * TILES + BEHIND + 4 and (n - BEHIND - 4) % (GROUP * TILES) == 0:
                            scale_y((n - BEHIND - 4) // (GROUP * TILES) - 1)
                    scale_y(HEADS // GROUP - 1)
                    for t in range(T):
                        dve.wait_ge(s["out_in_psum"], t + 1)
                        nc.vector.tensor_tensor(rows[t], yps[:, t % 2, 0:DIM], rows[t],
                                                ALU.add).then_inc(s["hid_done"], 1)

                @block.gpsimd
                def _(pool):
                    rstd_gpsimd(nc, pool, s["rstd_done"], mv, rstd, const["neg_half"], s["moments_done"], T)
                    for t in range(T):
                        pool.wait_ge(s["rot_products"], 3 * (t + 1))
                        nc.gpsimd.tensor_tensor(rc[:, t % 3], rc[:, t % 3], rs[:, t % 3],
                                                ALU.add).then_inc(s["rotated"], 1)
                        pool.wait_ge(s["rotated"], t + 1)
                        pool.wait_ge(s["hi_done"], 2 * (t + 1))
                        if t >= 3:
                            pool.wait_ge(s["stacks_in_psum"], 3 * (t - 2))
                        st = stack[:, t % 3]
                        for a in range(2):
                            heads = slice(a * NH, (a + 1) * NH)
                            nc.gpsimd.tensor_tensor(st[:, heads, parts(a, False), :].rearrange("p h o d -> p h (o d)"),
                                                    rc[:, t % 3, heads, :], st[:, heads, 0, :].bitcast(F32),
                                                    ALU.subtract).then_inc(s["lo_done"], 1)

                def copy_stacks(act, t):
                    for j in range(3):
                        n = 3 * t + j
                        act.wait_ge(s["stacks_in_psum"], n + 1)
                        seq, tt = divmod(t, TILES)
                        nc.scalar.copy(qkT[:, seq, 4 * j:4 * j + 4, tt * P:(tt + 1) * P],
                                       turn[:, n % 2, :].rearrange("p (c k) -> p c k", c=4)
                                       ).then_inc(s["stacks_done"], 1)

                @block.scalar
                def _(act):
                    for k in range(PAIR):
                        half = slice(k * SEQ, (k + 1) * SEQ)
                        act.wait_ge(s["xT_in_psum"], TILES * (k + 1))
                        nc.scalar.copy(xTa[:, half], ps_a[:, half]).then_inc(s["xT_done"], 1)
                        nc.scalar.copy(xTb[:, half], ps_b[:, half]).then_inc(s["xT_done"], 1)
                    for t in range(T):
                        act.wait_ge(s["v_in_psum"], t + 1)
                        nc.scalar.copy(v[:, t, :, 0:D0], work[:, 2 + t % 2, 0:DIM].rearrange(
                            "p (h d) -> p h d", h=NH)).then_inc(s["v_done"], 1)
                        if t >= 2:
                            copy_stacks(act, t - 2)
                        act.wait_ge(s["rotated"], t + 1)
                        if t >= 3:
                            act.wait_ge(s["stacks_in_psum"], 3 * (t - 2))
                        st = stack[:, t % 3]
                        for a in range(2):
                            heads = slice(a * NH, (a + 1) * NH)
                            r = rc[:, t % 3, heads, :].unsqueeze(2).broadcast_to([P, NH, 2, D0])
                            nc.scalar.copy(st[:, heads, parts(a, True), :], r).then_inc(s["hi_done"], 1)
                    copy_stacks(act, T - 2)
                    copy_stacks(act, T - 1)

                    def exponentials(n):
                        j = n % TILES
                        act.wait_ge(s["turned_in_psum"], n + 1)
                        if n >= RING:
                            act.wait_ge(s["pv_done"], n - RING + 1)
                        nc.scalar.activation(probs[:, n % RING, j * P:SEQ], work[:, 2 + n % 2, j * P:SEQ],
                                             ACT.Exp).then_inc(s["exp_done"], 1)

                    def copy_maxima(pair):
                        act.wait_ge(s["maxima_in_psum"], pair + 1)
                        for at in (32, 96):
                            seq, p = divmod(pair, NH // 2)
                            nc.scalar.copy(qkT[at:at + 1, seq, p, :], turn[at:at + 1, 0, :]
                                           ).then_inc(s["maxima_in_q"], 1)

                    def copy_group(g):
                        act.wait_ge(s["pv_done"], GROUP * TILES * (g + 1))
                        nc.scalar.copy(group[:, :], yps[:, g % 2, :]).then_inc(s["group_copied"], 1)

                    def take_group(g):
                        act.wait_ge(s["group_in_psum"], g + 1)
                        if g:
                            act.wait_ge(s["y_done"], g)
                        nc.scalar.copy(weighed[:, :, :, :], turn[:, 1, :].rearrange(
                            "p (t h d) -> p t h d", t=TILES, h=GROUP)).then_inc(s["group_done"], 1)

                    copy_maxima(0)
                    for n in range(N + BEHIND):
                        if n < N:
                            exponentials(n)
                        if n < N - 2 * TILES and n % (2 * TILES) == TURN:
                            copy_maxima(n // (2 * TILES) + 1)
                        if n >= GROUP * TILES + BEHIND and (n - BEHIND) % (GROUP * TILES) == 0:
                            copy_group((n - BEHIND) // (GROUP * TILES) - 1)
                        if n >= GROUP * TILES + BEHIND + 2 and (n - BEHIND - 2) % (GROUP * TILES) == 0:
                            take_group((n - BEHIND - 2) // (GROUP * TILES) - 1)
                    copy_group(HEADS // GROUP - 1)
                    take_group(HEADS // GROUP - 1)
                    act.wait_ge(s["yT_in_psum"], T)
                    nc.scalar.copy(xTa[:, :], ps_a).then_inc(s["yT_done"], 1)
                    nc.scalar.copy(xTb[0:CB, :], ps_b[0:CB, :]).then_inc(s["yT_done"], 1)

                @block.tensor
                def _(pe):
                    for t in range(T):
                        pe.wait_ge(s["norm_done"], 2 * (t + 1))
                        tok = slice(t * P, (t + 1) * P)
                        nc.tensor.transpose(ps_a[:, tok], xn[:, t, 0:CA], const["ident"][:, :])
                        nc.tensor.transpose(ps_b[:, tok], xn[:, t, CA:CA + P],
                                            const["ident"][:, :]).then_inc(s["xT_in_psum"], 1)

                    def stacks(t):
                        pe.wait_ge(s["hi_done"], 2 * (t + 1))
                        pe.wait_ge(s["lo_done"], 2 * (t + 1))
                        for j in range(3):
                            n = 3 * t + j
                            if n >= 2:
                                pe.wait_ge(s["stacks_done"], n - 1)
                            for c in range(4):
                                pair = stack[:, t % 3, 2 * (4 * j + c):2 * (4 * j + c) + 2].rearrange(
                                    "p h a d -> p (h a d)")
                                ins = nc.tensor.matmul(turn[:, n % 2, c * P:(c + 1) * P], pair,
                                                       const["ident_r"][:, :], start=True, stop=True)
                            ins.then_inc(s["stacks_in_psum"], 1)

                    for t in range(T):
                        tok = slice(t * P, (t + 1) * P)
                        if t >= 2:
                            pe.wait_ge(s["rot_products"], 3 * (t - 1))
                            pe.wait_ge(s["v_done"], t - 1)
                        if t == 0:
                            pe.wait_ge(s["xT_done"], 2 * PAIR)
                        if t % TILES == 0:
                            pe.wait_ge(s["x_hi_done"], 3 * (t // TILES + 1))
                            pe.wait_ge(s["x_lo_done"], 2 * (t // TILES + 1))
                        pairs = ((a_hi, w["a_hi"]), (b_both, w["b_hi"]), (a_lo, w["a_hi"]),
                                 (a_hi, w["a_lo"]), (b_one, w["b_lo"]))
                        for out, cols, done in ((work[:, t % 2, 0:2 * DIM], slice(0, 2 * DIM), "qk_in_psum"),
                                                (work[:, 2 + t % 2, 0:DIM], slice(2 * DIM, 3 * DIM), "v_in_psum")):
                            for i, (x, m) in enumerate(pairs):
                                ins = nc.tensor.matmul(out, x[:, tok], m[:, cols], start=(i == 0),
                                                       stop=(i == len(pairs) - 1))
                            ins.then_inc(s[done], 1)
                        if t >= 2:
                            stacks(t - 2)
                    stacks(T - 2)
                    stacks(T - 1)
                    pe.wait_ge(s["stacks_done"], 3 * T)
                    pe.wait_ge(s["v_done"], T)

                    def scores(m):
                        h, q = divmod(m, QT)
                        if m >= 2:
                            pe.wait_ge(s["max_done"], m - 1)
                        at = slice(64 * (h % 2), 64 * (h % 2) + 64)
                        seq, p = divmod(h // 2, NH // 2)
                        nc.tensor.matmul(work[:, m % 2, 0:(q + 1) * P], qkT[at, seq, p, q * P:(q + 1) * P],
                                         qkT[at, seq, NH // 2 + p, 0:(q + 1) * P], start=True, stop=False)
                        nc.tensor.matmul(work[:, m % 2, q * P:(q + 1) * P], const["ident_r"][:, :],
                                         const["causal_r"][:, :], start=False,
                                         stop=True).then_inc(s["scores_in_psum"], 1)

                    def turn_maxima(pair):
                        pe.wait_ge(s["max_done"], 2 * QT * (pair + 1))
                        if pair:
                            pe.wait_ge(s["maxima_in_q"], 2 * pair)
                        for q in range(QT):
                            ins = nc.tensor.matmul(turn[0:97, 0, q * P:(q + 1) * P], nmax[:, pair % 2, q, :],
                                                   const["ident_r"][:, :], start=True, stop=True)
                        ins.then_inc(s["maxima_in_psum"], 1)

                    def scores_turned(n):
                        h, j = divmod(n, TILES)
                        if n % (2 * TILES) == 0:
                            pe.wait_ge(s["maxima_in_q"], 2 * (n // (2 * TILES) + 1))
                        if n >= 2:
                            pe.wait_ge(s["exp_done"], n - 1)
                        at = slice(64 * (h % 2), 64 * (h % 2) + 64)
                        seq, p = divmod(h // 2, NH // 2)
                        nc.tensor.matmul(work[:, 2 + n % 2, j * P:SEQ],
                                         qkT[at, seq, NH // 2 + p, j * P:(j + 1) * P],
                                         qkT[at, seq, p, j * P:SEQ], start=True, stop=False)
                        nc.tensor.matmul(work[:, 2 + n % 2, j * P:(j + 1) * P], const["causal_r"][:, :],
                                         const["ident_r"][:, :], start=False,
                                         stop=True).then_inc(s["turned_in_psum"], 1)

                    def weigh_values(n):
                        h, j = divmod(n, TILES)
                        pe.wait_ge(s["exp_done"], n + 1)
                        g, i = divmod(h, GROUP)
                        if g >= 2 and i == 0 and j == 0:
                            pe.wait_ge(s["group_copied"], g - 1)
                        nc.tensor.matmul(yps[i * WIDE:(i + 1) * WIDE, g % 2, j * P:SEQ],
                                         v[:, (h // NH) * TILES + j, h % NH, :],
                                         probs[:, n % RING, j * P:SEQ], start=(j == 0),
                                         stop=(j == TILES - 1)).then_inc(s["pv_done"], 1)

                    def turn_group(g):
                        pe.wait_ge(s["group_copied"], g + 1)
                        if g:
                            pe.wait_ge(s["group_done"], g)
                        for t in range(TILES):
                            ins = nc.tensor.transpose(turn[:, 1, t * P:(t + 1) * P], group[:, t * P:(t + 1) * P],
                                                      const["ident"][:, :])
                        ins.then_inc(s["group_in_psum"], 1)

                    for m in range(AHEAD):
                        scores(m)
                        if m == 2 * QT:
                            turn_maxima(0)
                    for n in range(N + BEHIND):
                        if n + AHEAD < N:
                            scores(n + AHEAD)
                        if n < N - 2 * TILES and n % (2 * TILES) == TURN:
                            turn_maxima(n // (2 * TILES) + 1)
                        if n < N:
                            scores_turned(n)
                        if n >= BEHIND:
                            weigh_values(n - BEHIND)
                        if n >= GROUP * TILES + BEHIND + 1 and (n - BEHIND - 1) % (GROUP * TILES) == 0:
                            turn_group((n - BEHIND - 1) // (GROUP * TILES) - 1)
                    turn_group(HEADS // GROUP - 1)
                    pe.wait_ge(s["max_done"], N)
                    pe.wait_ge(s["y_done"], HEADS // GROUP)
                    for t in range(T):
                        tok = slice(t * P, (t + 1) * P)
                        nc.tensor.transpose(ps_a[:, tok], y[:, t, 0:CA], const["ident"][:, :])
                        nc.tensor.transpose(ps_b[0:CB, tok], y[:, t, CA:DIM],
                                            const["ident"][:, :]).then_inc(s["yT_in_psum"], 1)
                    pe.wait_ge(s["yT_done"], 2)
                    pe.wait_ge(s["ones_done"], 1)
                    for t in range(T):
                        tok = slice(t * P, (t + 1) * P)
                        if t >= 2:
                            pe.wait_ge(s["hid_done"], t - 1)
                        nc.tensor.matmul(yps[:, t % 2, 0:DIM], xTa[:, tok], w["proj_a"][:, :],
                                         start=True, stop=False)
                        nc.tensor.matmul(yps[:, t % 2, 0:DIM], xTb[0:CB + 1, tok], w["proj_b"][:, :],
                                         start=False, stop=True).then_inc(s["out_in_psum"], 1)
            reset(nc, s.values())


def second_attention(nc, hid, const, w):
    QT, NH = TILES, H1
    INNER = NH * D1
    CH = INNER // P
    VH = INNER // 2
    WIDE = D1 + 1
    scale = D1 ** -0.5

    shared = {(g, 3): [("maxima", g + 1)] for g in range(NH)}
    slots = [(g, j) for g in range(NH) for j in range(3)]

    def share(first, kind, numbers):
        for at, n in zip(slots[slots.index(first):], numbers):
            shared[at] = [(kind, n)]

    share((1, 0), "v_high", range(TILES - 1))
    share((2, 0), "yT", range(CH))
    share((4, 0), "v_high", [TILES - 1])
    share((4, 1), "out", range(TILES))
    share((8, 1), "xT_a", [0])
    share((8, 2), "xT_b", [0])
    share((10, 0), "v_low", range(TILES))
    steps = [(g, j) for g in range(NH) for j in range(4)]

    with ExitStack() as ctx:
        def sb(name, shape, dt=F32):
            return ctx.enter_context(nc.sbuf_tensor(name, shape, dt))

        s = signals(nc, ctx, "attn1", """stats_done moments_done rstd_done norm_done x_hi_done x_lo_done
            bank_filled bank_taken qk_in_psum qk_hi_done q_twice qk_lo_done k_copied scores_in_psum max_done
            turned_in_psum exp_done pv_done rden_done y_done hid_done""")
        stats, mv, rstd = sb("c_stats", [P, TILES, 6]), sb("c_mv", [P, TILES, 2]), sb("c_rstd", [P, TILES])
        xn = sb("c_xn", [P, TILES, DIM + CB])
        xa, xb = sb("c_xa", [P, SEQ]), sb("c_xb", [P, SEQ])
        a_hi, a_lo = sb("c_a_hi", [P, SEQ], F32R), sb("c_a_lo", [P, SEQ], F32R)
        b_both, b_one = sb("c_b_both", [P, SEQ], F32R), sb("c_b_one", [P, SEQ], F32R)
        q_hi, q_lo = sb("c_q_hi", [P, 4, SEQ], F32R), sb("c_q_lo", [WIDE, 4, SEQ], F32R)
        k_both, k_one = sb("c_k_both", [P, 4, SEQ], F32R), sb("c_k_one", [WIDE, 4, SEQ], F32R)
        v = sb("c_v", [P, TILES, NH, WIDE])
        probs = sb("c_probs", [P, 2, TILES, SEQ])
        nmax = sb("c_nmax", [P, NH * QT], F32R)
        rden = sb("c_rden", [P, NH, QT])
        y, yT = sb("c_y", [P, TILES, INNER]), sb("c_yT", [P, CH, SEQ])
        added = sb("c_added", [P, TILES, DIM])
        rows_ps = ctx.enter_context(nc.psum_tensor("c_scores", [P, 2, 512], F32))
        cols_ps = ctx.enter_context(nc.psum_tensor("c_turned", [P, 2, 512], F32))
        y_ps = ctx.enter_context(nc.psum_tensor("c_y_ps", [P, 2, 512], F32))
        qk_ps = ctx.enter_context(nc.psum_tensor("c_qk_ps", [P, 512], F32))
        bank = ctx.enter_context(nc.psum_tensor("c_bank", [P, 512], F32))
        nc.vector.tensor_copy(b_one[CB:P, :], const["bias_rows"][CB:P, 0:1].broadcast_to([CB, SEQ]))
        for k in range(4):
            nc.vector.tensor_copy(k_one[D1:WIDE, k, :], const["ones_row"][0:1, 0:1].broadcast_to([1, SEQ]))
        nc.vector.memset(v[:, :, :, D1:WIDE], 1.0)
        nc.all_engine_barrier()

        def wait(eng, sem, value):
            if value > 0:
                eng.wait_ge(s[sem], value)

        def halves(h):
            low, high = slice(0, D1), slice(D1, P)
            return (high, low) if h % 2 else (low, high)

        def sequence(b, has_prev, has_own, has_next):
            def mine(h):
                return has_prev if h < 0 else has_own if h < NH else has_next

            def rows(seq, t):
                return hid[:, bass.ds(seq * TILES + t, 1), :].rearrange("p o c -> p (o c)")

            def projected(g, j):
                h, is_k = (g + 3, 0) if g % 2 else (g + 2, 1)
                return [(h, is_k), (h + 1, is_k)] if j == (1 if is_k else 3) and mine(h) else []

            def repeated(g, j):
                return [g + 2, g + 3] if g % 2 == 0 and j == 3 and mine(g + 2) else []

            def uses(g, j):
                wanted = {"xT_a": has_next, "xT_b": has_next, "v_low": has_next, "v_high": has_own,
                          "yT": has_prev, "out": has_prev}
                return [(kind, n) for kind, n in shared.get((g, j), [])
                        if (mine(n) if kind == "maxima" else wanted[kind])]

            everything = [use for g, j in steps for use in uses(g, j)]
            place = {use: i for i, use in enumerate(everything)}
            qk = [hk for g, j in steps for hk in projected(g, j)]
            order = {hk: i for i, hk in enumerate(qk)}
            q_order = {h: i for i, h in enumerate(h for g, j in steps for h in repeated(g, j))}
            k_order = {h: i for i, (h, _) in enumerate(hk for hk in qk if hk[1])}
            scored = [h for h in range(1, NH + 1) if mine(h)]

            def score_place(h, q):
                return QT * (h - scored[0]) + q

            def turned_count(h):
                return TILES * (h + 1) if has_own else 0

            def pv_count(h):
                return QT * (h + (2 if has_prev else 1))

            def y_count(h):
                return h + (3 if has_prev else 1)

            with nc.Block() as block:
                @block.vector
                def _(dve):
                    def moments():
                        for t in range(TILES):
                            nc.vector.bn_stats(stats[:, t, :], rows(b + 1, t)).then_inc(s["stats_done"], 1)
                        for t in range(TILES):
                            dve.wait_ge(s["stats_done"], t + 1)
                            nc.vector.bn_aggr(mv[:, t, :], stats[:, t, :]).then_inc(s["moments_done"], 1)

                    def norm():
                        dve.wait_ge(s["rstd_done"], 2)
                        dve.wait_ge(s["moments_done"], TILES)
                        for t in range(TILES):
                            nc.vector.tensor_scalar(xn[:, t, 0:DIM], rows(b + 1, t), mv[:, t, 0:1], rstd[:, t:t + 1],
                                                    ALU.subtract, ALU.mult).then_inc(s["norm_done"], 1)
                        dve.wait_ge(s["norm_done"], TILES)
                        nc.vector.tensor_copy(xn[:, :, DIM:DIM + CB], xn[:, :, CA:DIM]).then_inc(s["norm_done"], 1)

                    def split_a():
                        dve.wait_ge(s["bank_taken"], place["xT_a", 0] + 1)
                        if has_own:
                            dve.wait_ge(s["qk_in_psum"], order[NH - 2, 1] // 2 + 1)
                        nc.vector.tensor_copy(a_hi[:, :], xa[:, :]).then_inc(s["x_hi_done"], 1)
                        dve.wait_ge(s["x_hi_done"], 1)
                        nc.vector.tensor_tensor(a_lo[:, :], xa[:, :], a_hi[:, :].bitcast(F32),
                                                ALU.subtract).then_inc(s["x_lo_done"], 1)

                    def split_b():
                        dve.wait_ge(s["bank_taken"], place["xT_b", 0] + 1)
                        nc.vector.tensor_copy(b_both[:, :], xb[:, :]).then_inc(s["x_hi_done"], 1)
                        nc.vector.tensor_copy(b_one[0:CB, :], xb[0:CB, :]).then_inc(s["x_hi_done"], 1)
                        dve.wait_ge(s["x_hi_done"], 2)
                        low = b_both[CB:P, :]
                        nc.vector.tensor_tensor(low, xb[CB:P, :], low.bitcast(F32),
                                                ALU.subtract).then_inc(s["x_lo_done"], 1)

                    def row_max(h, q):
                        n = score_place(h, q)
                        dve.wait_ge(s["scores_in_psum"], n + 1)
                        nc.vector.tensor_reduce(nmax[:, n:n + 1], rows_ps[:, n % 2, :], AX, ALU.max,
                                                negate=True).then_inc(s["max_done"], 1)

                    def low_part(h, is_k):
                        own, other = halves(h)
                        dve.wait_ge(s["qk_hi_done"], order[h, is_k] + 1)
                        wait(dve, "turned_in_psum", turned_count(h - 4))
                        if is_k:
                            nc.vector.tensor_tensor(k_both[other, h % 4, :], qk_ps[own, :],
                                                    k_both[own, h % 4, :].bitcast(F32),
                                                    ALU.subtract).then_inc(s["qk_lo_done"], 1)
                        else:
                            nc.vector.scalar_tensor_tensor(q_lo[0:D1, h % 4, :], qk_ps[own, :], scale,
                                                           q_hi[own, h % 4, :].bitcast(F32), ALU.mult,
                                                           ALU.subtract).then_inc(s["qk_lo_done"], 1)

                    def scale_y(h):
                        wait(dve, "pv_done", pv_count(h))
                        hh = h % NH
                        got = y_ps[:, h % 2, 0:QT * WIDE].rearrange("p (q d) -> p q d", q=QT)
                        nc.vector.reciprocal(rden[:, hh, :], got[:, :, D1]).then_inc(s["rden_done"], 1)
                        dve.wait_ge(s["rden_done"], y_count(h))
                        if h >= 0 and has_prev:
                            dve.wait_ge(s["bank_filled"], place["yT", hh // 2] + 1)
                        nc.vector.scalar_tensor_tensor(
                            y[:, :, hh * D1:(hh + 1) * D1], got[:, :, 0:D1], w["head_scale"][:, hh:hh + 1],
                            rden[:, hh, :].unsqueeze(2).broadcast_to([P, QT, D1]),
                            ALU.mult, ALU.mult).then_inc(s["y_done"], 1)

                    for g, j in steps:
                        if mine(g + 1):
                            for q in ((0, 1), (2, 3), (), ())[j]:
                                row_max(g + 1, q)
                        for h, is_k in projected(g, j):
                            low_part(h, is_k)
                        if j == 1 and mine(g - 2):
                            scale_y(g - 2)
                        if has_next and (g, j) == (4, 3):
                            moments()
                        if has_next and (g, j) == (6, 3):
                            norm()
                        if has_next and (g, j) == (8, 3):
                            split_a()
                        if has_next and (g, j) == (9, 2):
                            split_b()

                @block.gpsimd
                def _(pool):
                    for g, j in steps:
                        for h, is_k in projected(g, j):
                            if is_k:
                                pool.wait_ge(s["qk_hi_done"], order[h, 1] + 1)
                                wait(pool, "turned_in_psum", turned_count(h - 4))
                                nc.gpsimd.tensor_copy(k_one[0:D1, h % 4, :], k_both[halves(h)[0], h % 4, :]
                                                      ).then_inc(s["k_copied"], 1)
                                pool.wait_ge(s["k_copied"], k_order[h] + 1)
                        if has_next and (g, j) == (5, 3):
                            rstd_gpsimd(nc, pool, s["rstd_done"], mv, rstd, const["neg_half"],
                                        s["moments_done"], TILES)
                            pool.wait_ge(s["rstd_done"], 2)
                        for kind, t in uses(g, j):
                            if kind == "out":
                                pool.wait_ge(s["bank_taken"], place[kind, t] + 1)
                                nc.gpsimd.tensor_tensor(rows(b - 1, t), added[:, t, :], rows(b - 1, t),
                                                        ALU.add).then_inc(s["hid_done"], 1)
                                pool.wait_ge(s["hid_done"], t + 1)

                @block.scalar
                def _(act):
                    def high_part(h, is_k):
                        own, _ = halves(h)
                        act.wait_ge(s["qk_in_psum"], order[h, is_k] // 2 + 1)
                        wait(act, "turned_in_psum", turned_count(h - 4))
                        dst, by = (k_both, 1.0) if is_k else (q_hi, scale)
                        nc.scalar.activation(dst[own, h % 4, :], qk_ps[own, :], ACT.Copy,
                                             scale=by).then_inc(s["qk_hi_done"], 1)

                    def repeat_q(h):
                        own, other = halves(h)
                        if (h, 0) in order:
                            act.wait_ge(s["qk_hi_done"], order[h, 0] + 1)
                            wait(act, "turned_in_psum", turned_count(h - 4))
                        nc.scalar.copy(q_hi[other, h % 4, :], q_hi[own, h % 4, :]).then_inc(s["q_twice"], 1)

                    def exponentials(h, j):
                        n = TILES * h + j
                        act.wait_ge(s["turned_in_psum"], n + 1)
                        if mine(h - 2):
                            wait(act, "pv_done", pv_count(h - 2))
                        nc.scalar.activation(probs[:, h % 2, j, :], cols_ps[:, n % 2, :],
                                             ACT.Exp).then_inc(s["exp_done"], 1)

                    def take(kind, n):
                        act.wait_ge(s["bank_filled"], place[kind, n] + 1)
                        src = bank[:, :]
                        if kind == "maxima":
                            dst, src = q_lo[D1:WIDE, n % 4, :], bank[D1:WIDE, :]
                        elif kind == "xT_a":
                            dst = xa[:, :]
                        elif kind == "xT_b":
                            dst = xb[:, :]
                        elif kind in ("v_low", "v_high"):
                            if kind == "v_high" and has_prev:
                                act.wait_ge(s["pv_done"], pv_count(-1))
                            if kind == "v_low" and has_own:
                                act.wait_ge(s["pv_done"], pv_count(NH // 2 - 1))
                            heads = slice(0, NH // 2) if kind == "v_low" else slice(NH // 2, NH)
                            dst = v[:, n, heads, 0:D1]
                            src = bank[:, 0:VH].rearrange("p (h d) -> p h d", d=D1)
                        elif kind == "yT":
                            dst = yT[:, n, :]
                        else:
                            dst, src = added[:, n, :], bank[:, 0:DIM]
                        nc.scalar.copy(dst, src).then_inc(s["bank_taken"], 1)

                    for g, j in steps:
                        for use in uses(g, j):
                            take(*use)
                        if mine(g):
                            exponentials(g, j)
                        for h, is_k in projected(g, j):
                            high_part(h, is_k)
                        for h in repeated(g, j):
                            repeat_q(h)

                @block.tensor
                def _(pe):
                    def wait_x(h):
                        if h >= NH:
                            pe.wait_ge(s["x_hi_done"], 3)
                            pe.wait_ge(s["x_lo_done"], 2)

                    def project(h, is_k):
                        wait(pe, "qk_lo_done", order[h, is_k])
                        wait_x(h)
                        hh = h % NH
                        c = slice((is_k * NH + hh) * D1, (is_k * NH + hh + 2) * D1)
                        pairs = ((w["a_hi"], a_hi), (w["b_hi"], b_both), (w["a_hi"], a_lo),
                                 (w["a_lo"], a_hi), (w["b_lo"], b_one))
                        for i, (m, x) in enumerate(pairs):
                            ins = nc.tensor.matmul(qk_ps[:, :], m[:, c], x[:, :], start=(i == 0),
                                                   stop=(i == len(pairs) - 1))
                        ins.then_inc(s["qk_in_psum"], 1)

                    def scores(h, q):
                        n = score_place(h, q)
                        if q == 0:
                            if (h, 1) in order:
                                pe.wait_ge(s["qk_lo_done"], order[h, 1] + 1)
                            if h in q_order:
                                pe.wait_ge(s["q_twice"], q_order[h] + 1)
                        wait(pe, "max_done", n - 1)
                        nc.tensor.matmul(rows_ps[:, n % 2, :], q_hi[:, h % 4, q * P:(q + 1) * P],
                                         k_both[:, h % 4, :], start=True, stop=True).then_inc(s["scores_in_psum"], 1)

                    def scores_turned(h, j):
                        n = TILES * h + j
                        if j == 0:
                            if ("maxima", h) in place:
                                pe.wait_ge(s["bank_taken"], place["maxima", h] + 1)
                            if h in k_order:
                                pe.wait_ge(s["k_copied"], k_order[h] + 1)
                        wait(pe, "exp_done", n - 1)
                        keys = slice(j * P, (j + 1) * P)
                        nc.tensor.matmul(cols_ps[:, n % 2, :], k_both[:, h % 4, keys], q_hi[:, h % 4, :],
                                         start=True, stop=False)
                        nc.tensor.matmul(cols_ps[:, n % 2, :], k_one[:, h % 4, keys], q_lo[:, h % 4, :],
                                         start=False, stop=True).then_inc(s["turned_in_psum"], 1)

                    def weigh_values(h, q):
                        if q == 0:
                            if h >= 0:
                                pe.wait_ge(s["exp_done"], TILES * (h + 1))
                            if mine(h - 2):
                                wait(pe, "y_done", y_count(h - 2))
                            if h >= NH // 2:
                                pe.wait_ge(s["bank_taken"], place["v_high", TILES - 1] + 1)
                        for j in range(TILES):
                            ins = nc.tensor.matmul(y_ps[:, h % 2, q * WIDE:(q + 1) * WIDE],
                                                   probs[:, h % 2, j, q * P:(q + 1) * P],
                                                   v[:, j, h % NH, :],
                                                   start=(j == 0), stop=(j == TILES - 1))
                        ins.then_inc(s["pv_done"], 1)

                    def fill(kind, n):
                        wait(pe, "bank_taken", place[kind, n])
                        if kind == "maxima":
                            pe.wait_ge(s["max_done"], score_place(n, QT - 1) + 1)
                            for q in range(QT):
                                i = score_place(n, q)
                                ins = nc.tensor.matmul(bank[0:WIDE, q * P:(q + 1) * P],
                                                       nmax[:, i:i + 1].broadcast_to([P, WIDE]),
                                                       const["ident_r"][:, :], start=True, stop=True)
                        elif kind in ("xT_a", "xT_b"):
                            pe.wait_ge(s["norm_done"], TILES + 1)
                            c = 0 if kind == "xT_a" else CA
                            for t in range(TILES):
                                ins = nc.tensor.transpose(bank[:, t * P:(t + 1) * P], xn[:, t, c:c + P],
                                                          const["ident"][:, :])
                        elif kind in ("v_low", "v_high"):
                            if kind == "v_low":
                                wait_x(NH)
                            tok = slice(n * P, (n + 1) * P)
                            first = 2 * INNER + (0 if kind == "v_low" else VH)
                            cols = slice(first, first + VH)
                            pairs = ((a_hi, w["a_hi"]), (b_both, w["b_hi"]), (a_lo, w["a_hi"]),
                                     (a_hi, w["a_lo"]), (b_one, w["b_lo"]))
                            for i, (x, m) in enumerate(pairs):
                                ins = nc.tensor.matmul(bank[:, 0:VH], x[:, tok], m[:, cols],
                                                       start=(i == 0), stop=(i == len(pairs) - 1))
                        elif kind == "yT":
                            pe.wait_ge(s["y_done"], y_count(-1))
                            for t in range(TILES):
                                ins = nc.tensor.transpose(bank[:, t * P:(t + 1) * P],
                                                          y[:, t, n * P:(n + 1) * P], const["ident"][:, :])
                        else:
                            nc.tensor.matmul(bank[:, 0:DIM], const["ones_row"][0:1, :], w["out_bias"][0:1, :],
                                             start=True, stop=False)
                            for c in range(CH):
                                ins = nc.tensor.matmul(bank[:, 0:DIM], yT[:, c, n * P:(n + 1) * P],
                                                       w["out"][:, c, :], start=False, stop=(c == CH - 1))
                        ins.then_inc(s["bank_filled"], 1)

                    for g, j in steps:
                        for use in uses(g, j):
                            fill(*use)
                        if mine(g + 1):
                            for q in ((0, 1), (2, 3), (), ())[j]:
                                scores(g + 1, q)
                        if mine(g):
                            scores_turned(g, j)
                        if mine(g - 1):
                            weigh_values(g - 1, j)
                        for h, is_k in projected(g, j)[0:1]:
                            project(h, is_k)
            reset(nc, s.values())

        sequence(-1, False, False, True)
        sequence(0, False, True, True)
        with nc.Fori(1, BATCH - 1) as b:
            sequence(b, True, True, True)
        sequence(BATCH - 1, True, True, False)
        sequence(BATCH, True, False, False)


def route(nc, hid, xn_all, const, w, tag, first_layer, logits):
    ALL = BATCH * TILES
    R = 8
    with ExitStack() as ctx:
        def sb(name, shape, dt=F32):
            return ctx.enter_context(nc.sbuf_tensor(f"{tag}_{name}", shape, dt))

        s = signals(nc, ctx, tag + "route", """stats_done moments_done rstd_done norm_done kept xT_in_psum
            xTa_done xTb_done gate_in_psum gate_done logits_in_psum logits_done""")
        stats, mv, rstd = sb("stats", [P, ALL, 6]), sb("mv", [P, ALL, 2]), sb("rstd", [P, ALL])
        xn = sb("xn", [P, R, DIM])
        xTa, xTb = sb("xTa", [P, R * P]), sb("xTb", [CB, R * P])
        gT = sb("gT", [GATE_HID + 1, R * P])
        ps_a = ctx.enter_context(nc.psum_tensor(f"{tag}_xT_a", [P, R * P], F32))
        ps_b = ctx.enter_context(nc.psum_tensor(f"{tag}_xT_b", [P, R * P], F32))
        ps_g = ctx.enter_context(nc.psum_tensor(f"{tag}_gate", [P, R * P], F32))
        ps_l = ctx.enter_context(nc.psum_tensor(f"{tag}_logits_ps", [P, 512], F32))
        with nc.Block() as block:
            @block.vector
            def _(dve):
                nc.vector.memset(gT[GATE_HID:GATE_HID + 1, :], 1.0).then_inc(s["gate_done"], 1)
                dve.wait_ge(s["gate_done"], 1)
                for t in range(ALL):
                    nc.vector.bn_stats(stats[:, t, :], hid[:, t, :]).then_inc(s["stats_done"], 1)
                dve.wait_ge(s["stats_done"], ALL)
                for t in range(ALL):
                    nc.vector.bn_aggr(mv[:, t, :], stats[:, t, :]).then_inc(s["moments_done"], 1)

            @block.gpsimd
            def _(pool):
                pool.wait_ge(s["moments_done"], ALL)
                nc.gpsimd.tensor_scalar(rstd[:, :], mv[:, :, 1], LN_EPS, None,
                                        ALU.add).then_inc(s["rstd_done"], 1)
                pool.wait_ge(s["rstd_done"], 1)
                nc.gpsimd.tensor_tensor(rstd[:, :], rstd[:, :], const["neg_half"][:, 0:1].broadcast_to([P, ALL]),
                                        ALU.pow).then_inc(s["rstd_done"], 1)
                pool.wait_ge(s["rstd_done"], 2)
        reset(nc, s.values())

        with nc.Fori(0, ALL // R) as r:
            with nc.Block() as block:
                @block.vector
                def _(dve):
                    for j in range(R):
                        t = bass.ds(r * R + j, 1)
                        nc.vector.tensor_scalar(xn[:, j, :], hid[:, t, :].rearrange("p o c -> p (o c)"),
                                                mv[:, t, 0], rstd[:, t], ALU.subtract,
                                                ALU.mult).then_inc(s["norm_done"], 1)
                    for k in range(2):
                        half = slice(k * 512, (k + 1) * 512)
                        dve.wait_ge(s["xT_in_psum"], (R // 2) * (k + 1))
                        nc.vector.tensor_copy(xTb[:, half], ps_b[0:CB, half]).then_inc(s["xTb_done"], 1)
                    dve.wait_ge(s["logits_in_psum"], 1)
                    nc.vector.tensor_copy(logits[:, bass.ds(r * R, R), :],
                                          ps_l[:, 0:R * EXPERTS].rearrange("p (t e) -> p t e", t=R)
                                          ).then_inc(s["logits_done"], 1)
                    dve.wait_ge(s["logits_done"], 1)

                @block.gpsimd
                def _(pool):
                    pool.wait_ge(s["norm_done"], R)
                    nc.gpsimd.tensor_copy(xn_all[:, bass.ds(r * R, R), :], xn[:, :, :]).then_inc(s["kept"], 1)
                    pool.wait_ge(s["kept"], 1)

                @block.scalar
                def _(act):
                    for k in range(2):
                        half = slice(k * 512, (k + 1) * 512)
                        act.wait_ge(s["xT_in_psum"], (R // 2) * (k + 1))
                        nc.scalar.copy(xTa[:, half], ps_a[:, half]).then_inc(s["xTa_done"], 1)
                    if first_layer:
                        for k in range(2):
                            half = slice(k * 512, (k + 1) * 512)
                            act.wait_ge(s["gate_in_psum"], k + 1)
                            nc.scalar.activation(gT[0:GATE_HID, half], ps_g[0:GATE_HID, half], ACT.Gelu,
                                                 bias=w["gate_bias"][:, 0:1]).then_inc(s["gate_done"], 1)

                @block.tensor
                def _(pe):
                    for j in range(R):
                        pe.wait_ge(s["norm_done"], j + 1)
                        tok = slice(j * P, (j + 1) * P)
                        nc.tensor.transpose(ps_a[:, tok], xn[:, j, 0:CA], const["ident"][:, :])
                        nc.tensor.transpose(ps_b[0:CB, tok], xn[:, j, CA:DIM],
                                            const["ident"][:, :]).then_inc(s["xT_in_psum"], 1)
                    if first_layer:
                        for k in range(2):
                            half = slice(k * 512, (k + 1) * 512)
                            pe.wait_ge(s["xTa_done"], k + 1)
                            pe.wait_ge(s["xTb_done"], k + 1)
                            nc.tensor.matmul(ps_g[0:GATE_HID, half], w["gate_a"][:, :], xTa[:, half],
                                             start=True, stop=False)
                            nc.tensor.matmul(ps_g[0:GATE_HID, half], w["gate_b"][:, :], xTb[:, half],
                                             start=False, stop=True).then_inc(s["gate_in_psum"], 1)
                        pe.wait_ge(s["gate_done"], 2)
                    else:
                        pe.wait_ge(s["xTa_done"], 2)
                        pe.wait_ge(s["xTb_done"], 2)
                    for j in range(R):
                        tok = slice(j * P, (j + 1) * P)
                        lg = ps_l[:, j * EXPERTS:(j + 1) * EXPERTS]
                        if first_layer:
                            ins = nc.tensor.matmul(lg, gT[:, tok], w["gate2"][:, :], start=True, stop=True)
                        else:
                            nc.tensor.matmul(lg, xTa[:, tok], w["router_a"][:, :], start=True, stop=False)
                            ins = nc.tensor.matmul(lg, xTb[:, tok], w["router_b"][:, :], start=False, stop=True)
                    ins.then_inc(s["logits_in_psum"], 1)
            reset(nc, s.values())


def assign(nc, const, tag, first_layer, logits, weight, slot, owner):
    ALL = BATCH * TILES
    E = EXPERTS
    with ExitStack() as ctx:
        def sb(name, shape, dt=F32):
            return ctx.enter_context(nc.sbuf_tensor(f"{tag}_{name}", shape, dt))

        s = signals(nc, ctx, tag + "assign", "step shifted exp_done marked counts_in_psum")
        e = sb("probs", [P, ALL, E])
        top, norm = sb("top", [P, ALL]), sb("norm", [P, ALL])
        best, where, wheref = sb("best", [P, ALL, 8]), sb("where", [P, ALL, 8], U32), sb("wheref", [P, ALL, 8])
        pick = sb("pick", [P, 2, ALL, E])
        both, tmp = sb("both", [P, ALL, E]), sb("tmp", [P, ALL, E])
        run = sb("run", [P, 2, ALL, E])
        full = sb("full", [P, E, ALL])
        tiles, first, last = sb("tiles", [P, E]), sb("first", [P, E]), sb("last", [P, E])
        square = sb("square", [P, E, E])
        slotf = sb("slotf", [P, 2, ALL])
        ended = sb("ended", [1, SLOT_TILES, E])
        ownerf = sb("ownerf", [1, SLOT_TILES])
        ps = ctx.enter_context(nc.psum_tensor(f"{tag}_counts", [P, 2, 512], F32))
        wide = [P, ALL, E]
        with nc.Block() as block:
            @block.vector
            def _(dve):
                n = 0

                def chain(ins):
                    nonlocal n
                    n += 1
                    ins.then_inc(s["step"], 1)
                    dve.wait_ge(s["step"], n)

                chain(nc.vector.tensor_reduce(top[:, :], logits[:, :, :], AX, ALU.max))
                nc.vector.tensor_tensor(e[:, :, :], logits[:, :, :], top[:, :].unsqueeze(2).broadcast_to(wide),
                                        ALU.subtract).then_inc(s["shifted"], 1)
                dve.wait_ge(s["exp_done"], 1)
                chain(nc.vector.tensor_reduce(norm[:, :], e[:, :, :], AX, ALU.add))
                chain(nc.vector.reciprocal(norm[:, :], norm[:, :]))
                chain(nc.vector.tensor_tensor(e[:, :, :], e[:, :, :], norm[:, :].unsqueeze(2).broadcast_to(wide),
                                              ALU.mult))
                for t in range(ALL):
                    ins = nc.vector.max(best[:, t, :], e[:, t, :])
                chain(ins)
                for t in range(ALL):
                    ins = nc.vector.max_index(where[:, t, :], best[:, t, :], e[:, t, :])
                chain(ins)
                chain(nc.vector.tensor_copy(wheref[:, :, :], where[:, :, :]))
                for k in range(2):
                    ins = nc.vector.tensor_tensor(pick[:, k], const["places"][:, 0:1, :].broadcast_to(wide),
                                                  wheref[:, :, k:k + 1].broadcast_to(wide), ALU.is_equal)
                chain(ins)
                nc.vector.tensor_tensor(both[:, :, :], pick[:, 0], pick[:, 1], ALU.add).then_inc(s["marked"], 1)
                chain(nc.vector.tensor_tensor(norm[:, :], best[:, :, 0], best[:, :, 1], ALU.add))
                if first_layer:
                    chain(nc.vector.tensor_scalar(norm[:, :], norm[:, :], 1e-8, None, ALU.add))
                chain(nc.vector.reciprocal(norm[:, :], norm[:, :]))
                for k in range(2):
                    ins = nc.vector.tensor_tensor(weight[:, k, :], best[:, :, k], norm[:, :], ALU.mult)
                chain(ins)
                dve.wait_ge(s["counts_in_psum"], 1)
                total = ps[:, 1, 0:ALL * E].rearrange("p (t e) -> p t e", t=ALL)
                before = ps[:, 0, 0:ALL * E].rearrange("p (t e) -> p t e", t=ALL)
                chain(nc.vector.tensor_copy(run[:, 0], total))
                cur, d = 0, 1
                while d < ALL:
                    chain(nc.vector.tensor_copy(run[:, 1 - cur, 0:d, :], run[:, cur, 0:d, :]))
                    chain(nc.vector.tensor_tensor(run[:, 1 - cur, d:ALL, :], run[:, cur, d:ALL, :],
                                                  run[:, cur, 0:ALL - d, :], ALU.add))
                    cur, d = 1 - cur, 2 * d
                count = run[:, cur, ALL - 1, :].unsqueeze(2).broadcast_to([P, E, ALL])
                chain(nc.vector.tensor_tensor(full[:, :, :], count,
                                              const["steps"][:, 0:ALL].unsqueeze(1).broadcast_to([P, E, ALL]),
                                              ALU.is_gt))
                chain(nc.vector.tensor_reduce(tiles[:, :], full[:, :, :], AX, ALU.add))
                chain(nc.vector.tensor_tensor(square[:, :, :], const["lower"][:, :, :],
                                              tiles[:, :].unsqueeze(1).broadcast_to([P, E, E]), ALU.mult))
                chain(nc.vector.tensor_reduce(first[:, :], square[:, :, :], AX, ALU.add))
                chain(nc.vector.tensor_tensor(last[:, :], first[:, :], tiles[:, :], ALU.add))
                chain(nc.vector.tensor_tensor(ended[:, :, :],
                                              const["counting"][0:1, :].unsqueeze(2).broadcast_to(
                                                  [1, SLOT_TILES, E]),
                                              last[0:1, :].unsqueeze(1).broadcast_to([1, SLOT_TILES, E]),
                                              ALU.is_ge))
                chain(nc.vector.tensor_reduce(ownerf[:, :], ended[:, :, :], AX, ALU.add))
                chain(nc.vector.tensor_scalar(owner[:, :], ownerf[:, :], float(E - 1), None, ALU.min))
                chain(nc.vector.tensor_tensor(run[:, cur], run[:, cur], total, ALU.subtract))
                chain(nc.vector.tensor_tensor(run[:, cur], before, run[:, cur], ALU.add))
                chain(nc.vector.tensor_scalar(first[:, :], first[:, :], float(P), None, ALU.mult))
                chain(nc.vector.tensor_tensor(run[:, cur], run[:, cur],
                                              first[:, :].unsqueeze(1).broadcast_to(wide), ALU.add))
                for k in range(2):
                    chain(nc.vector.tensor_tensor(tmp[:, :, :], pick[:, k], run[:, cur], ALU.mult))
                    chain(nc.vector.tensor_reduce(slotf[:, k, :], tmp[:, :, :], AX, ALU.add))
                chain(nc.vector.tensor_copy(slot[:, :, :], slotf[:, :, :]))

            @block.scalar
            def _(act):
                act.wait_ge(s["shifted"], 1)
                nc.scalar.activation(e[:, :, :], e[:, :, :], ACT.Exp).then_inc(s["exp_done"], 1)

            @block.tensor
            def _(pe):
                pe.wait_ge(s["marked"], 1)
                marks = both[:, :, :].rearrange("p t e -> p (t e)")
                nc.tensor.matmul(ps[:, 0, 0:ALL * E], const["before"][:, :], marks, start=True, stop=True)
                nc.tensor.matmul(ps[:, 1, 0:ALL * E], const["ones"][:, :], marks, start=True,
                                 stop=True).then_inc(s["counts_in_psum"], 1)
        reset(nc, s.values())


def experts(nc, hid, const, w, tag, width, first_layer, scratch, out=None, arrival=None):
    ALL = BATCH * TILES
    NF = width // P
    HALF = width // 2 if width > 512 else width
    NH = width // HALF
    U = SLOT_TILES // ROUNDS
    rows_in, rows_out, zeroed, pool_sems = scratch
    with ExitStack() as ctx:
        def sb(name, shape, dt=F32):
            return ctx.enter_context(nc.sbuf_tensor(f"{tag}_{name}", shape, dt))

        xn_all = sb("xn_all", [P, ALL, DIM])
        logits = sb("logits", [P, ALL, EXPERTS])
        weight = sb("weight", [P, 2, ALL])
        slot = sb("slot", [P, 2, ALL], U32)
        owner = sb("owner", [1, SLOT_TILES], mybir.dt.int32)
        route(nc, hid, xn_all, const, w, tag, first_layer, logits)
        assign(nc, const, tag, first_layer, logits, weight, slot, owner)

        sent = pool_sems[-1]
        with nc.Block() as block:
            @block.sync
            def _(sp):
                if arrival is not None:
                    sp.wait_ge(*arrival)

            @block.gpsimd
            def _(pool):
                if first_layer:
                    pool.wait_ge(zeroed, 16 * ROUNDS)
                for t in range(ALL):
                    for k in range(2):
                        nc.gpsimd.indirect_dma_start(
                            rows_in, bass.IndirectOffsetOnAxis(ap=slot[:, k, t:t + 1], axis=0),
                            xn_all[:, t, :], None).then_inc(sent, 16)
                pool.wait_ge(sent, 16 * 2 * ALL * (1 if first_layer else 2))

        with ExitStack() as loop:
            def lsb(name, shape, dt=F32):
                return loop.enter_context(nc.sbuf_tensor(f"{tag}_{name}", shape, dt))

            def lps(name, shape):
                return loop.enter_context(nc.psum_tensor(f"{tag}_{name}", shape, F32))

            s = signals(nc, loop, tag + "mlp", """xT_in_psum xT_done hidden_in_psum gelu_done
                hiddenT_in_psum hiddenT_done y_in_psum y_done stored""")
            x_in = [loop.enter_context(nc.semaphore(f"{tag}mlp.x_in{j}")) for j in range(U)]
            x = lsb("x", [P, U, DIM])
            xTa, xTb = lsb("mxTa", [P, 2, P]), lsb("mxTb", [CB + 1, 2, P])
            hidden = lsb("hidden", [P, 2, width])
            hiddenT = lsb("hiddenT", [P, 2, NF, P])
            y = lsb("y", [P, 2, DIM])
            xT_ps = lps("mxT_ps", [P, 512])
            h_ps = lps("h_ps", [P, 2 * NH, 512])
            hT_ps = lps("hT_ps", [P, NH, 512])
            y_ps = lps("y_ps", [P, 512])
            CH = NF // NH
            nc.vector.memset(xTb[CB:CB + 1, :, :], 1.0)
            nc.all_engine_barrier()
            x_tiles = rows_in.rearrange("(i p) c -> p i c", p=P)
            y_tiles = rows_out.rearrange("(i p) c -> p i c", p=P)
            with nc.Fori(0, ROUNDS) as r:
                with nc.Block() as block:
                    @block.sync
                    def _(sp):
                        for j in range(U):
                            sp.dma_start(x[:, j:j + 1, :], x_tiles[:, bass.ds(r * U + j, 1), :]
                                         ).then_inc(x_in[j], 16)
                        for j in range(U):
                            sp.wait_ge(s["y_done"], j + 1)
                            sp.dma_start(y_tiles[:, bass.ds(r * U + j, 1), :], y[:, j % 2:j % 2 + 1, :]
                                         ).then_inc(s["stored"], 16)
                            sp.wait_ge(s["stored"], 16 * (j + 1))

                    @block.vector
                    def _(dve):
                        def copy_x(j):
                            dve.wait_ge(s["xT_in_psum"], j + 1)
                            if j >= 2:
                                dve.wait_ge(s["hidden_in_psum"], NH * (j - 1))
                            nc.vector.tensor_copy(xTa[:, j % 2, :], xT_ps[:, 0:P]).then_inc(s["xT_done"], 1)
                            nc.vector.tensor_copy(xTb[0:CB, j % 2, :], xT_ps[0:CB, P:2 * P]
                                                  ).then_inc(s["xT_done"], 1)

                        def copy_hidden(j):
                            for k in range(NH):
                                dve.wait_ge(s["hiddenT_in_psum"], NH * j + k + 1)
                                if k == 0 and j >= 2:
                                    dve.wait_ge(s["y_in_psum"], j - 1)
                                nc.vector.tensor_copy(
                                    hiddenT[:, j % 2, k * CH:(k + 1) * CH, :],
                                    hT_ps[:, k, 0:CH * P].rearrange("p (c q) -> p c q", c=CH)
                                ).then_inc(s["hiddenT_done"], 1)

                        def copy_y(j):
                            dve.wait_ge(s["y_in_psum"], j + 1)
                            if j >= 2:
                                dve.wait_ge(s["stored"], 16 * (j - 1))
                            nc.vector.tensor_copy(y[:, j % 2, :], y_ps[:, 0:DIM]).then_inc(s["y_done"], 1)

                        copy_x(0)
                        for j in range(U + 2):
                            if j + 1 < U:
                                copy_x(j + 1)
                            if 1 <= j < U + 1:
                                copy_hidden(j - 1)
                            if j >= 2:
                                copy_y(j - 2)

                    @block.scalar
                    def _(act):
                        for j in range(U):
                            for k in range(NH):
                                n = NH * j + k
                                act.wait_ge(s["hidden_in_psum"], n + 1)
                                if j >= 2:
                                    act.wait_ge(s["hiddenT_in_psum"], NH * (j - 1))
                                nc.scalar.activation(hidden[:, j % 2, k * HALF:(k + 1) * HALF],
                                                     h_ps[:, n % (2 * NH), 0:HALF], ACT.Gelu
                                                     ).then_inc(s["gelu_done"], 1)

                    @block.tensor
                    def _(pe):
                        own = [None] * U

                        def turn_x(j):
                            pe.wait_ge(x_in[j], 16)
                            if j >= 1:
                                pe.wait_ge(s["xT_done"], 2 * j)
                            nc.tensor.transpose(xT_ps[:, 0:P], x[:, j, 0:CA], const["ident"][:, :])
                            nc.tensor.transpose(xT_ps[0:CB, P:2 * P], x[:, j, CA:DIM],
                                                const["ident"][:, :]).then_inc(s["xT_in_psum"], 1)

                        def down(j):
                            own[j] = pe.value_load(owner[0:1, bass.ds(r * U + j, 1)], min_val=0,
                                                   max_val=EXPERTS - 1)
                            pe.wait_ge(s["xT_done"], 2 * (j + 1))
                            for k in range(NH):
                                n = NH * j + k
                                if j >= 2:
                                    pe.wait_ge(s["gelu_done"], n - 2 * NH + 1)
                                cols = slice(k * HALF, (k + 1) * HALF)
                                wa = w["down_a"][:, bass.ds(own[j], 1), cols].rearrange("p o c -> p (o c)")
                                wb = w["down_b"][:, bass.ds(own[j], 1), cols].rearrange("p o c -> p (o c)")
                                o = h_ps[:, n % (2 * NH), 0:HALF]
                                nc.tensor.matmul(o, xTa[:, j % 2, :], wa, start=True, stop=False)
                                nc.tensor.matmul(o, xTb[:, j % 2, :], wb, start=False,
                                                 stop=True).then_inc(s["hidden_in_psum"], 1)

                        def turn_hidden(j):
                            for k in range(NH):
                                pe.wait_ge(s["gelu_done"], NH * j + k + 1)
                                if j >= 1:
                                    pe.wait_ge(s["hiddenT_done"], NH * (j - 1) + k + 1)
                                for c in range(CH):
                                    f = (k * CH + c) * P
                                    ins = nc.tensor.transpose(hT_ps[:, k, c * P:(c + 1) * P],
                                                              hidden[:, j % 2, f:f + P], const["ident"][:, :])
                                ins.then_inc(s["hiddenT_in_psum"], 1)

                        def up(j):
                            pe.wait_ge(s["hiddenT_done"], NH * (j + 1))
                            if j >= 1:
                                pe.wait_ge(s["y_done"], j)
                            if not first_layer:
                                b2 = w["bias2"][0:1, bass.ds(own[j], 1), :].rearrange("p o c -> p (o c)")
                                nc.tensor.matmul(y_ps[:, 0:DIM], const["ones_row"][0:1, :], b2,
                                                 start=True, stop=False)
                            for c in range(NF):
                                wu = w["up"][:, bass.ds(own[j], 1), c, :].rearrange("p o c -> p (o c)")
                                ins = nc.tensor.matmul(y_ps[:, 0:DIM], hiddenT[:, j % 2, c, :], wu,
                                                       start=(first_layer and c == 0), stop=(c == NF - 1))
                            ins.then_inc(s["y_in_psum"], 1)

                        turn_x(0)
                        for j in range(U + 2):
                            if j < U:
                                down(j)
                            if j + 1 < U:
                                turn_x(j + 1)
                            if 1 <= j < U + 1:
                                turn_hidden(j - 1)
                            if j >= 2:
                                up(j - 2)
                reset(nc, [*s.values(), *x_in])

        combine(nc, hid, xn_all, const, w, tag, first_layer, weight, slot, rows_out, pool_sems, out)


def combine(nc, hid, xn_all, const, w, tag, first_layer, weight, slot, rows_out, pool_sems, out):
    ALL = BATCH * TILES
    RING = 8
    with ExitStack() as ctx:
        def sb(name, shape, dt=F32):
            return ctx.enter_context(nc.sbuf_tensor(f"{tag}_{name}", shape, dt))

        s = signals(nc, ctx, tag + "combine", "added stats_done moments_done rstd_done norm_done hid_done stored")
        got = pool_sems[0:RING]
        y = sb("gathered", [P, RING, 2, DIM])
        stats, mv, rstd = sb("cstats", [P, ALL, 6]), sb("cmv", [P, ALL, 2]), sb("crstd", [P, ALL])
        acc = xn_all if first_layer else hid
        with nc.Block() as block:
            @block.gpsimd
            def _(pool):
                def rstds(g):
                    part = slice(g * RING, (g + 1) * RING)
                    pool.wait_ge(s["moments_done"], RING * (g + 1))
                    nc.gpsimd.tensor_scalar(rstd[:, part], mv[:, part, 1], LN_EPS, None,
                                            ALU.add).then_inc(s["rstd_done"], 1)
                    pool.wait_ge(s["rstd_done"], 2 * g + 1)
                    nc.gpsimd.tensor_tensor(rstd[:, part], rstd[:, part],
                                            const["neg_half"][:, 0:1].broadcast_to([P, RING]),
                                            ALU.pow).then_inc(s["rstd_done"], 1)

                after_gather = {RING * (g + 1) + 4: g for g in range(ALL // RING - 1)}
                for t in range(ALL):
                    if t >= RING:
                        pool.wait_ge(s["added"], 2 * (t - RING + 1))
                    for k in range(2):
                        nc.gpsimd.indirect_dma_start(
                            y[:, t % RING, k, :], None, rows_out,
                            bass.IndirectOffsetOnAxis(ap=slot[:, k, t:t + 1], axis=0)
                        ).then_inc(got[t % RING], 16)
                    if first_layer and t in after_gather:
                        rstds(after_gather[t])
                if first_layer:
                    rstds(ALL // RING - 1)

            @block.vector
            def _(dve):
                def moments(t):
                    dve.wait_ge(s["stats_done"], t + 1)
                    nc.vector.bn_aggr(mv[:, t, :], stats[:, t, :]).then_inc(s["moments_done"], 1)

                def second_norm(g):
                    tiles = slice(g * RING, (g + 1) * RING)
                    dve.wait_ge(s["moments_done"], RING * (g + 1))
                    dve.wait_ge(s["rstd_done"], 2 * (g + 1))
                    for t in range(g * RING, (g + 1) * RING):
                        nc.vector.tensor_scalar(acc[:, t, :], acc[:, t, :], mv[:, t, 0:1], rstd[:, t:t + 1],
                                                ALU.subtract, ALU.mult).then_inc(s["norm_done"], 1)
                    n = (RING + 2) * g + RING
                    dve.wait_ge(s["norm_done"], n)
                    a = acc[:, tiles, :]
                    for k, (par, op) in enumerate(((w["gamma"], ALU.mult), (w["beta"], ALU.add))):
                        nc.vector.tensor_tensor(a, a, par[:, :].unsqueeze(1).broadcast_to([P, RING, DIM]),
                                                op).then_inc(s["norm_done"], 1)
                        dve.wait_ge(s["norm_done"], n + k + 1)
                    nc.vector.tensor_tensor(hid[:, tiles, :], a, hid[:, tiles, :],
                                            ALU.add).then_inc(s["hid_done"], 1)

                after_adding = {RING * (g + 1) + 6: g for g in range(ALL // RING - 1)}
                had = 16 * TILES + (0 if first_layer else 32 * (ALL // RING))
                for t in range(ALL):
                    dve.wait_ge(got[t % RING], had + 32 * (t // RING + 1))
                    for k in range(2):
                        if k:
                            dve.wait_ge(s["added"], 2 * t + 1)
                        nc.vector.scalar_tensor_tensor(acc[:, t, :], y[:, t % RING, k, :],
                                                       weight[:, k, t:t + 1], acc[:, t, :],
                                                       ALU.mult, ALU.add).then_inc(s["added"], 1)
                    if first_layer:
                        dve.wait_ge(s["added"], 2 * (t + 1))
                        nc.vector.bn_stats(stats[:, t, :], acc[:, t, :]).then_inc(s["stats_done"], 1)
                        if t >= 1:
                            moments(t - 1)
                        if t in after_adding:
                            second_norm(after_adding[t])
                if first_layer:
                    moments(ALL - 1)
                    second_norm(ALL // RING - 1)

            @block.sync
            def _(sp):
                if out is not None:
                    for g in range(BATCH):
                        sp.wait_ge(s["added"], 2 * TILES * (g + 1))
                        sp.dma_start(out.rearrange("(t p) c -> p t c", p=P)[:, g * TILES:(g + 1) * TILES, :],
                                     hid[:, g * TILES:(g + 1) * TILES, :]).then_inc(s["stored"], 16)
                    sp.wait_ge(s["stored"], 16 * BATCH)
        reset(nc, s.values())


def build(nc, io, out):
    with ExitStack() as ctx:
        def sb(name, shape, dt=F32):
            return ctx.enter_context(nc.sbuf_tensor(name, shape, dt))

        hid = sb("hid", [P, BATCH * TILES, DIM])
        idx = sb("tok_ids", [P, BATCH * TILES], U32)
        const = {}
        const["ident"] = sb("ident", [P, P])
        const["ident_r"], const["causal_r"] = sb("ident_r", [P, P], F32R), sb("causal_r", [P, P], F32R)
        const["causal"] = sb("causal", [P, P])
        const["cos"], const["sin"] = sb("rope_cos", [P, TILES, 2, D0]), sb("rope_sin", [P, TILES, 2, D0])
        const["places"] = sb("places", [P, 1, EXPERTS])
        const["steps"] = sb("steps", [P, BATCH * TILES])
        const["counting"] = sb("counting", [1, SLOT_TILES])
        const["lower"] = sb("lower", [P, EXPERTS, EXPERTS])
        const["bias_rows"] = sb("bias_rows", [P, 1])
        const["before"], const["ones"] = sb("before", [P, P]), sb("ones", [P, P])
        rows_in = nc.dram_tensor("dispatch_in", (SLOT_TILES * P, DIM), F32, kind="Internal").ap()
        rows_out = nc.dram_tensor("dispatch_out", (SLOT_TILES * P, DIM), F32, kind="Internal").ap()
        zeroed = ctx.enter_context(nc.semaphore("zeroed"))
        cleared = ctx.enter_context(nc.semaphore("cleared"))
        const["neg_half"] = sb("neg_half", [P, 2 * TILES])
        const["ones_row"] = sb("ones_row", [1, P])
        inputs_in = ctx.enter_context(nc.semaphore("inputs_in"))
        consts_done = ctx.enter_context(nc.semaphore("consts_done"))

        pool_sems = [ctx.enter_context(nc.semaphore(f"pool_dma{i}")) for i in range(BATCH + 1)]
        scratch = (rows_in, rows_out, zeroed, pool_sems)
        w_first = ExitStack()
        w0, f0 = {}, {}
        loads = []

        def weight(scope, group, name, shape, src):
            t = scope.enter_context(nc.sbuf_tensor(name, shape, F32))
            group[name.split(".")[1]] = t
            loads.append((t, src))

        with w_first:
            def w(group, name, shape, src):
                weight(w_first, group, name, shape, src)

            w(w0, "attn0.proj_a", [P, DIM], io["L0_proj"][0:CA, :])
            w(w0, "attn0.proj_b", [CB + 1, DIM], io["L0_proj"][CA:DIM + 1, :])
            w(f0, "ffn0.gate_a", [P, GATE_HID], io["L0_ffn_w1"][0:CA, :])
            w(f0, "ffn0.gate_b", [CB, GATE_HID], io["L0_ffn_w1"][CA:DIM, :])
            w(f0, "ffn0.gate_bias", [GATE_HID, 1], io["L0_ffn_b1"])
            w(f0, "ffn0.gate2", [GATE_HID + 1, EXPERTS], io["L0_gate2"])
            w(f0, "ffn0.down_a", [P, EXPERTS, F0], io["L0_down"][0:CA])
            w(f0, "ffn0.down_b", [CB + 1, EXPERTS, F0], io["L0_down"][CA:DIM + 1])
            w(f0, "ffn0.up", [P, EXPERTS, F0 // P, DIM], io["L0_up"])
            w(f0, "ffn0.gamma", [P, DIM], io["L0_ffn_gamma"].broadcast_to([P, DIM]))
            w(f0, "ffn0.beta", [P, DIM], io["L0_ffn_beta"].broadcast_to([P, DIM]))
            for t, src in ((const["ident"], io["ident"]), (const["causal"], io["causal"]), (const["cos"], io["cos"]),
                           (const["sin"], io["sin"]), (const["places"], io["places"]),
                           (const["steps"], io["steps"]), (const["counting"], io["counting"]),
                           (const["lower"], io["lower"]), (const["before"], io["before"]),
                           (const["bias_rows"], io["bias_rows"])):
                loads.append((t, src))

            def weights_in(sp):
                for t, src in loads:
                    sp.dma_start(t[:], src).then_inc(inputs_in, 16)
                sp.wait_ge(cleared, 1)
                for r in range(ROUNDS):
                    u = SLOT_TILES // ROUNDS
                    sp.dma_start(rows_in.rearrange("(i p) c -> p i c", p=P)[:, r * u:(r + 1) * u, :],
                                 zeros[:, :, :]).then_inc(zeroed, 16)
                sp.wait_ge(zeroed, 16 * ROUNDS)

            nc.vector.memset(const["ones"][:, :], 1.0)
            with ExitStack() as temp:
                split = split_weights(nc, ctx, w0, "attn0", w_first, temp, io["L0_qkv"], 3 * DIM)
                zeros = temp.enter_context(nc.sbuf_tensor("zeros", [P, SLOT_TILES // ROUNDS, DIM], F32))
                nc.vector.memset(zeros[:, :, :], 0.0).then_inc(cleared, 1)
                embed(nc, io, hid, idx, weights_in, split, pool_sems)
            with nc.Block() as block:
                @block.vector
                def _(dve):
                    dve.wait_ge(inputs_in, 16 * len(loads))
                    nc.vector.tensor_copy(const["ident_r"][:, :], const["ident"][:, :])
                    nc.vector.tensor_copy(const["causal_r"][:, :], const["causal"][:, :])
                    nc.vector.memset(const["neg_half"][:, :], -0.5)
                    nc.vector.memset(const["ones_row"][:, :], 1.0).then_inc(consts_done, 1)
                    dve.wait_ge(consts_done, 1)
            first_attention(nc, hid, const, w0)
            experts(nc, hid, const, f0, "ffn0", F0, True, scratch)

        def load_weights(name, scope, group, which, wait=True):
            done = ctx.enter_context(nc.semaphore(name))
            loads.clear()
            for n, shape, src in which:
                weight(scope, group, n, shape, src)
            with nc.Block() as block:
                @block.sync
                def _(sp):
                    for t, src in loads:
                        sp.dma_start(t[:], src).then_inc(done, 16)
                    if wait:
                        sp.wait_ge(done, 16 * len(loads))
            return done, 16 * len(loads)

        with ExitStack() as scope:
            w1 = {}
            load_weights("w1_in", scope, w1, [
                ("attn1.out", [P, H1 * D1 // P, DIM], io["L1_out"]),
                ("attn1.out_bias", [1, DIM], io["L1_attn_b_out"])])
            w1["head_scale"] = scope.enter_context(nc.sbuf_tensor("head_scale", [P, H1], F32))
            with ExitStack() as sub:
                load, high_parts, low_parts = split_weights(nc, ctx, w1, "attn1", scope, sub,
                                                            io["L1_qkv"], 3 * H1 * D1)
                reattn = sub.enter_context(nc.sbuf_tensor("reattn", [H1, D1 * D1], F32))
                reattn_in = sub.enter_context(nc.semaphore("reattn_in"))
                hs = sub.enter_context(nc.sbuf_tensor("reattn_sum", [H1, 1], F32))
                diag = sub.enter_context(nc.sbuf_tensor("reattn_diag", [H1, H1], F32))
                ones = sub.enter_context(nc.sbuf_tensor("ones_heads", [H1, P], F32))
                ps = sub.enter_context(nc.psum_tensor("head_scale_ps", [P, 512], F32))
                summed = sub.enter_context(nc.semaphore("reattn_summed"))
                spread = sub.enter_context(nc.semaphore("reattn_spread"))
                with nc.Block() as block:
                    @block.sync
                    def _(sp):
                        sp.dma_start(reattn[:, :], io["L1_attn_reattn_weights"]).then_inc(reattn_in, 16)
                        load(sp)

                    @block.scalar
                    def _(act):
                        high_parts(act)

                    @block.vector
                    def _(dve):
                        nc.vector.memset(ones[:, :], 1.0).then_inc(summed, 1)
                        dve.wait_ge(reattn_in, 16)
                        nc.vector.tensor_reduce(hs[:, :], reattn[:, :], AX, ALU.add).then_inc(summed, 1)
                        dve.wait_ge(summed, 2)
                        nc.vector.tensor_scalar(diag[:, :], const["ident"][0:H1, 0:H1], hs[:, 0:1], None,
                                                ALU.mult).then_inc(summed, 1)
                        dve.wait_ge(spread, 1)
                        nc.vector.tensor_copy(w1["head_scale"][:, :], ps[:, 0:H1]).then_inc(summed, 1)
                        low_parts(dve)
                        dve.wait_ge(summed, 4)

                    @block.tensor
                    def _(pe):
                        pe.wait_ge(summed, 3)
                        nc.tensor.matmul(ps[:, 0:H1], ones[:, :], diag[:, :], start=True,
                                         stop=True).then_inc(spread, 1)
            second_attention(nc, hid, const, w1)
        with ExitStack() as scope:
            f1 = {}
            load_weights("router_in", scope, f1, [
                ("ffn1.router_a", [P, EXPERTS], io["L1_router"][0:CA, :]),
                ("ffn1.router_b", [CB, EXPERTS], io["L1_router"][CA:DIM, :])])
            arrival = load_weights("f1_in", scope, f1, [
                ("ffn1.down_a", [P, EXPERTS, F1], io["L1_down"][0:CA]),
                ("ffn1.down_b", [CB + 1, EXPERTS, F1], io["L1_down"][CA:DIM + 1]),
                ("ffn1.up", [P, EXPERTS, F1 // P, DIM], io["L1_up"]),
                ("ffn1.bias2", [1, EXPERTS, DIM], io["L1_ffn_b2"])], wait=False)
            experts(nc, hid, const, f1, "ffn1", F1, False, scratch, out, arrival)


def layout(x, L0_tok_weights, L0_tok_emb_weight, L0_attn_Wq, L0_attn_bq, L0_attn_Wk, L0_attn_bk, L0_attn_Wv,
           L0_attn_bv, L0_attn_Wp, L0_attn_bp, L0_ffn_w1, L0_ffn_b1, L0_ffn_w2, L0_ffn_b2, L0_ffn_down_w,
           L0_ffn_down_b, L0_ffn_up_w, L0_ffn_gamma, L0_ffn_beta, L1_attn_w_qkv, L1_attn_b_qkv,
           L1_attn_reattn_weights, L1_attn_w_out, L1_attn_b_out, L1_ffn_router_w, L1_ffn_w1, L1_ffn_b1,
           L1_ffn_w2, L1_ffn_b2):
    a = {}
    a["tok"] = x.reshape(BATCH * TILES, P).T.astype(np.uint32)
    a["L0_tok_weights"] = L0_tok_weights[:, None]
    a["L0_tok_emb_weight"] = L0_tok_emb_weight
    a["L0_qkv"] = np.concatenate([np.concatenate([wt.T, bi[None]]) for wt, bi in (
        (L0_attn_Wq, L0_attn_bq), (L0_attn_Wk, L0_attn_bk), (L0_attn_Wv, L0_attn_bv))], axis=1)
    a["L0_proj"] = np.concatenate([L0_attn_Wp.T, L0_attn_bp[None]])
    a["L0_ffn_w1"], a["L0_ffn_b1"] = L0_ffn_w1, L0_ffn_b1[:, None]
    a["L0_gate2"] = np.concatenate([L0_ffn_w2, L0_ffn_b2[None]])
    a["L0_down"] = np.concatenate([L0_ffn_down_w.transpose(1, 0, 2), L0_ffn_down_b[None]])
    a["L0_up"] = L0_ffn_up_w.reshape(EXPERTS, F0 // P, P, DIM).transpose(2, 0, 1, 3)
    a["L0_ffn_gamma"], a["L0_ffn_beta"] = L0_ffn_gamma[None], L0_ffn_beta[None]
    a["L1_qkv"] = np.concatenate([L1_attn_w_qkv, L1_attn_b_qkv[None]])
    a["L1_out"] = L1_attn_w_out.reshape(H1 * D1 // P, P, DIM).transpose(1, 0, 2)
    a["L1_attn_b_out"] = L1_attn_b_out[None]
    a["L1_attn_reattn_weights"] = L1_attn_reattn_weights.reshape(H1, D1 * D1)
    a["L1_router"] = L1_ffn_router_w.T
    a["L1_down"] = np.concatenate([L1_ffn_w1.transpose(1, 0, 2), L1_ffn_b1[None]])
    a["L1_up"] = L1_ffn_w2.reshape(EXPERTS, F1 // P, P, DIM).transpose(2, 0, 1, 3)
    a["L1_ffn_b2"] = L1_ffn_b2[None]
    a["mix_mask"] = (np.arange(DIM)[None] < np.array(EMBED_DIMS)[:, None]).astype(np.float32)
    a["ident"] = np.eye(P, dtype=np.float32)
    a["causal"] = np.where(np.arange(P)[None] > np.arange(P)[:, None], MASKED, 0).astype(np.float32)
    a["places"] = np.broadcast_to(np.arange(EXPERTS, dtype=np.float32), (P, 1, EXPERTS))
    a["steps"] = np.broadcast_to(np.arange(BATCH * TILES, dtype=np.float32) * P, (P, BATCH * TILES))
    a["counting"] = np.arange(SLOT_TILES, dtype=np.float32)[None]
    a["lower"] = np.broadcast_to(np.tri(EXPERTS, k=-1, dtype=np.float32), (P, EXPERTS, EXPERTS))
    a["bias_rows"] = np.isin(np.arange(P), (CB, 96)).astype(np.float32)[:, None]
    a["before"] = np.triu(np.ones((P, P), np.float32), 1)
    f = np.float32
    inv = (f(1) / f(10000) ** (f(2) * np.arange(D0 // 2, dtype=f) / f(D0))).astype(f)
    ang = np.arange(SEQ, dtype=f)[:, None] * inv[None]
    cos = np.repeat(np.cos(ang), 2, axis=1)
    sin = np.stack([-np.sin(ang), np.sin(ang)], axis=-1).reshape(SEQ, D0)
    for name, table in (("cos", cos), ("sin", sin)):
        both = np.stack([table * f(D0 ** -0.5), table], axis=1)
        a[name] = both.reshape(TILES, P, 2, D0).transpose(1, 0, 2, 3)
    return {k: np.ascontiguousarray(v) for k, v in a.items()}


def declare(nc, arrays):
    io = {}
    for name, v in arrays.items():
        io[name] = nc.dram_tensor(f"in_{name}", v.shape, mybir.dt.from_np(v.dtype), kind="ExternalInput").ap()
    out = nc.dram_tensor("out", (BATCH * SEQ, DIM), F32, kind="ExternalOutput").ap()
    return io, out


def kernel(**inputs):
    import concourse.bacc as bacc
    from concourse.bass_utils import run_bass_kernel_spmd

    arrays = layout(**{k: np.asarray(v) for k, v in inputs.items()})
    nc = bacc.Bacc("TRN2", target_bir_lowering=False, num_devices=1)
    io, out = declare(nc, arrays)
    build(nc, io, out)
    r = run_bass_kernel_spmd(nc, [{f"in_{k}": v for k, v in arrays.items()}], core_ids=[0])
    return r.results[0]["out"].reshape(BATCH, SEQ, DIM)
```
